# Optimizing a Trainium2 kernel written in Bass

```python
import numpy as np
import jax
import jax.numpy as jnp

def _softmax(x, axis=-1):
    return jax.nn.softmax(x, axis=axis)

def _gelu(x):
    return jax.nn.gelu(x, approximate=True)

def _silu(x):
    return jax.nn.silu(x)

def _sigmoid(x):
    return jax.nn.sigmoid(x)

def _layernorm(x, axis=-1, eps=1e-05):
    m = jnp.mean(x, axis=axis, keepdims=True)
    v = jnp.var(x, axis=axis, keepdims=True)
    return (x - m) / jnp.sqrt(v + eps)

def _scatter_add(tgt, idx, src, axis=0):
    return tgt.at[idx].add(src)

def _segment_sum(src, seg, n):
    return jax.ops.segment_sum(src, seg, n)
kernel_name = 'mk_adj_resnorm_d2_adj_r2_ea862b'

def setup_inputs(seed: int=0):
    np.random.seed(seed)
    _w = jnp.asarray

    def _rec_inputs():
        import jax
        import jax.numpy as jnp
        _gk = jax.random.key(seed)
        x = -0.0002928 + 1 * jax.random.normal(jax.random.fold_in(_gk, 1), (4096, 256), jnp.float32)
        _w = (1.0 + jnp.arange(4096, dtype=jnp.float32)) ** (-0.5)
        _w = _w / _w.mean()
        _pij = jnp.clip(0.00390625 * _w[:, None] * _w[None, :], 0.0, 1.0)
        _a = jax.random.uniform(jax.random.fold_in(_gk, 2), (4096, 4096)) < _pij
        _af = _a.astype(jnp.float32)
        adj = _af
        return (x, adj)
    x, adj = _rec_inputs()

    def _L0_gnn_setup():
        import jax, jax.numpy as jnp
        import numpy as np
        N = 4096
        D = 256
        NEG_SLOPE = 0.2
        EDGE_P = 0.004

        def _dense_gat_layer(h_in, mask, W, b, asrc, adst):
            h = h_in @ W
            e = (h @ adst)[:, None] + (h @ asrc)[None, :]
            e = jax.nn.leaky_relu(e, NEG_SLOPE)
            e = jnp.where(mask, e, -jnp.inf)
            alpha = jax.nn.softmax(e, axis=1)
            return alpha @ h + b
        key = jax.random.key(seed)
        ks = jax.random.split(key, 12)
        x = jax.random.normal(ks[0], (N, D), dtype=jnp.float32)
        adj = (jax.random.uniform(ks[1], (N, N)) < EDGE_P).astype(jnp.float32)
        s = np.sqrt(2.0 / (D + D)).astype(np.float32) * 1.414

        def lin(k):
            return jax.random.normal(k, (D, D), dtype=jnp.float32) * s

        def att(k):
            return jax.random.normal(k, (D,), dtype=jnp.float32) * s
        return {'x': x, 'adj': adj, 'W1': lin(ks[2]), 'b1': jnp.zeros((D,), jnp.float32), 'asrc1': att(ks[3]), 'adst1': att(ks[4]), 'W2': lin(ks[5]), 'b2': jnp.zeros((D,), jnp.float32), 'asrc2': att(ks[6]), 'adst2': att(ks[7])}
    _L0_gnn_all = _L0_gnn_setup()
    _L0_gnn_in = {k: v for k, v in _L0_gnn_all.items() if k in ('W1', 'b1', 'asrc1', 'adst1', 'W2', 'b2', 'asrc2', 'adst2')}
    del _L0_gnn_all

    def _L1_gnn_setup():
        import jax, jax.numpy as jnp
        import numpy as np
        import math
        N = 4096
        D_IN = 256
        D_H = 256

        def _layer(x, cooccur, wq, bq, wk, bk, wv, bv, scale):
            q = x @ wq.T + bq
            k = x @ wk.T + bk
            v = x @ wv.T + bv
            att = jax.nn.softmax(jnp.einsum('ac,bc->ab', q, k) * scale, axis=-1)
            att = att + cooccur
            return jax.nn.relu(att @ v)
        key = jax.random.key(seed)
        ks = jax.random.split(key, 18)
        s_in = 1.0 / math.sqrt(D_IN)
        s_h = 1.0 / math.sqrt(D_H)
        f32 = jnp.float32
        return {'x': jax.random.normal(ks[0], (N, D_IN), dtype=f32), 'cooccur': jax.random.normal(ks[1], (N, N), dtype=f32) * 0.01, 'wq0': jax.random.normal(ks[2], (D_H, D_IN), dtype=f32) * s_in, 'bq0': jnp.zeros((D_H,), dtype=f32), 'wk0': jax.random.normal(ks[3], (D_H, D_IN), dtype=f32) * s_in, 'bk0': jnp.zeros((D_H,), dtype=f32), 'wv0': jax.random.normal(ks[4], (D_H, D_IN), dtype=f32) * s_in, 'bv0': jnp.zeros((D_H,), dtype=f32), 'wres': jax.random.normal(ks[5], (D_H, D_IN), dtype=f32) * s_in, 'bres': jnp.zeros((D_H,), dtype=f32), 'wq1': jax.random.normal(ks[6], (D_H, D_H), dtype=f32) * s_h, 'bq1': jnp.zeros((D_H,), dtype=f32), 'wk1': jax.random.normal(ks[7], (D_H, D_H), dtype=f32) * s_h, 'bk1': jnp.zeros((D_H,), dtype=f32), 'wv1': jax.random.normal(ks[8], (D_H, D_H), dtype=f32) * s_h, 'bv1': jnp.zeros((D_H,), dtype=f32)}
    _L1_gnn_all = _L1_gnn_setup()
    _L1_gnn_in = {k: v for k, v in _L1_gnn_all.items() if k in ('wq0', 'bq0', 'wk0', 'bk0', 'wv0', 'bv0', 'wres', 'bres', 'wq1', 'bq1', 'wk1', 'bk1', 'wv1', 'bv1')}
    del _L1_gnn_all
    return {'x': x, 'adj': adj, 'L0_gnn_W1': _L0_gnn_in['W1'], 'L0_gnn_b1': _L0_gnn_in['b1'], 'L0_gnn_asrc1': _L0_gnn_in['asrc1'], 'L0_gnn_adst1': _L0_gnn_in['adst1'], 'L0_gnn_W2': _L0_gnn_in['W2'], 'L0_gnn_b2': _L0_gnn_in['b2'], 'L0_gnn_asrc2': _L0_gnn_in['asrc2'], 'L0_gnn_adst2': _L0_gnn_in['adst2'], 'L1_gnn_wq0': _L1_gnn_in['wq0'], 'L1_gnn_bq0': _L1_gnn_in['bq0'], 'L1_gnn_wk0': _L1_gnn_in['wk0'], 'L1_gnn_bk0': _L1_gnn_in['bk0'], 'L1_gnn_wv0': _L1_gnn_in['wv0'], 'L1_gnn_bv0': _L1_gnn_in['bv0'], 'L1_gnn_wres': _L1_gnn_in['wres'], 'L1_gnn_bres': _L1_gnn_in['bres'], 'L1_gnn_wq1': _L1_gnn_in['wq1'], 'L1_gnn_bq1': _L1_gnn_in['bq1'], 'L1_gnn_wk1': _L1_gnn_in['wk1'], 'L1_gnn_bk1': _L1_gnn_in['bk1'], 'L1_gnn_wv1': _L1_gnn_in['wv1'], 'L1_gnn_bv1': _L1_gnn_in['bv1']}

def reference(x, adj, L0_gnn_W1, L0_gnn_b1, L0_gnn_asrc1, L0_gnn_adst1, L0_gnn_W2, L0_gnn_b2, L0_gnn_asrc2, L0_gnn_adst2, L1_gnn_wq0, L1_gnn_bq0, L1_gnn_wk0, L1_gnn_bk0, L1_gnn_wv0, L1_gnn_bv0, L1_gnn_wres, L1_gnn_bres, L1_gnn_wq1, L1_gnn_bq1, L1_gnn_wk1, L1_gnn_bk1, L1_gnn_wv1, L1_gnn_bv1):
    import jax
    import jax.numpy as jnp

    def _L0_gnn_ref(x, adj, W1, b1, asrc1, adst1, W2, b2, asrc2, adst2):
        import jax, jax.numpy as jnp
        import numpy as np
        N = 4096
        D = 256
        NEG_SLOPE = 0.2
        EDGE_P = 0.004

        def _dense_gat_layer(h_in, mask, W, b, asrc, adst):
            h = h_in @ W
            e = (h @ adst)[:, None] + (h @ asrc)[None, :]
            e = jax.nn.leaky_relu(e, NEG_SLOPE)
            e = jnp.where(mask, e, -jnp.inf)
            alpha = jax.nn.softmax(e, axis=1)
            return alpha @ h + b
        mask = (adj != 0) | jnp.eye(N, dtype=bool)
        h1 = jax.nn.relu(_dense_gat_layer(x, mask, W1, b1, asrc1, adst1))
        h2 = jax.nn.relu(_dense_gat_layer(h1, mask, W2, b2, asrc2, adst2))
        return h2

    def _L1_gnn_ref(x, cooccur, wq0, bq0, wk0, bk0, wv0, bv0, wres, bres, wq1, bq1, wk1, bk1, wv1, bv1):
        import jax, jax.numpy as jnp
        import numpy as np
        import math
        N = 4096
        D_IN = 256
        D_H = 256

        def _layer(x, cooccur, wq, bq, wk, bk, wv, bv, scale):
            q = x @ wq.T + bq
            k = x @ wk.T + bk
            v = x @ wv.T + bv
            att = jax.nn.softmax(jnp.einsum('ac,bc->ab', q, k) * scale, axis=-1)
            att = att + cooccur
            return jax.nn.relu(att @ v)
        scale = 1.0 / math.sqrt(D_H)
        x = _layer(x, cooccur, wq0, bq0, wk0, bk0, wv0, bv0, scale) + (x @ wres.T + bres)
        x = _layer(x, cooccur, wq1, bq1, wk1, bk1, wv1, bv1, scale) + x
        return x
    x = _layernorm(x + _L0_gnn_ref(x, adj, L0_gnn_W1, L0_gnn_b1, L0_gnn_asrc1, L0_gnn_adst1, L0_gnn_W2, L0_gnn_b2, L0_gnn_asrc2, L0_gnn_adst2), axis=-1)
    x = _layernorm(x + _L1_gnn_ref(x, adj, L1_gnn_wq0, L1_gnn_bq0, L1_gnn_wk0, L1_gnn_bk0, L1_gnn_wv0, L1_gnn_bv0, L1_gnn_wres, L1_gnn_bres, L1_gnn_wq1, L1_gnn_bq1, L1_gnn_wk1, L1_gnn_bk1, L1_gnn_wv1, L1_gnn_bv1), axis=-1)
    return x

_drawn_inputs = setup_inputs


def setup_inputs(seed=0):
    import zlib

    import numpy as np

    out = dict(_drawn_inputs(seed))
    spreads = {'L0_gnn_b1': (0.0, 0.1),
     'L0_gnn_b2': (0.0, 0.1),
     'L1_gnn_bq0': (0.0, 0.8),
     'L1_gnn_bk0': (0.0, 0.8),
     'L1_gnn_bv0': (0.0, 0.1),
     'L1_gnn_bres': (0.0, 0.322),
     'L1_gnn_bq1': (0.0, 0.504),
     'L1_gnn_bk1': (0.0, 0.8),
     'L1_gnn_bv1': (0.0, 0.485)}
    factors = {'L0_gnn_adst2': 3.481, 'L1_gnn_wq0': 5.74, 'L1_gnn_wk0': 5.928}
    for name, (base, spread) in spreads.items():
        noise = np.random.default_rng([zlib.crc32(name.encode()), seed]).standard_normal(out[name].shape)
        drawn = base * np.exp(spread * noise) if base else spread * noise
        out[name] = jnp.asarray(drawn.astype(out[name].dtype))
    for name, factor in factors.items():
        out[name] = (out[name] * factor).astype(out[name].dtype)
    return out
```

```python
import numpy as np
import concourse.bass as bass
from concourse import mybir
from contextlib import ExitStack

F32 = mybir.dt.float32
F32R = mybir.dt.float32r
ACT = mybir.ActivationFunctionType
ALU = mybir.AluOpType
AX = mybir.AxisListType

P = 128
N = 4096
D = 256
TILES = N // P
HALVES = D // P
CHUNK = 512
CHUNKS = N // CHUNK
BLOCKS = CHUNK // P
QUARTER = 1024
QUARTERS = N // QUARTER
CPQ = CHUNKS // QUARTERS
GROUP = 4
GROUPS = TILES // GROUP
SCALE = 1.0 / 16.0
SLOPE = 0.2
EPS = 1e-5
MASKED = -1e38
LAG = 3


class Signal:

    def __init__(self, sem, base):
        self.sem, self.base = sem, base

    def __call__(self, count):
        return self.sem, count + self.base


def due(count):
    return not isinstance(count, int) or count > 0


def steps(eng, body, first, steady, steady_end, last):
    for t in range(first, steady):
        body(t, t % 2)
    with eng.Fori(steady // 2, steady_end // 2) as u:
        body(2 * u, 0)
        body(2 * u + 1, 1)
    for t in range(steady_end, last):
        body(t, t % 2)


def exists(t):
    return not isinstance(t, int) or 0 <= t < TILES


def build(nc, x, adj, W1, b1, asrc1, adst1, W2, b2, asrc2, adst2,
          wq0, bq0, wk0, bk0, wv0, bv0, wres, bres, wq1, bq1, wk1, bk1, wv1, bv1, out):
    top = ExitStack()
    count = [0]

    def sem(name):
        count[0] += 1
        return top.enter_context(nc.semaphore(name))

    def scratch(name, shape, dt):
        return nc.dram_tensor(name, shape, dt, kind="Internal").ap()

    h1_dram = scratch("h1_scratch", (N, D), F32)
    x1_dram = scratch("x1_scratch", (N, D), F32)
    xa_dram = scratch("xa_scratch", (N, D), F32)
    res_dram = scratch("res_scratch", (N, D), F32)
    q_dram = [scratch(f"q_scratch{a}", (TILES, P, 2 * HALVES * P), F32) for a in range(2)]

    with top:
        ident = top.enter_context(nc.sbuf_tensor("ident", [P, P], F32))
        ones = top.enter_context(nc.sbuf_tensor("ones", [P, P], F32))
        power = top.enter_context(nc.sbuf_tensor("power", [P, 1], F32))
        bank = [top.enter_context(nc.psum_tensor(f"bank{i}", [P, CHUNK], F32)) for i in range(8)]
        off_diag = top.enter_context(nc.sbuf_tensor("off_diag", [P, P], F32))
        ident_step = sem("ident_step")
        consts_ready = sem("consts_ready")
        waits_passed = sem("waits_passed")

        class Space:
            pass

        def sb(mem, name, shape, dt):
            return mem.enter_context(nc.sbuf_tensor(name, shape, dt))

        handles = {}

        def signal(name, a, total):
            if name not in handles:
                handles[name] = sem(name)
            return Signal(handles[name], a * total)

        def gat_layer(a):
            s = Space()
            with ExitStack() as kept:
                s.hv = sb(kept, f"g{a}_hv", [P, TILES, 2 * D], F32R)
                s.s_row = sb(kept, f"g{a}_s_row", [P, N], F32)
                s.d_col = sb(kept, f"g{a}_d_col", [P, TILES], F32)
                with ExitStack() as projection:
                    s.w_in = sb(projection, f"gp{a}_w_in", [P, HALVES, D], F32)
                    s.w_hi = sb(projection, f"gp{a}_w_hi", [P, HALVES, D], F32R)
                    s.w_lo = sb(projection, f"gp{a}_w_lo", [P, HALVES, D], F32R)
                    s.asrc = sb(projection, f"gp{a}_asrc", [P, D], F32)
                    s.adst = sb(projection, f"gp{a}_adst", [P, D], F32)
                    s.xin0 = sb(projection, f"gp{a}_xin0", [P, GROUP, D], F32)
                    s.xin1 = sb(projection, f"gp{a}_xin1", [P, GROUP, D], F32)
                    s.xt_hi = sb(projection, f"gp{a}_xt_hi", [P, HALVES, CHUNK], F32R)
                    s.xt_lo = sb(projection, f"gp{a}_xt_lo", [P, HALVES, CHUNK], F32R)
                    s.h = sb(projection, f"gp{a}_h", [P, GROUP, D], F32)
                    s.junk = sb(projection, f"gp{a}_junk", [P, D], F32)
                    s.s4 = sb(projection, f"gp{a}_s4", [P, GROUP], F32)
                    s.d4 = sb(projection, f"gp{a}_d4", [P, GROUP], F32)
                    s.diag = sb(projection, f"gp{a}_diag", [P, CHUNK], F32)
                with ExitStack() as main:
                    s.bias = sb(main, f"gm{a}_bias", [P, D], F32)
                    s.adj = sb(main, f"gm{a}_adj", [P, N], F32)
                    s.t0 = sb(main, f"gm{a}_t0", [P, N], F32)
                    s.t1 = sb(main, f"gm{a}_t1", [P, N], F32)
                    s.pt_hi0 = sb(main, f"gm{a}_pt_hi0", [P, CHUNK], F32R)
                    s.pt_hi1 = sb(main, f"gm{a}_pt_hi1", [P, CHUNK], F32R)
                    s.pt_lo0 = sb(main, f"gm{a}_pt_lo0", [P, CHUNK], F32R)
                    s.pt_lo1 = sb(main, f"gm{a}_pt_lo1", [P, CHUNK], F32R)
                    s.max4 = sb(main, f"gm{a}_max4", [P, QUARTERS], F32)
                    s.smax = sb(main, f"gm{a}_smax", [P, 1], F32)
                    s.zmax = sb(main, f"gm{a}_zmax", [P, 1], F32)
                    s.m = sb(main, f"gm{a}_m", [P, 1], F32)
                    s.k_pos = sb(main, f"gm{a}_k_pos", [P, 1], F32)
                    s.k_neg = sb(main, f"gm{a}_k_neg", [P, 1], F32)
                    s.v = sb(main, f"gm{a}_v", [P, N], F32)
                    s.sum4 = sb(main, f"gm{a}_sum4", [P, 2, QUARTERS], F32)
                    s.total = sb(main, f"gm{a}_total", [P, 1], F32)
                    s.rinv = sb(main, f"gm{a}_rinv", [P, 2], F32)
                    s.o_lo = sb(main, f"gm{a}_o_lo", [P, D], F32)
                    s.o = sb(main, f"gm{a}_o", [P, D], F32)
                    s.xres0 = sb(main, f"gm{a}_xres0", [P, D], F32)
                    s.xres1 = sb(main, f"gm{a}_xres1", [P, D], F32)
                    s.stats = sb(main, f"gm{a}_stats", [P, 6], F32)
                    s.mv = sb(main, f"gm{a}_mv", [P, 2], F32)
                    s.ve = sb(main, f"gm{a}_ve", [P, 1], F32)
                    s.rstd = sb(main, f"gm{a}_rstd", [P, 1], F32)
                    s.y0 = sb(main, f"gm{a}_y0", [P, D], F32)
                    s.y1 = sb(main, f"gm{a}_y1", [P, D], F32)
            s.gp = k = Space()
            k.consts_in = signal("gp_consts_in", a, 3 * 16)
            k.x_in0 = signal("gp_x_in0", a, 8 * GROUPS)
            k.x_in1 = signal("gp_x_in1", a, 8 * GROUPS)
            k.w_hi_ready = signal("gp_w_hi_ready", a, 1)
            k.w_lo_ready = signal("gp_w_lo_ready", a, 1)
            k.xt_ready = signal("gp_xt_ready", a, HALVES * GROUPS)
            k.xt_hi_ready = signal("gp_xt_hi_ready", a, HALVES * GROUPS)
            k.xt_lo_ready = signal("gp_xt_lo_ready", a, HALVES * GROUPS)
            k.h_ready = signal("gp_h_ready", a, TILES)
            k.h_stored = signal("gp_h_stored", a, TILES)
            k.hv_hi_ready = signal("gp_hv_hi_ready", a, TILES)
            k.hv_lo_ready = signal("gp_hv_lo_ready", a, TILES)
            k.dots_ready = signal("gp_dots_ready", a, 2 * TILES)
            k.diag_ready = signal("gp_diag_ready", a, GROUPS)
            k.s_bcast_ready = signal("gp_s_bcast_ready", a, GROUPS)
            k.s_row_ready = signal("gp_s_row_ready", a, GROUPS)
            k.d_ready = signal("gp_d_ready", a, GROUPS)
            s.gm = k = Space()
            k.bias_in = signal("gm_bias_in", a, 16)
            k.adj_in0 = signal("gm_adj_in0", a, 16 * TILES)
            k.adj_in1 = signal("gm_adj_in1", a, 16 * TILES)
            k.adj_in2 = signal("gm_adj_in2", a, 16 * TILES)
            k.adj_in3 = signal("gm_adj_in3", a, 16 * TILES)
            k.x_res_in0 = signal("gm_x_res_in0", a, 0)
            k.x_res_in1 = signal("gm_x_res_in1", a, 0)
            k.nb_ready = signal("gm_nb_ready", a, QUARTERS * TILES)
            k.mask_ready = signal("gm_mask_ready", a, TILES)
            k.t_ready = signal("gm_t_ready", a, QUARTERS * TILES)
            k.smax_ready = signal("gm_smax_ready", a, TILES)
            k.zmax_ready = signal("gm_zmax_ready", a, TILES)
            k.m_ready = signal("gm_m_ready", a, TILES)
            k.k_ready = signal("gm_k_ready", a, 2 * TILES)
            k.v_ready = signal("gm_v_ready", a, QUARTERS * TILES)
            k.leaky_ready = signal("gm_leaky_ready", a, QUARTERS * TILES)
            k.p_ready = signal("gm_p_ready", a, QUARTERS * TILES)
            k.transposed = signal("gm_transposed", a, CHUNKS * TILES)
            k.hi_ready = signal("gm_hi_ready", a, CHUNKS * TILES)
            k.lo_ready = signal("gm_lo_ready", a, CHUNKS * TILES)
            k.pv_done = signal("gm_pv_done", a, CHUNKS * TILES)
            k.o_lo_ready = signal("gm_o_lo_ready", a, TILES)
            k.o_taken = signal("gm_o_taken", a, TILES)
            k.sum_ready = signal("gm_sum_ready", a, TILES)
            k.rinv_ready = signal("gm_rinv_ready", a, TILES)
            k.biased = signal("gm_biased", a, TILES)
            k.residual_added = signal("gm_residual_added", a, 0)
            k.stats_ready = signal("gm_stats_ready", a, 0)
            k.mean_ready = signal("gm_mean_ready", a, 0)
            k.ve_ready = signal("gm_ve_ready", a, 0)
            k.rstd_ready = signal("gm_rstd_ready", a, 0)
            k.y_ready = signal("gm_y_ready", a, TILES)
            k.y_stored0 = signal("gm_y_stored0", a, 8 * TILES)
            k.y_stored1 = signal("gm_y_stored1", a, 8 * TILES)
            return s

        def att_layer(a):
            s = Space()
            with ExitStack() as kept:
                s.kt_hi = sb(kept, f"a{a}_kt_hi", [P, HALVES, N], F32R)
                s.kt_lo = sb(kept, f"a{a}_kt_lo", [P, HALVES, N], F32R)
                s.v = sb(kept, f"a{a}_v", [P, TILES, 2 * D], F32R)
                with ExitStack() as projection:
                    s.wn = sb(projection, f"ap{a}_wn", [P, 4, HALVES, D], F32)
                    s.wqk_hi = sb(projection, f"ap{a}_wqk_hi", [P, HALVES, 2 * D], F32R)
                    s.wqk_lo = sb(projection, f"ap{a}_wqk_lo", [P, HALVES, 2 * D], F32R)
                    s.wvr_hi = sb(projection, f"ap{a}_wvr_hi", [P, HALVES, 2 * D], F32R)
                    s.wvr_lo = sb(projection, f"ap{a}_wvr_lo", [P, HALVES, 2 * D], F32R)
                    s.bqk = sb(projection, f"ap{a}_bqk", [P, 2, HALVES], F32)
                    s.bvr = sb(projection, f"ap{a}_bvr", [P, 2 * D], F32)
                    s.xin0 = sb(projection, f"ap{a}_xin0", [P, GROUP, D], F32)
                    s.xin1 = sb(projection, f"ap{a}_xin1", [P, GROUP, D], F32)
                    s.xt_hi = sb(projection, f"ap{a}_xt_hi", [P, HALVES, CHUNK], F32R)
                    s.xt_lo = sb(projection, f"ap{a}_xt_lo", [P, HALVES, CHUNK], F32R)
                    s.q_hl = sb(projection, f"ap{a}_q_hl", [P, 2, HALVES, CHUNK], F32R)
                    s.vr = sb(projection, f"ap{a}_vr", [P, GROUP, 2 * D], F32)
                with ExitStack() as main:
                    s.adj = sb(main, f"am{a}_adj", [P, N], F32)
                    s.s0 = sb(main, f"am{a}_s0", [P, N], F32)
                    s.s1 = sb(main, f"am{a}_s1", [P, N], F32)
                    s.q0 = sb(main, f"am{a}_q0", [P, 2, HALVES, P], F32R)
                    s.q1 = sb(main, f"am{a}_q1", [P, 2, HALVES, P], F32R)
                    s.pt_hi0 = sb(main, f"am{a}_pt_hi0", [P, CHUNK], F32R)
                    s.pt_hi1 = sb(main, f"am{a}_pt_hi1", [P, CHUNK], F32R)
                    s.pt_lo0 = sb(main, f"am{a}_pt_lo0", [P, CHUNK], F32R)
                    s.pt_lo1 = sb(main, f"am{a}_pt_lo1", [P, CHUNK], F32R)
                    s.max8 = sb(main, f"am{a}_max8", [P, 2, CHUNKS], F32)
                    s.neg_max = sb(main, f"am{a}_neg_max", [P, 1], F32)
                    s.bias = sb(main, f"am{a}_bias", [P, 2], F32)
                    s.sum4 = sb(main, f"am{a}_sum4", [P, 2, QUARTERS], F32)
                    s.total = sb(main, f"am{a}_total", [P, 1], F32)
                    s.rinv = sb(main, f"am{a}_rinv", [P, 1], F32)
                    s.o_lo = sb(main, f"am{a}_o_lo", [P, D], F32)
                    s.o = sb(main, f"am{a}_o", [P, D], F32)
                    s.res0 = sb(main, f"am{a}_res0", [P, D], F32)
                    s.res1 = sb(main, f"am{a}_res1", [P, D], F32)
                    s.xln0 = sb(main, f"am{a}_xln0", [P, D], F32)
                    s.xln1 = sb(main, f"am{a}_xln1", [P, D], F32)
                    s.stats = sb(main, f"am{a}_stats", [P, 6], F32)
                    s.mv = sb(main, f"am{a}_mv", [P, 2], F32)
                    s.ve = sb(main, f"am{a}_ve", [P, 1], F32)
                    s.rstd = sb(main, f"am{a}_rstd", [P, 1], F32)
                    s.y0 = sb(main, f"am{a}_y0", [P, D], F32)
                    s.y1 = sb(main, f"am{a}_y1", [P, D], F32)
            s.ap = k = Space()
            k.consts_in = signal("ap_consts_in", a, 8 * 16)
            k.x_in0 = signal("ap_x_in0", a, 8 * GROUPS)
            k.x_in1 = signal("ap_x_in1", a, 8 * GROUPS)
            k.wt_ready = signal("ap_wt_ready", a, 1)
            k.wt_hi_ready = signal("ap_wt_hi_ready", a, 4)
            k.wt_lo_ready = signal("ap_wt_lo_ready", a, 4)
            k.xt_ready = signal("ap_xt_ready", a, HALVES * GROUPS)
            k.xt_hi_ready = signal("ap_xt_hi_ready", a, HALVES * GROUPS)
            k.xt_lo_ready = signal("ap_xt_lo_ready", a, HALVES * GROUPS)
            k.qk_ready = signal("ap_qk_ready", a, 4 * GROUPS)
            k.qk_hi_ready = signal("ap_qk_hi_ready", a, 4 * GROUPS)
            k.qk_lo_ready = signal("ap_qk_lo_ready", a, 4 * GROUPS)
            k.q_stored = signal("ap_q_stored", a, 16 * TILES)
            k.vr_ready = signal("ap_vr_ready", a, TILES)
            k.vr_biased = signal("ap_vr_biased", a, TILES)
            k.v_hi_ready = signal("ap_v_hi_ready", a, TILES)
            k.v_lo_ready = signal("ap_v_lo_ready", a, TILES)
            k.res_stored = signal("ap_res_stored", a, 16 * GROUPS)
            s.am = k = Space()
            k.q_in0 = signal("am_q_in0", a, 8 * TILES)
            k.q_in1 = signal("am_q_in1", a, 8 * TILES)
            k.adj_in0 = signal("am_adj_in0", a, 16 * TILES)
            k.adj_in1 = signal("am_adj_in1", a, 16 * TILES)
            k.adj_in2 = signal("am_adj_in2", a, 16 * TILES)
            k.adj_in3 = signal("am_adj_in3", a, 16 * TILES)
            k.res_in0 = signal("am_res_in0", a, 8 * TILES)
            k.res_in1 = signal("am_res_in1", a, 8 * TILES)
            k.scores_ready = signal("am_scores_ready", a, CHUNKS * TILES)
            k.scores_taken = signal("am_scores_taken", a, CHUNKS * TILES)
            k.max_ready = signal("am_max_ready", a, TILES)
            k.bias_ready = signal("am_bias_ready", a, TILES)
            k.exp_done = signal("am_exp_done", a, QUARTERS * TILES)
            k.att_ready = signal("am_att_ready", a, QUARTERS * TILES)
            k.transposed = signal("am_transposed", a, CHUNKS * TILES)
            k.hi_ready = signal("am_hi_ready", a, CHUNKS * TILES)
            k.lo_ready = signal("am_lo_ready", a, CHUNKS * TILES)
            k.pv_done = signal("am_pv_done", a, CHUNKS * TILES)
            k.o_lo_ready = signal("am_o_lo_ready", a, TILES)
            k.o_taken = signal("am_o_taken", a, TILES)
            k.sum_ready = signal("am_sum_ready", a, TILES)
            k.rinv_ready = signal("am_rinv_ready", a, TILES)
            k.residual_added = signal("am_residual_added", a, 0)
            k.x1_added = signal("am_x1_added", a, 0)
            k.stats_ready = signal("am_stats_ready", a, 0)
            k.mean_ready = signal("am_mean_ready", a, 0)
            k.ve_ready = signal("am_ve_ready", a, 0)
            k.rstd_ready = signal("am_rstd_ready", a, 0)
            k.y_ready = signal("am_y_ready", a, TILES)
            k.y_stored0 = signal("am_y_stored0", a, 8 * TILES)
            k.y_stored1 = signal("am_y_stored1", a, 8 * TILES)
            return s

        gat = [gat_layer(a) for a in range(2)]
        att = [att_layer(a) for a in range(2)]

        gat_args = [(x, W1, b1, asrc1, adst1, h1_dram), (h1_dram, W2, b2, asrc2, adst2, x1_dram)]
        att_args = [(x1_dram, wq0, bq0, wk0, bk0, wv0, bv0, wres, bres, xa_dram),
                    (xa_dram, wq1, bq1, wk1, bk1, wv1, bv1, None, None, out)]
        adj_quarters = adj.rearrange("(t p) (q n) -> t q p n", p=P, n=QUARTER)

        def node_tiles(t):
            return t.rearrange("(t p) d -> t p d", p=P)

        def node_groups(t):
            return t.rearrange("(g t p) d -> g p t d", p=P, t=GROUP)

        def on_all_partitions(v):
            return v.rearrange("(a d) -> a d", a=1).broadcast_to([P, v.shape[0]])

        def halves(w):
            return w.rearrange("(h p) d -> p h d", p=P)

        def apart(eng):
            eng.sem_inc(waits_passed, 1)

        def gp_over(eng, s, a):
            eng.wait_ge(*s.gp.h_ready(TILES))
            eng.wait_ge(*s.gp.hv_hi_ready(TILES))
            eng.wait_ge(*s.gp.hv_lo_ready(TILES))
            eng.wait_ge(*s.gp.s_row_ready(GROUPS))
            eng.wait_ge(*s.gp.d_ready(GROUPS))
            eng.wait_ge(*s.gp.s_bcast_ready(GROUPS))

        def gp_sync(sp, s, a):
            src, W, _, asrc, adst, _ = gat_args[a]
            sp.dma_start(s.w_in[:, :, :], halves(W)).then_inc(s.gp.consts_in.sem, 16)
            sp.dma_start(s.asrc[:, :], on_all_partitions(asrc)).then_inc(s.gp.consts_in.sem, 16)
            sp.dma_start(s.adst[:, :], on_all_partitions(adst)).then_inc(s.gp.consts_in.sem, 16)

            def load(g, p):
                if due(HALVES * (g - 1)):
                    sp.wait_ge(*s.gp.xt_ready(HALVES * (g - 1)))
                sp.dma_start([s.xin0, s.xin1][p][:, :, :], node_groups(src)[g]).then_inc([s.gp.x_in0, s.gp.x_in1][p].sem, 16)

            steps(sp, load, 0, 2, GROUPS, GROUPS)

        def gp_tensor(pe, s, a):
            pe.wait_ge(*s.gp.w_hi_ready(1))
            pe.wait_ge(*s.gp.w_lo_ready(1))

            def group(g, p):
                pe.wait_ge(*[s.gp.x_in0, s.gp.x_in1][p](8 * (g - p) + 16))
                if due(HALVES * (g - 1)):
                    pe.wait_ge(*s.gp.xt_hi_ready(HALVES * (g - 1)))
                if due(HALVES * (g - 1)):
                    pe.wait_ge(*s.gp.xt_lo_ready(HALVES * (g - 1)))
                xin = [s.xin0, s.xin1][p]
                for ch in range(HALVES):
                    for tt in range(GROUP):
                        last = nc.tensor.transpose(bank[2 * p + ch][:, tt * P:(tt + 1) * P],
                                                   xin[:, tt, ch * P:(ch + 1) * P], ident[:, :])
                    last.then_inc(s.gp.xt_ready.sem, 1)
                pe.wait_ge(*s.gp.xt_hi_ready(HALVES * (g + 1)))
                pe.wait_ge(*s.gp.xt_lo_ready(HALVES * (g + 1)))
                for tt in range(GROUP):
                    if due(GROUP * g + tt - 1):
                        pe.wait_ge(*s.gp.h_stored(GROUP * g + tt - 1))
                    o = bank[4 + tt % 2][:, 0:D]
                    c = slice(tt * P, (tt + 1) * P)
                    parts = [(x_, w_, ch) for ch in range(HALVES)
                             for x_, w_ in ((s.xt_hi, s.w_hi), (s.xt_hi, s.w_lo), (s.xt_lo, s.w_hi))]
                    for i, (x_, w_, ch) in enumerate(parts):
                        last = nc.tensor.matmul(o, x_[:, ch, c], w_[:, ch, :], start=i == 0, stop=i == len(parts) - 1)
                    last.then_inc(s.gp.h_ready.sem, 1)
                pe.wait_ge(*s.gp.diag_ready(g + 1))
                if due(g):
                    pe.wait_ge(*s.gp.s_row_ready(g))
                nc.tensor.matmul(bank[6][:, :], ones[:, :], s.diag[:, :], start=True, stop=True)\
                    .then_inc(s.gp.s_bcast_ready.sem, 1)

            steps(pe, group, 0, 2, GROUPS, GROUPS)

        def gp_scalar(act, s, a):
            act.wait_ge(*s.gp.consts_in(48))
            nc.scalar.activation(s.w_hi[:, :, :], s.w_in[:, :, :], ACT.Copy).then_inc(s.gp.w_hi_ready.sem, 1)

            def group(g, p):
                if due(GROUP * g):
                    act.wait_ge(*s.gp.h_ready(GROUP * g))
                for ch in range(HALVES):
                    act.wait_ge(*s.gp.xt_ready(HALVES * g + ch + 1))
                    nc.scalar.activation(s.xt_hi[:, ch, :], bank[2 * p + ch][:, :], ACT.Copy).then_inc(s.gp.xt_hi_ready.sem, 1)
                for tt in range(GROUP):
                    act.wait_ge(*s.gp.h_stored(GROUP * g + tt + 1))
                    apart(act)
                    nc.scalar.activation(s.hv[:, GROUP * g + tt, 0:D], s.h[:, tt, :], ACT.Copy)\
                        .then_inc(s.gp.hv_hi_ready.sem, 1)
                act.wait_ge(*s.gp.s_bcast_ready(g + 1))
                apart(act)
                nc.scalar.activation(s.s_row[:, bass.ds(g * CHUNK, CHUNK)], bank[6][:, :], ACT.Copy)\
                    .then_inc(s.gp.s_row_ready.sem, 1)

            steps(act, group, 0, 2, GROUPS, GROUPS)

        def gp_vector(dve, s, a):
            dve.wait_ge(*s.gp.w_hi_ready(1))
            nc.vector.tensor_tensor(s.w_lo[:, :, :], s.w_in[:, :, :], s.w_hi[:, :, :].bitcast(F32), ALU.subtract)\
                .then_inc(s.gp.w_lo_ready.sem, 1)

            def group(g, p):
                if due(GROUP * g):
                    dve.wait_ge(*s.gp.h_ready(GROUP * g))
                for ch in range(HALVES):
                    dve.wait_ge(*s.gp.xt_hi_ready(HALVES * g + ch + 1))
                    nc.vector.tensor_tensor(s.xt_lo[:, ch, :], bank[2 * p + ch][:, :],
                                            s.xt_hi[:, ch, :].bitcast(F32), ALU.subtract).then_inc(s.gp.xt_lo_ready.sem, 1)
                if due(GROUP * g):
                    dve.wait_ge(*s.gp.hv_hi_ready(GROUP * g))
                for tt in range(GROUP):
                    dve.wait_ge(*s.gp.h_ready(GROUP * g + tt + 1))
                    nc.vector.tensor_copy(s.h[:, tt, :], bank[4 + tt % 2][:, 0:D]).then_inc(s.gp.h_stored.sem, 1)
                for tt in range(GROUP):
                    dve.wait_ge(*s.gp.h_stored(GROUP * g + tt + 1))
                    if due(2 * (GROUP * g + tt)):
                        dve.wait_ge(*s.gp.dots_ready(2 * (GROUP * g + tt)))
                    nc.vector.tensor_tensor_reduce(out=s.junk[:, :], in0=s.h[:, tt, :], in1=s.asrc[:, :], scale=1.0,
                                                   scalar=0.0, op0=ALU.mult, op1=ALU.add,
                                                   accum_out=s.s4[:, tt:tt + 1]).then_inc(s.gp.dots_ready.sem, 1)
                    dve.wait_ge(*s.gp.dots_ready(2 * (GROUP * g + tt) + 1))
                    nc.vector.tensor_tensor_reduce(out=s.junk[:, :], in0=s.h[:, tt, :], in1=s.adst[:, :], scale=1.0,
                                                   scalar=0.0, op0=ALU.mult, op1=ALU.add,
                                                   accum_out=s.d4[:, tt:tt + 1]).then_inc(s.gp.dots_ready.sem, 1)
                if due(g):
                    dve.wait_ge(*s.gp.s_bcast_ready(g))
                dve.wait_ge(*s.gp.dots_ready(2 * GROUP * (g + 1)))
                for tt in range(GROUP):
                    last = nc.vector.tensor_scalar(s.diag[:, tt * P:(tt + 1) * P], ident[:, :], s.s4[:, tt:tt + 1],
                                                   None, ALU.mult)
                last.then_inc(s.gp.diag_ready.sem, 1)
                nc.vector.tensor_copy(s.d_col[:, bass.ds(g * GROUP, GROUP)], s.d4[:, :]).then_inc(s.gp.d_ready.sem, 1)
                for tt in range(GROUP):
                    dve.wait_ge(*s.gp.hv_hi_ready(GROUP * g + tt + 1))
                    nc.vector.tensor_tensor(s.hv[:, GROUP * g + tt, D:2 * D], s.h[:, tt, :],
                                            s.hv[:, GROUP * g + tt, 0:D].bitcast(F32), ALU.subtract)\
                        .then_inc(s.gp.hv_lo_ready.sem, 1)

            steps(dve, group, 0, 2, GROUPS, GROUPS)

        def gm_over(eng, s, a):
            eng.wait_ge(*s.gm.pv_done(TILES * CHUNKS))
            eng.wait_ge(*s.gm.hi_ready(TILES * CHUNKS))
            eng.wait_ge(*s.gm.lo_ready(TILES * CHUNKS))
            eng.wait_ge(*s.gm.o_lo_ready(TILES))
            eng.wait_ge(*s.gm.y_ready(TILES))
            eng.wait_ge(*s.gm.y_stored0(8 * TILES))
            eng.wait_ge(*s.gm.y_stored1(8 * TILES))

        def gm_sync(sp, s, a):
            src, _, bias, _, _, dst = gat_args[a]
            sp.dma_start(s.bias[:, :], on_all_partitions(bias)).then_inc(s.gm.bias_in.sem, 16)

            def tile(t, p):
                if exists(t):
                    for q in range(QUARTERS):
                        if due(QUARTERS * (t - 1) + q + 1):
                            sp.wait_ge(*s.gm.t_ready(QUARTERS * (t - 1) + q + 1))
                        sp.dma_start(s.adj[:, q * QUARTER:(q + 1) * QUARTER], adj_quarters[t, q]).then_inc(
                            [s.gm.adj_in0, s.gm.adj_in1, s.gm.adj_in2, s.gm.adj_in3][q].sem, 16)
                    if a == 1:
                        if due(t - 1):
                            sp.wait_ge(*s.gm.y_ready(t - 1))
                        sp.dma_start([s.xres0, s.xres1][p][:, :], node_tiles(x)[t]).then_inc(
                            [s.gm.x_res_in0, s.gm.x_res_in1][p].sem, 16)
                if exists(t - 2):
                    if due(t - 1):
                        sp.wait_ge(*s.gm.y_ready(t - 1))
                    sp.dma_start(node_tiles(dst)[t - 2], [s.y0, s.y1][p][:, :]).then_inc(
                        [s.gm.y_stored0, s.gm.y_stored1][p].sem, 16)

            steps(sp, tile, 0, 4, TILES, TILES + 2)

        def gm_tensor(pe, s, a):

            def transposes(t, p, c):
                g = CHUNKS * t + c
                if c % CPQ == 0:
                    pe.wait_ge(*s.gm.p_ready(QUARTERS * t + c // CPQ + 1))
                if due(g - 1):
                    pe.wait_ge(*s.gm.hi_ready(g - 1))
                if due(g - 1):
                    pe.wait_ge(*s.gm.lo_ready(g - 1))
                for b in range(BLOCKS):
                    j = c * BLOCKS + b
                    last = nc.tensor.transpose(bank[c % 2][:, b * P:(b + 1) * P],
                                               [s.t0, s.t1][p][:, j * P:(j + 1) * P], ident[:, :])
                last.then_inc(s.gm.transposed.sem, 1)

            def values(t, p, c):
                g = CHUNKS * t + c
                if c == 0:
                    if due(t - 1):
                        pe.wait_ge(*s.gm.o_taken(t - 1))
                pe.wait_ge(*s.gm.hi_ready(g + 1))
                pe.wait_ge(*s.gm.lo_ready(g + 1))
                hi, lo = [s.pt_hi0, s.pt_hi1][c % 2], [s.pt_lo0, s.pt_lo1][c % 2]
                for b in range(BLOCKS):
                    j = c * BLOCKS + b
                    w = slice(b * P, (b + 1) * P)
                    nc.tensor.matmul(bank[4 + p][:, :], hi[:, w], s.hv[:, j, :], start=j == 0, stop=False)
                    last = nc.tensor.matmul(bank[4 + p][:, 0:D], lo[:, w], s.hv[:, j, 0:D], start=False,
                                            stop=j == TILES - 1)
                last.then_inc(s.gm.pv_done.sem, 1)

            def tile(t, p):
                for c in range(CHUNKS):
                    if exists(t - 1):
                        transposes(t - 1, 1 - p, c)
                    if c == 0:
                        if exists(t - 2):
                            values(t - 2, p, CHUNKS - 1)
                    elif exists(t - 1):
                        values(t - 1, 1 - p, c - 1)

            steps(pe, tile, 1, 4, TILES, TILES + 2)

        def gm_scalar(act, s, a):

            def tile(t, p):
                for c in range(CHUNKS):
                    if exists(t) and c in (3, 4):
                        for q in (2 * c - 6, 2 * c - 5):
                            col = slice(q * QUARTER, (q + 1) * QUARTER)
                            act.wait_ge(*s.gm.k_ready(2 * (t + 1)))
                            nc.scalar.activation(s.v[:, col], [s.t0, s.t1][p][:, col], ACT.Identity,
                                                 bias=s.k_neg[:, :], scale=SLOPE).then_inc(s.gm.v_ready.sem, 1)
                    for step, q in (((t, p), c - 5) if c >= 5 else ((t - 1, 1 - p), c + 3),):
                        if 0 <= q < QUARTERS and exists(step[0]):
                            col = slice(q * QUARTER, (q + 1) * QUARTER)
                            buf = [s.t0, s.t1][step[1]][:, col]
                            act.wait_ge(*s.gm.leaky_ready(QUARTERS * step[0] + q + 1))
                            nc.scalar.activation(buf, buf, ACT.Exp, bias=0.0, scale=1.0,
                                                 accum_out=s.sum4[:, step[1], q:q + 1]).then_inc(s.gm.p_ready.sem, 1)
                    if exists(t - 1):
                        g = CHUNKS * (t - 1) + c
                        act.wait_ge(*s.gm.transposed(g + 1))
                        if due(g - 1):
                            act.wait_ge(*s.gm.pv_done(g - 1))
                        nc.scalar.activation([s.pt_hi0, s.pt_hi1][c % 2][:, :], bank[c % 2][:, :], ACT.Copy)\
                            .then_inc(s.gm.hi_ready.sem, 1)
                    if c == 1 and exists(t - 2):
                        if due(CHUNKS * (t - 1)):
                            act.wait_ge(*s.gm.pv_done(CHUNKS * (t - 1)))
                        if due(t - 2):
                            act.wait_ge(*s.gm.o_taken(t - 2))
                        nc.scalar.activation(s.o_lo[:, :], bank[4 + p][:, D:2 * D], ACT.Copy)\
                            .then_inc(s.gm.o_lo_ready.sem, 1)

            steps(act, tile, 0, 4, TILES, TILES + 2)

        def gm_vector(dve, s, a):
            chain = 3 if a == 0 else 6

            def row_sum(t, p):
                dve.wait_ge(*s.gm.p_ready(QUARTERS * (t + 1)))
                nc.vector.reduce_sum(s.total[:, :], s.sum4[:, p, :], AX.X).then_inc(s.gm.sum_ready.sem, 1)
                dve.wait_ge(*s.gm.sum_ready(t + 1))
                nc.vector.reciprocal(s.rinv[:, p:p + 1], s.total[:, :]).then_inc(s.gm.rinv_ready.sem, 1)

            def row_constants(t):
                d = s.d_col[:, bass.ds(t, 1)]
                dve.wait_ge(*s.gm.t_ready(QUARTERS * (t + 1)))
                nc.vector.reduce_max(s.smax[:, :], s.max4[:, :], AX.X).then_inc(s.gm.smax_ready.sem, 1)
                dve.wait_ge(*s.gm.smax_ready(t + 1))
                apart(dve)
                nc.vector.tensor_scalar(s.zmax[:, :], s.smax[:, :], d, None, ALU.add).then_inc(s.gm.zmax_ready.sem, 1)
                dve.wait_ge(*s.gm.zmax_ready(t + 1))
                nc.vector.scalar_tensor_tensor(s.m[:, :], s.zmax[:, :], SLOPE, s.zmax[:, :], ALU.mult, ALU.max)\
                    .then_inc(s.gm.m_ready.sem, 1)
                dve.wait_ge(*s.gm.m_ready(t + 1))
                apart(dve)
                nc.vector.tensor_scalar(s.k_pos[:, :], d, s.m[:, :], None, ALU.subtract).then_inc(s.gm.k_ready.sem, 1)
                nc.vector.scalar_tensor_tensor(s.k_neg[:, :], d, SLOPE, s.m[:, :], ALU.mult, ALU.subtract)\
                    .then_inc(s.gm.k_ready.sem, 1)

            def finish(t, p):
                dve.wait_ge(*s.gm.o_lo_ready(t + 1))
                nc.vector.tensor_tensor(s.o[:, :], bank[4 + p][:, 0:D], s.o_lo[:, :], ALU.add).then_inc(s.gm.o_taken.sem, 1)
                dve.wait_ge(*s.gm.o_taken(t + 1))
                dve.wait_ge(*s.gm.rinv_ready(t + 1))
                nc.vector.scalar_tensor_tensor(s.o[:, :], s.o[:, :], s.rinv[:, p:p + 1], s.bias[:, :], ALU.mult,
                                               ALU.add).then_inc(s.gm.biased.sem, 1)
                dve.wait_ge(*s.gm.biased(t + 1))
                y = [s.y0, s.y1][p]
                if due(8 * (t - p)):
                    dve.wait_ge(*[s.gm.y_stored0, s.gm.y_stored1][p](8 * (t - p)))
                if a == 0:
                    nc.vector.tensor_scalar(y[:, :], s.o[:, :], 0.0, None, ALU.max).then_inc(s.gm.y_ready.sem, 1)
                    return
                dve.wait_ge(*[s.gm.x_res_in0, s.gm.x_res_in1][p](8 * (t - p) + 16))
                nc.vector.scalar_tensor_tensor(s.o[:, :], s.o[:, :], 0.0, [s.xres0, s.xres1][p][:, :],
                                               ALU.max, ALU.add).then_inc(s.gm.residual_added.sem, 1)
                dve.wait_ge(*s.gm.residual_added(t + 1))
                layer_norm(dve, s, s.gm, s.o, y, t)

            def tile(t, p):
                for c in range(CHUNKS):
                    if exists(t) and c < 2:
                        for q in (2 * c, 2 * c + 1):
                            dve.wait_ge(*[s.gm.adj_in0, s.gm.adj_in1, s.gm.adj_in2, s.gm.adj_in3][q](16 * (t + 1)))
                            nc.vector.tensor_scalar(s.adj[:, q * QUARTER:(q + 1) * QUARTER],
                                                    s.adj[:, q * QUARTER:(q + 1) * QUARTER], 0.0, MASKED,
                                                    ALU.is_equal, ALU.mult).then_inc(s.gm.nb_ready.sem, 1)
                    if exists(t) and c == 1:
                        dve.wait_ge(*s.gm.nb_ready(QUARTERS * (t + 1)))
                        diagonal = s.adj[:, bass.ds(t * P, P)]
                        nc.vector.tensor_tensor(diagonal, diagonal, off_diag[:, :], ALU.mult).then_inc(s.gm.mask_ready.sem, 1)
                        dve.wait_ge(*s.gm.mask_ready(t + 1))
                    if exists(t) and 1 <= c < 4:
                        for q in ([0], [1, 2], [3])[c - 1]:
                            col = slice(q * QUARTER, (q + 1) * QUARTER)
                            apart(dve)
                            nc.vector.tensor_tensor_reduce(out=[s.t0, s.t1][p][:, col], in0=s.s_row[:, col],
                                                           in1=s.adj[:, col], scale=1.0, scalar=-3e38,
                                                           op0=ALU.add, op1=ALU.max, accum_out=s.max4[:, q:q + 1])\
                                .then_inc(s.gm.t_ready.sem, 1)
                    if exists(t) and c == 3:
                        row_constants(t)
                    if exists(t) and c >= 4:
                        q = c - 4
                        col = slice(q * QUARTER, (q + 1) * QUARTER)
                        buf = [s.t0, s.t1][p][:, col]
                        dve.wait_ge(*s.gm.v_ready(QUARTERS * t + q + 1))
                        nc.vector.scalar_tensor_tensor(buf, buf, s.k_pos[:, :], s.v[:, col], ALU.add, ALU.max)\
                            .then_inc(s.gm.leaky_ready.sem, 1)
                    if exists(t - 1):
                        g = CHUNKS * (t - 1) + c
                        dve.wait_ge(*s.gm.transposed(g + 1))
                        dve.wait_ge(*s.gm.hi_ready(g + 1))
                        if due(g - 1):
                            dve.wait_ge(*s.gm.pv_done(g - 1))
                        nc.vector.tensor_tensor([s.pt_lo0, s.pt_lo1][c % 2][:, :], bank[c % 2][:, :],
                                                [s.pt_hi0, s.pt_hi1][c % 2][:, :].bitcast(F32), ALU.subtract)\
                            .then_inc(s.gm.lo_ready.sem, 1)
                    if c == 2 and exists(t - 1):
                        row_sum(t - 1, 1 - p)
                    if c == 4 and exists(t - 2):
                        finish(t - 2, p)

            dve.wait_ge(*s.gm.bias_in(16))
            steps(dve, tile, 0, 4, TILES, TILES + 2)

        def gm_pool(pool, s):
            inverse_roots(pool, s, s.gm)

        def inverse_roots(pool, s, k):
            def tile(t, p):
                pool.wait_ge(*k.ve_ready(t + 1))
                nc.gpsimd.tensor_tensor(s.rstd[:, :], s.ve[:, :], power[:, :], ALU.pow).then_inc(k.rstd_ready.sem, 1)
            steps(pool, tile, 0, 2, TILES, TILES)

        def layer_norm(dve, s, k, u, y, t):
            nc.vector.bn_stats(s.stats[:, :], u[:, :]).then_inc(k.stats_ready.sem, 1)
            dve.wait_ge(*k.stats_ready(t + 1))
            apart(dve)
            nc.vector.bn_aggr(s.mv[:, :], s.stats[:, :]).then_inc(k.mean_ready.sem, 1)
            dve.wait_ge(*k.mean_ready(t + 1))
            nc.vector.tensor_scalar(s.ve[:, :], s.mv[:, 1:2], EPS, None, ALU.add).then_inc(k.ve_ready.sem, 1)
            dve.wait_ge(*k.rstd_ready(t + 1))
            nc.vector.tensor_scalar(y[:, :], u[:, :], s.mv[:, 0:1], s.rstd[:, :], ALU.subtract, ALU.mult)\
                .then_inc(k.y_ready.sem, 1)

        def ap_over(eng, s, a):
            eng.wait_ge(*s.ap.qk_hi_ready(4 * GROUPS))
            eng.wait_ge(*s.ap.qk_lo_ready(4 * GROUPS))
            eng.wait_ge(*s.ap.v_hi_ready(TILES))
            eng.wait_ge(*s.ap.v_lo_ready(TILES))
            eng.wait_ge(*s.ap.vr_ready(TILES))
            eng.wait_ge(*s.ap.q_stored(16 * TILES))
            if a == 0:
                eng.wait_ge(*s.ap.res_stored(16 * GROUPS))

        def ap_sync(sp, s, a):
            src, wq, bq, wk, bk, wv, bv, wr, br, _ = att_args[a]
            for i, w in enumerate([wq, wk, wv] + ([wr] if a == 0 else [])):
                sp.dma_start(s.wn[:, i, :, :], halves(w)).then_inc(s.ap.consts_in.sem, 16)
            for i, b in enumerate((bq, bk)):
                sp.dma_start(s.bqk[:, i, :], b.rearrange("(h p) -> p h", p=P),
                             allow_slow_non_contiguous=True).then_inc(s.ap.consts_in.sem, 16)
            for i, b in enumerate([bv] + ([br] if a == 0 else [])):
                sp.dma_start(s.bvr[:, i * D:(i + 1) * D], on_all_partitions(b)).then_inc(s.ap.consts_in.sem, 16)

            def load(g, p):
                if due(HALVES * (g - 1)):
                    sp.wait_ge(*s.ap.xt_ready(HALVES * (g - 1)))
                sp.dma_start([s.xin0, s.xin1][p][:, :, :], node_groups(src)[g]).then_inc([s.ap.x_in0, s.ap.x_in1][p].sem, 16)
                if exists(g - 1):
                    store(g - 1)

            def store(g):
                sp.wait_ge(*s.ap.qk_hi_ready(4 * g + 2))
                sp.wait_ge(*s.ap.qk_lo_ready(4 * g + 2))
                for tt in range(GROUP):
                    to = q_dram[a].rearrange("(g t) p (hl h n) -> g t p hl h n", t=GROUP, hl=2, h=HALVES)[g, tt]
                    last = sp.dma_start(to, s.q_hl[:, :, :, tt * P:(tt + 1) * P].bitcast(F32)).then_inc(s.ap.q_stored.sem, 16)
                if a == 0:
                    sp.wait_ge(*s.ap.vr_biased(GROUP * (g + 1)))
                    sp.dma_start(node_groups(res_dram)[g], s.vr[:, :, D:2 * D]).then_inc(s.ap.res_stored.sem, 16)

            steps(sp, load, 0, 2, GROUPS, GROUPS)
            store(GROUPS - 1)

        def ap_tensor(pe, s, a):
            nw = 4 if a == 0 else 3
            pe.wait_ge(*s.ap.consts_in(16 * (nw + 2 + nw - 2)))
            for w in range(nw):
                for ci in range(HALVES):
                    for co in range(HALVES):
                        last = nc.tensor.transpose(bank[(w // 2) * 4 + ci][:, ((w % 2) * HALVES + co) * P:
                                                                           ((w % 2) * HALVES + co + 1) * P],
                                                   s.wn[:, w, co, ci * P:(ci + 1) * P], ident[:, :])
            last.then_inc(s.ap.wt_ready.sem, 1)
            pe.wait_ge(*s.ap.wt_hi_ready(4))
            pe.wait_ge(*s.ap.wt_lo_ready(4))
            nvr = D * (nw - 2)

            def group(g, p):
                pe.wait_ge(*[s.ap.x_in0, s.ap.x_in1][p](8 * (g - p) + 16))
                if due(HALVES * g):
                    pe.wait_ge(*s.ap.xt_lo_ready(HALVES * g))
                for ch in range(HALVES):
                    for tt in range(GROUP):
                        last = nc.tensor.transpose(bank[ch][:, tt * P:(tt + 1) * P],
                                                   [s.xin0, s.xin1][p][:, tt, ch * P:(ch + 1) * P], ident[:, :])
                    last.then_inc(s.ap.xt_ready.sem, 1)
                pe.wait_ge(*s.ap.xt_hi_ready(HALVES * (g + 1)))
                pe.wait_ge(*s.ap.xt_lo_ready(HALVES * (g + 1)))
                for i in range(4):
                    if due(4 * (g - 1) + i + 1):
                        pe.wait_ge(*s.ap.qk_hi_ready(4 * (g - 1) + i + 1))
                    if due(4 * (g - 1) + i + 1):
                        pe.wait_ge(*s.ap.qk_lo_ready(4 * (g - 1) + i + 1))
                    w = slice(i * P, (i + 1) * P)
                    parts = [(w_, x_, ci) for ci in range(HALVES)
                             for w_, x_ in ((s.wqk_hi, s.xt_hi), (s.wqk_hi, s.xt_lo), (s.wqk_lo, s.xt_hi))]
                    for n, (w_, x_, ci) in enumerate(parts):
                        last = nc.tensor.matmul(bank[2 + i][:, :], w_[:, ci, w], x_[:, ci, :], start=n == 0,
                                                stop=n == len(parts) - 1)
                    last.then_inc(s.ap.qk_ready.sem, 1)
                for tt in range(GROUP):
                    if due(GROUP * g + tt - 1):
                        pe.wait_ge(*s.ap.vr_biased(GROUP * g + tt - 1))
                    c = slice(tt * P, (tt + 1) * P)
                    parts = [(x_, w_, ci) for ci in range(HALVES)
                             for x_, w_ in ((s.xt_hi, s.wvr_hi), (s.xt_hi, s.wvr_lo), (s.xt_lo, s.wvr_hi))]
                    for n, (x_, w_, ci) in enumerate(parts):
                        last = nc.tensor.matmul(bank[6 + tt % 2][:, 0:nvr], x_[:, ci, c], w_[:, ci, 0:nvr],
                                                start=n == 0, stop=n == len(parts) - 1)
                    last.then_inc(s.ap.vr_ready.sem, 1)

            steps(pe, group, 0, 2, GROUPS, GROUPS)

        def ap_scalar(act, s, a):
            act.wait_ge(*s.ap.wt_ready(1))
            nvr = D * (2 if a == 0 else 1)
            for ci in range(HALVES):
                nc.scalar.activation(s.wqk_hi[:, ci, :], bank[ci][:, :], ACT.Copy).then_inc(s.ap.wt_hi_ready.sem, 1)
                nc.scalar.activation(s.wvr_hi[:, ci, 0:nvr], bank[4 + ci][:, 0:nvr], ACT.Copy)\
                    .then_inc(s.ap.wt_hi_ready.sem, 1)
            act.wait_ge(*s.ap.consts_in(128 if a == 0 else 96))

            def group(g, p):
                if due(GROUP * g):
                    act.wait_ge(*s.ap.vr_ready(GROUP * g))
                for ch in range(HALVES):
                    act.wait_ge(*s.ap.xt_ready(HALVES * g + ch + 1))
                    nc.scalar.activation(s.xt_hi[:, ch, :], bank[ch][:, :], ACT.Copy).then_inc(s.ap.xt_hi_ready.sem, 1)
                if due(16 * GROUP * g):
                    act.wait_ge(*s.ap.q_stored(16 * GROUP * g))
                for i in range(4):
                    act.wait_ge(*s.ap.qk_ready(4 * g + i + 1))
                    to = s.q_hl[:, 0, i, :] if i < 2 else s.kt_hi[:, i - 2, bass.ds(g * CHUNK, CHUNK)]
                    apart(act)
                    nc.scalar.activation(to, bank[2 + i][:, :], ACT.Identity, bias=s.bqk[:, i // 2, i % 2:i % 2 + 1],
                                         scale=1.0).then_inc(s.ap.qk_hi_ready.sem, 1)
                for tt in range(GROUP):
                    act.wait_ge(*s.ap.vr_biased(GROUP * g + tt + 1))
                    apart(act)
                    nc.scalar.activation(s.v[:, GROUP * g + tt, 0:D], s.vr[:, tt, 0:D], ACT.Copy)\
                        .then_inc(s.ap.v_hi_ready.sem, 1)

            steps(act, group, 0, 2, GROUPS, GROUPS)

        def ap_vector(dve, s, a):
            nvr = D * (2 if a == 0 else 1)
            dve.wait_ge(*s.ap.wt_ready(1))
            dve.wait_ge(*s.ap.wt_hi_ready(4))
            for ci in range(HALVES):
                nc.vector.tensor_tensor(s.wqk_lo[:, ci, :], bank[ci][:, :], s.wqk_hi[:, ci, :].bitcast(F32),
                                        ALU.subtract).then_inc(s.ap.wt_lo_ready.sem, 1)
                nc.vector.tensor_tensor(s.wvr_lo[:, ci, 0:nvr], bank[4 + ci][:, 0:nvr],
                                        s.wvr_hi[:, ci, 0:nvr].bitcast(F32), ALU.subtract)\
                    .then_inc(s.ap.wt_lo_ready.sem, 1)
            dve.wait_ge(*s.ap.consts_in(128 if a == 0 else 96))

            def group(g, p):
                if due(GROUP * g):
                    dve.wait_ge(*s.ap.vr_ready(GROUP * g))
                for ch in range(HALVES):
                    dve.wait_ge(*s.ap.xt_hi_ready(HALVES * g + ch + 1))
                    nc.vector.tensor_tensor(s.xt_lo[:, ch, :], bank[ch][:, :], s.xt_hi[:, ch, :].bitcast(F32),
                                            ALU.subtract).then_inc(s.ap.xt_lo_ready.sem, 1)
                if due(16 * GROUP * g):
                    dve.wait_ge(*s.ap.q_stored(16 * GROUP * g))
                for i in range(4):
                    dve.wait_ge(*s.ap.qk_hi_ready(4 * g + i + 1))
                    cols = bass.ds(g * CHUNK, CHUNK)
                    hi = s.q_hl[:, 0, i, :] if i < 2 else s.kt_hi[:, i - 2, cols]
                    lo = s.q_hl[:, 1, i, :] if i < 2 else s.kt_lo[:, i - 2, cols]
                    nc.vector.scalar_tensor_tensor(lo, bank[2 + i][:, :], s.bqk[:, i // 2, i % 2:i % 2 + 1],
                                                   hi.bitcast(F32), ALU.add, ALU.subtract).then_inc(s.ap.qk_lo_ready.sem, 1)
                if due(GROUP * g):
                    dve.wait_ge(*s.ap.v_hi_ready(GROUP * g))
                if a == 0:
                    if due(16 * g):
                        dve.wait_ge(*s.ap.res_stored(16 * g))
                for tt in range(GROUP):
                    dve.wait_ge(*s.ap.vr_ready(GROUP * g + tt + 1))
                    nc.vector.tensor_tensor(s.vr[:, tt, 0:nvr], bank[6 + tt % 2][:, 0:nvr], s.bvr[:, 0:nvr], ALU.add)\
                        .then_inc(s.ap.vr_biased.sem, 1)
                for tt in range(GROUP):
                    dve.wait_ge(*s.ap.v_hi_ready(GROUP * g + tt + 1))
                    nc.vector.tensor_tensor(s.v[:, GROUP * g + tt, D:2 * D], s.vr[:, tt, 0:D],
                                            s.v[:, GROUP * g + tt, 0:D].bitcast(F32), ALU.subtract)\
                        .then_inc(s.ap.v_lo_ready.sem, 1)

            steps(dve, group, 0, 2, GROUPS, GROUPS)

        def behind(t, p, c, lag):
            return (t - 1, 1 - p, c - lag) if c >= lag else (t - 2, p, c - lag + CHUNKS)

        def am_over(eng, s, a):
            eng.wait_ge(*s.am.pv_done(TILES * CHUNKS))
            eng.wait_ge(*s.am.hi_ready(TILES * CHUNKS))
            eng.wait_ge(*s.am.lo_ready(TILES * CHUNKS))
            eng.wait_ge(*s.am.o_lo_ready(TILES))
            eng.wait_ge(*s.am.y_ready(TILES))
            eng.wait_ge(*s.am.y_stored0(8 * TILES))
            eng.wait_ge(*s.am.y_stored1(8 * TILES))

        def am_sync(sp, s, a):
            dst = att_args[a][-1]
            res = res_dram if a == 0 else xa_dram

            def load_q(t, p):
                if due(CHUNKS * (t - 1)):
                    sp.wait_ge(*s.am.scores_ready(CHUNKS * (t - 1)))
                sp.dma_start([s.q0, s.q1][p][:, :, :, :].bitcast(F32),
                             q_dram[a].rearrange("t p (hl h n) -> t p hl h n", hl=2, h=HALVES)[t])\
                    .then_inc([s.am.q_in0, s.am.q_in1][p].sem, 16)

            def load_adj(t, q):
                if due(QUARTERS * (t - 1) + q + 1):
                    sp.wait_ge(*s.am.att_ready(QUARTERS * (t - 1) + q + 1))
                sp.dma_start(s.adj[:, q * QUARTER:(q + 1) * QUARTER], adj_quarters[t, q]).then_inc(
                    [s.am.adj_in0, s.am.adj_in1, s.am.adj_in2, s.am.adj_in3][q].sem, 16)

            def load_res(t, p):
                if due(t - 1):
                    sp.wait_ge(*s.am.y_ready(t - 1))
                sp.dma_start([s.res0, s.res1][p][:, :], node_tiles(res)[t]).then_inc([s.am.res_in0, s.am.res_in1][p].sem, 16)
                if a == 1:
                    sp.dma_start([s.xln0, s.xln1][p][:, :], node_tiles(x1_dram)[t]).then_inc(
                        [s.am.res_in0, s.am.res_in1][p].sem, 16)

            def store(t, p):
                sp.wait_ge(*s.am.y_ready(t + 1))
                sp.dma_start(node_tiles(dst)[t], [s.y0, s.y1][p][:, :]).then_inc([s.am.y_stored0, s.am.y_stored1][p].sem, 16)

            load_q(0, 0)

            def tile(t, p):
                if exists(t + 1):
                    load_q(t + 1, 1 - p)
                for q in range(QUARTERS):
                    if exists(t):
                        load_adj(t, q)
                    if q == 2 and exists(t - 2):
                        store(t - 2, p)
                        if exists(t):
                            load_res(t, p)
                    elif q == 2 and exists(t):
                        load_res(t, p)

            steps(sp, tile, 0, 4, TILES - 2, TILES + 2)

        def am_tensor(pe, s, a):

            def scores(t, p, c):
                k = CHUNKS * t + c
                if c == 0:
                    pe.wait_ge(*[s.am.q_in0, s.am.q_in1][p](8 * (t - p) + 16))
                if due(k - 3):
                    pe.wait_ge(*s.am.scores_taken(k - 3))
                q = [s.q0, s.q1][p]
                cols = slice(c * CHUNK, (c + 1) * CHUNK)
                parts = [(0, s.kt_hi, ch) for ch in range(HALVES)] + [(0, s.kt_lo, ch) for ch in range(HALVES)]\
                    + [(1, s.kt_hi, ch) for ch in range(HALVES)]
                for n, (hl, k_, ch) in enumerate(parts):
                    last = nc.tensor.matmul(bank[c % 4][:, :], q[:, hl, ch, :], k_[:, ch, cols], start=n == 0,
                                            stop=n == len(parts) - 1)
                last.then_inc(s.am.scores_ready.sem, 1)

            def transposes(t, p, c):
                g = CHUNKS * t + c
                if c % CPQ == 0:
                    pe.wait_ge(*s.am.att_ready(QUARTERS * t + c // CPQ + 1))
                if due(g - 1):
                    pe.wait_ge(*s.am.hi_ready(g - 1))
                if due(g - 1):
                    pe.wait_ge(*s.am.lo_ready(g - 1))
                for b in range(BLOCKS):
                    j = c * BLOCKS + b
                    last = nc.tensor.transpose(bank[4 + c % 2][:, b * P:(b + 1) * P],
                                               [s.s0, s.s1][p][:, j * P:(j + 1) * P], ident[:, :])
                last.then_inc(s.am.transposed.sem, 1)

            def values(t, p, c):
                g = CHUNKS * t + c
                if c == 0:
                    if due(t - 1):
                        pe.wait_ge(*s.am.o_taken(t - 1))
                pe.wait_ge(*s.am.hi_ready(g + 1))
                pe.wait_ge(*s.am.lo_ready(g + 1))
                hi, lo = [s.pt_hi0, s.pt_hi1][c % 2], [s.pt_lo0, s.pt_lo1][c % 2]
                for b in range(BLOCKS):
                    j = c * BLOCKS + b
                    w = slice(b * P, (b + 1) * P)
                    nc.tensor.matmul(bank[6 + p][:, :], hi[:, w], s.v[:, j, :], start=j == 0, stop=False)
                    last = nc.tensor.matmul(bank[6 + p][:, 0:D], lo[:, w], s.v[:, j, 0:D], start=False,
                                            stop=j == TILES - 1)
                last.then_inc(s.am.pv_done.sem, 1)

            def tile(t, p):
                for c in range(CHUNKS):
                    if exists(t):
                        scores(t, p, c)
                    if exists(behind(t, p, c, LAG)[0]):
                        transposes(*behind(t, p, c, LAG))
                    if exists(behind(t, p, c, LAG + 1)[0]):
                        values(*behind(t, p, c, LAG + 1))

            steps(pe, tile, 0, 4, TILES, TILES + 2)

        def am_scalar(act, s, a):

            def exponentials(t, p, q):
                if q == 0:
                    act.wait_ge(*s.am.bias_ready(t + 1))
                col = slice(q * QUARTER, (q + 1) * QUARTER)
                buf = [s.s0, s.s1][p][:, col]
                nc.scalar.activation(buf, buf, ACT.Exp, bias=s.bias[:, p:p + 1], scale=SCALE,
                                     accum_out=s.sum4[:, p, q:q + 1]).then_inc(s.am.exp_done.sem, 1)

            def tile(t, p):
                for c in range(CHUNKS):
                    tt, tp, tc = behind(t, p, c, LAG)
                    if exists(tt):
                        g = CHUNKS * tt + tc
                        act.wait_ge(*s.am.transposed(g + 1))
                        if due(g - 1):
                            act.wait_ge(*s.am.pv_done(g - 1))
                        nc.scalar.activation([s.pt_hi0, s.pt_hi1][tc % 2][:, :], bank[4 + tc % 2][:, :], ACT.Copy)\
                            .then_inc(s.am.hi_ready.sem, 1)
                    if c < 2 and exists(t - 1):
                        exponentials(t - 1, 1 - p, 2 * c)
                        exponentials(t - 1, 1 - p, 2 * c + 1)
                    if c == LAG + 2 and exists(t - 2):
                        if due(CHUNKS * (t - 1)):
                            act.wait_ge(*s.am.pv_done(CHUNKS * (t - 1)))
                        if due(t - 2):
                            act.wait_ge(*s.am.o_taken(t - 2))
                        nc.scalar.activation(s.o_lo[:, :], bank[6 + p][:, D:2 * D], ACT.Copy).then_inc(s.am.o_lo_ready.sem, 1)

            steps(act, tile, 0, 4, TILES, TILES + 2)

        def am_vector(dve, s, a):

            def take_scores(t, p, c):
                dve.wait_ge(*s.am.scores_ready(CHUNKS * t + c + 1))
                nc.vector.tensor_scalar([s.s0, s.s1][p][:, c * CHUNK:(c + 1) * CHUNK], bank[c % 4][:, :], 1.0, None,
                                        ALU.mult, ALU.max, accum_out=s.max8[:, p, c:c + 1])\
                    .then_inc(s.am.scores_taken.sem, 1)

            def row_max(t, p):
                dve.wait_ge(*s.am.scores_taken(CHUNKS * (t + 1)))
                nc.vector.tensor_reduce(s.neg_max[:, :], s.max8[:, p, :], AX.X, ALU.max, negate=True)\
                    .then_inc(s.am.max_ready.sem, 1)
                dve.wait_ge(*s.am.max_ready(t + 1))
                nc.vector.tensor_scalar(s.bias[:, p:p + 1], s.neg_max[:, :], SCALE, None, ALU.mult)\
                    .then_inc(s.am.bias_ready.sem, 1)

            def row_sum(t, p):
                dve.wait_ge(*s.am.exp_done(QUARTERS * (t + 1)))
                nc.vector.reduce_sum(s.total[:, :], s.sum4[:, p, :], AX.X).then_inc(s.am.sum_ready.sem, 1)
                dve.wait_ge(*s.am.sum_ready(t + 1))
                nc.vector.reciprocal(s.rinv[:, :], s.total[:, :]).then_inc(s.am.rinv_ready.sem, 1)
                dve.wait_ge(*s.am.rinv_ready(t + 1))

            def attention_rows(t, p, q):
                col = slice(q * QUARTER, (q + 1) * QUARTER)
                dve.wait_ge(*[s.am.adj_in0, s.am.adj_in1, s.am.adj_in2, s.am.adj_in3][q](16 * (t + 1)))
                buf = [s.s0, s.s1][p][:, col]
                nc.vector.scalar_tensor_tensor(buf, buf, s.rinv[:, :], s.adj[:, col], ALU.mult, ALU.add)\
                    .then_inc(s.am.att_ready.sem, 1)

            def finish(t, p):
                dve.wait_ge(*s.am.o_lo_ready(t + 1))
                nc.vector.tensor_tensor(s.o[:, :], bank[6 + p][:, 0:D], s.o_lo[:, :], ALU.add).then_inc(s.am.o_taken.sem, 1)
                dve.wait_ge(*s.am.o_taken(t + 1))
                dve.wait_ge(*[s.am.res_in0, s.am.res_in1][p]((8 * (t - p) + 16) * (1 + a)))
                if due(8 * (t - p)):
                    dve.wait_ge(*[s.am.y_stored0, s.am.y_stored1][p](8 * (t - p)))
                y, res = [s.y0, s.y1][p], [s.res0, s.res1][p]
                if a == 0:
                    nc.vector.scalar_tensor_tensor(y[:, :], s.o[:, :], 0.0, res[:, :], ALU.max, ALU.add)\
                        .then_inc(s.am.y_ready.sem, 1)
                    return
                nc.vector.scalar_tensor_tensor(s.o[:, :], s.o[:, :], 0.0, res[:, :], ALU.max, ALU.add)\
                    .then_inc(s.am.residual_added.sem, 1)
                dve.wait_ge(*s.am.residual_added(t + 1))
                nc.vector.tensor_tensor(s.o[:, :], s.o[:, :], [s.xln0, s.xln1][p][:, :], ALU.add)\
                    .then_inc(s.am.x1_added.sem, 1)
                dve.wait_ge(*s.am.x1_added(t + 1))
                layer_norm(dve, s, s.am, s.o, y, t)

            def tile(t, p):
                for c in range(CHUNKS):
                    if exists(t):
                        take_scores(t, p, c)
                    tt, tp, tc = behind(t, p, c, LAG)
                    if exists(tt):
                        g = CHUNKS * tt + tc
                        dve.wait_ge(*s.am.transposed(g + 1))
                        dve.wait_ge(*s.am.hi_ready(g + 1))
                        if due(g - 1):
                            dve.wait_ge(*s.am.pv_done(g - 1))
                        nc.vector.tensor_tensor([s.pt_lo0, s.pt_lo1][tc % 2][:, :], bank[4 + tc % 2][:, :],
                                                [s.pt_hi0, s.pt_hi1][tc % 2][:, :].bitcast(F32), ALU.subtract)\
                            .then_inc(s.am.lo_ready.sem, 1)
                    if exists(t - 1):
                        if c == LAG - 1:
                            row_sum(t - 1, 1 - p)
                        if c in (LAG - 1, LAG, LAG + 2, LAG + 4):
                            attention_rows(t - 1, 1 - p, (LAG - 1, LAG, LAG + 2, LAG + 4).index(c))
                    if c == LAG + 2 and exists(t - 2):
                        finish(t - 2, p)
                    if c == CHUNKS - 1 and exists(t):
                        row_max(t, p)

            steps(dve, tile, 0, 4, TILES, TILES + 2)

        def am_pool(pool, s):
            inverse_roots(pool, s, s.am)

        block = top.enter_context(nc.Block())

        @block.sync
        def _(sp):
            for a, s in enumerate(gat):
                gp_sync(sp, s, a)
                gp_over(sp, s, a)
                gm_sync(sp, s, a)
                gm_over(sp, s, a)
            for a, s in enumerate(att):
                ap_sync(sp, s, a)
                ap_over(sp, s, a)
                am_sync(sp, s, a)
                am_over(sp, s, a)

        @block.gpsimd
        def _(pool):
            nc.gpsimd.memset(ident[:, :], 0.0).then_inc(ident_step, 1)
            nc.gpsimd.memset(off_diag[:, :], 1.0).then_inc(ident_step, 1)
            nc.gpsimd.memset(ones[:, :], 1.0).then_inc(consts_ready, 1)
            nc.gpsimd.memset(power[:, :], -0.5).then_inc(consts_ready, 1)
            pool.wait_ge(ident_step, 2)
            for m, fill in ((ident, 1.0), (off_diag, 0.0)):
                nc.gpsimd.affine_select(out=m[:, :], in_=m[:, :], compare_op=ALU.not_equal, fill=fill, base=0,
                                        pattern=[[-1, P]], channel_multiplier=1).then_inc(consts_ready, 1)
            pool.wait_ge(consts_ready, 4)
            gp_over(pool, gat[1], 1)
            gm_pool(pool, gat[1])
            ap_over(pool, att[1], 1)
            am_pool(pool, att[1])

        @block.tensor
        def _(pe):
            pe.wait_ge(consts_ready, 4)
            for a, s in enumerate(gat):
                gp_tensor(pe, s, a)
                gp_over(pe, s, a)
                gm_tensor(pe, s, a)
                gm_over(pe, s, a)
            for a, s in enumerate(att):
                ap_tensor(pe, s, a)
                ap_over(pe, s, a)
                am_tensor(pe, s, a)
                am_over(pe, s, a)

        @block.scalar
        def _(act):
            for a, s in enumerate(gat):
                gp_scalar(act, s, a)
                gp_over(act, s, a)
                gm_scalar(act, s, a)
                gm_over(act, s, a)
            for a, s in enumerate(att):
                ap_scalar(act, s, a)
                ap_over(act, s, a)
                am_scalar(act, s, a)
                am_over(act, s, a)

        @block.vector
        def _(dve):
            dve.wait_ge(consts_ready, 4)
            for a, s in enumerate(gat):
                gp_vector(dve, s, a)
                gp_over(dve, s, a)
                gm_vector(dve, s, a)
                gm_over(dve, s, a)
            for a, s in enumerate(att):
                ap_vector(dve, s, a)
                ap_over(dve, s, a)
                am_vector(dve, s, a)
                am_over(dve, s, a)


_INS = ['x', 'adj', 'L0_gnn_W1', 'L0_gnn_b1', 'L0_gnn_asrc1', 'L0_gnn_adst1', 'L0_gnn_W2', 'L0_gnn_b2',
        'L0_gnn_asrc2', 'L0_gnn_adst2', 'L1_gnn_wq0', 'L1_gnn_bq0', 'L1_gnn_wk0', 'L1_gnn_bk0', 'L1_gnn_wv0',
        'L1_gnn_bv0', 'L1_gnn_wres', 'L1_gnn_bres', 'L1_gnn_wq1', 'L1_gnn_bq1', 'L1_gnn_wk1', 'L1_gnn_bk1',
        'L1_gnn_wv1', 'L1_gnn_bv1']


def kernel(**inputs):
    import concourse.bacc as bacc
    from concourse.bass_utils import run_bass_kernel_spmd

    nc = bacc.Bacc("TRN2", target_bir_lowering=False, num_devices=1)
    arrays, args = {}, []
    for name in _INS:
        a = np.ascontiguousarray(inputs[name])
        arrays[f"in_{name}"] = a
        args.append(nc.dram_tensor(f"in_{name}", a.shape, mybir.dt.from_np(a.dtype), kind="ExternalInput").ap())
    out = nc.dram_tensor("out", (N, D), F32, kind="ExternalOutput").ap()
    build(nc, *args, out)
    r = run_bass_kernel_spmd(nc, [arrays], core_ids=[0])
    return r.results[0]["out"]
```

```python
import numpy as np
import concourse.bass as bass
from concourse import mybir
from contextlib import ExitStack

F32 = mybir.dt.float32
F32R = mybir.dt.float32r
BF16 = mybir.dt.bfloat16
ACT = mybir.ActivationFunctionType
ALU = mybir.AluOpType
AX = mybir.AxisListType

P = 128
N = 4096
D = 256
TILES = N // P
HALVES = D // P
CHUNK = 512
CHUNKS = N // CHUNK
BLOCKS = CHUNK // P
QUARTER = 1024
QUARTERS = N // QUARTER
CPQ = CHUNKS // QUARTERS
GROUP = 4
GROUPS = TILES // GROUP
SCALE = 1.0 / 16.0
SLOPE = 0.2
EPS = 1e-5
MASKED = -1e38
EXP_LAG = 2
GAT_LAG = 5
LOW_BY_PE = ((0, 1, 2, 4, 5, 6), (1, 2, 5, 6))
LAG = 3


class Signal:

    def __init__(self, sem, base):
        self.sem, self.base = sem, base

    def __call__(self, count):
        return self.sem, count + self.base


def due(count):
    return not isinstance(count, int) or count > 0


def steps(eng, body, first, steady, steady_end, last):
    for t in range(first, steady):
        body(t, t % 2)
    with eng.Fori(steady // 2, steady_end // 2) as u:
        body(2 * u, 0)
        body(2 * u + 1, 1)
    for t in range(steady_end, last):
        body(t, t % 2)


def exists(t):
    return not isinstance(t, int) or 0 <= t < TILES


def build(nc, x, adj, W1, b1, asrc1, adst1, W2, b2, asrc2, adst2,
          wq0, bq0, wk0, bk0, wv0, bv0, wres, bres, wq1, bq1, wk1, bk1, wv1, bv1, out):
    top = ExitStack()
    count = [0]

    def sem(name):
        count[0] += 1
        return top.enter_context(nc.semaphore(name))

    def scratch(name, shape, dt):
        return nc.dram_tensor(name, shape, dt, kind="Internal").ap()

    mask_dram = scratch("mask_scratch", (TILES, P, N), BF16)
    h1_dram = scratch("h1_scratch", (N, D), F32)
    x1_dram = scratch("x1_scratch", (N, D), F32)
    xa_dram = scratch("xa_scratch", (N, D), F32)
    res_dram = scratch("res_scratch", (N, D), F32)
    q_dram = [scratch(f"q_scratch{a}", (TILES, P, 2 * HALVES * P), F32) for a in range(2)]

    with top:
        ident = top.enter_context(nc.sbuf_tensor("ident", [P, P], F32))
        ones = top.enter_context(nc.sbuf_tensor("ones", [P, P], F32))
        power = top.enter_context(nc.sbuf_tensor("power", [P, 1], F32))
        bank = [top.enter_context(nc.psum_tensor(f"bank{i}", [P, CHUNK], F32)) for i in range(8)]
        off_diag = top.enter_context(nc.sbuf_tensor("off_diag", [P, P], F32))
        neg_ident = top.enter_context(nc.sbuf_tensor("neg_ident", [P, P], F32R))
        neg_ident_ready = sem("neg_ident_ready")
        ident_step = sem("ident_step")
        consts_ready = sem("consts_ready")
        waits_passed = sem("waits_passed")

        class Space:
            pass

        def sb(mem, name, shape, dt):
            return mem.enter_context(nc.sbuf_tensor(name, shape, dt))

        handles = {}

        def signal(name, a, total):
            if name not in handles:
                handles[name] = sem(name)
            return Signal(handles[name], a * total)

        def gat_layer(a):
            s = Space()
            with ExitStack() as kept:
                s.hv = sb(kept, f"g{a}_hv", [P, TILES, 2 * D], F32R)
                s.s_row = sb(kept, f"g{a}_s_row", [P, N], F32)
                s.d_col = sb(kept, f"g{a}_d_col", [P, TILES], F32)
                with ExitStack() as projection:
                    s.w_in = sb(projection, f"gp{a}_w_in", [P, HALVES, D], F32)
                    s.w_hi = sb(projection, f"gp{a}_w_hi", [P, HALVES, D], F32R)
                    s.w_lo = sb(projection, f"gp{a}_w_lo", [P, HALVES, D], F32R)
                    s.asrc = sb(projection, f"gp{a}_asrc", [P, D], F32)
                    s.adst = sb(projection, f"gp{a}_adst", [P, D], F32)
                    s.xin0 = sb(projection, f"gp{a}_xin0", [P, GROUP, D], F32)
                    s.xin1 = sb(projection, f"gp{a}_xin1", [P, GROUP, D], F32)
                    s.xt_hi = sb(projection, f"gp{a}_xt_hi", [P, HALVES, CHUNK], F32R)
                    s.xt_lo = sb(projection, f"gp{a}_xt_lo", [P, HALVES, CHUNK], F32R)
                    s.h = sb(projection, f"gp{a}_h", [P, GROUP, D], F32)
                    s.junk = sb(projection, f"gp{a}_junk", [P, D], F32)
                    s.s4 = sb(projection, f"gp{a}_s4", [P, GROUP], F32)
                    s.d4 = sb(projection, f"gp{a}_d4", [P, GROUP], F32)
                    s.diag = sb(projection, f"gp{a}_diag", [P, CHUNK], F32)
                with ExitStack() as main:
                    s.bias = sb(main, f"gm{a}_bias", [P, D], F32)
                    s.adj = sb(main, f"gm{a}_adj", [P, N], F32)
                    s.mask0 = sb(main, f"gm{a}_mask0", [P, N], BF16)
                    s.mask1 = sb(main, f"gm{a}_mask1", [P, N], BF16)
                    s.t0 = sb(main, f"gm{a}_t0", [P, N], F32)
                    s.t1 = sb(main, f"gm{a}_t1", [P, N], F32)
                    s.pt_hi = [sb(main, f"gm{a}_pt_hi{i}", [P, CHUNK], F32R) for i in range(4)]
                    s.pt_lo = [sb(main, f"gm{a}_pt_lo{i}", [P, CHUNK], F32R) for i in range(4)]
                    s.max4 = sb(main, f"gm{a}_max4", [P, QUARTERS], F32)
                    s.smax = sb(main, f"gm{a}_smax", [P, 1], F32)
                    s.zmax = sb(main, f"gm{a}_zmax", [P, 1], F32)
                    s.m = sb(main, f"gm{a}_m", [P, 1], F32)
                    s.k_pos = sb(main, f"gm{a}_k_pos", [P, 2], F32)
                    s.k_neg = sb(main, f"gm{a}_k_neg", [P, 2], F32)
                    s.v = sb(main, f"gm{a}_v", [P, N], F32)
                    s.sum4 = sb(main, f"gm{a}_sum4", [P, 2, QUARTERS], F32)
                    s.total = sb(main, f"gm{a}_total", [P, 1], F32)
                    s.rinv = sb(main, f"gm{a}_rinv", [P, 2], F32)
                    s.o_lo = sb(main, f"gm{a}_o_lo", [P, D], F32)
                    s.o = sb(main, f"gm{a}_o", [P, D], F32)
                    s.xres0 = sb(main, f"gm{a}_xres0", [P, D], F32)
                    s.xres1 = sb(main, f"gm{a}_xres1", [P, D], F32)
                    s.stats = sb(main, f"gm{a}_stats", [P, 6], F32)
                    s.mv = sb(main, f"gm{a}_mv", [P, 2], F32)
                    s.ve = sb(main, f"gm{a}_ve", [P, 1], F32)
                    s.rstd = sb(main, f"gm{a}_rstd", [P, 1], F32)
                    s.y0 = sb(main, f"gm{a}_y0", [P, D], F32)
                    s.y1 = sb(main, f"gm{a}_y1", [P, D], F32)
            s.gp = k = Space()
            k.consts_in = signal("gp_consts_in", a, 3 * 16)
            k.x_in0 = signal("gp_x_in0", a, 8 * GROUPS)
            k.x_in1 = signal("gp_x_in1", a, 8 * GROUPS)
            k.w_hi_ready = signal("gp_w_hi_ready", a, 1)
            k.w_lo_ready = signal("gp_w_lo_ready", a, 1)
            k.xt_ready = signal("gp_xt_ready", a, HALVES * GROUPS)
            k.xt_hi_ready = signal("gp_xt_hi_ready", a, HALVES * GROUPS)
            k.xt_lo_ready = signal("gp_xt_lo_ready", a, HALVES * GROUPS)
            k.h_ready = signal("gp_h_ready", a, TILES)
            k.h_stored = signal("gp_h_stored", a, TILES)
            k.hv_hi_ready = signal("gp_hv_hi_ready", a, TILES)
            k.hv_lo_ready = signal("gp_hv_lo_ready", a, TILES)
            k.dots_ready = signal("gp_dots_ready", a, 2 * TILES)
            k.diag_ready = signal("gp_diag_ready", a, GROUPS)
            k.s_bcast_ready = signal("gp_s_bcast_ready", a, GROUPS)
            k.s_row_ready = signal("gp_s_row_ready", a, GROUPS)
            k.d_ready = signal("gp_d_ready", a, GROUPS)
            s.gm = k = Space()
            k.bias_in = signal("gm_bias_in", a, 16)
            k.adj_in0 = signal("gm_adj_in0", a, 16 * TILES)
            k.adj_in1 = signal("gm_adj_in1", a, 16 * TILES)
            k.adj_in2 = signal("gm_adj_in2", a, 16 * TILES)
            k.adj_in3 = signal("gm_adj_in3", a, 16 * TILES)
            k.x_res_in0 = signal("gm_x_res_in0", a, 0)
            k.x_res_in1 = signal("gm_x_res_in1", a, 0)
            k.mask_in0 = signal("gm_mask_in0", a, 0)
            k.mask_in1 = signal("gm_mask_in1", a, 0)
            k.nb_ready = signal("gm_nb_ready", a, QUARTERS * TILES)
            k.mask_ready = signal("gm_mask_ready", a, TILES)
            k.mask_stored0 = signal("gm_mask_stored0", a, 8 * TILES)
            k.mask_stored1 = signal("gm_mask_stored1", a, 8 * TILES)
            k.subtracted = signal("gm_subtracted", a, len(LOW_BY_PE[0]) * TILES)
            k.lo_act_ready = signal("gm_lo_act_ready", a, len(LOW_BY_PE[0]) * TILES)
            k.t_ready = signal("gm_t_ready", a, QUARTERS * TILES)
            k.smax_ready = signal("gm_smax_ready", a, TILES)
            k.zmax_ready = signal("gm_zmax_ready", a, TILES)
            k.m_ready = signal("gm_m_ready", a, TILES)
            k.k_ready = signal("gm_k_ready", a, 2 * TILES)
            k.v_ready = signal("gm_v_ready", a, QUARTERS * TILES)
            k.leaky_ready = signal("gm_leaky_ready", a, QUARTERS * TILES)
            k.p_ready = signal("gm_p_ready", a, QUARTERS * TILES)
            k.transposed = signal("gm_transposed", a, CHUNKS * TILES)
            k.hi_ready = signal("gm_hi_ready", a, CHUNKS * TILES)
            k.lo_ready = signal("gm_lo_ready", a, (CHUNKS - len(LOW_BY_PE[0])) * TILES)
            k.pv_done = signal("gm_pv_done", a, CHUNKS * TILES)
            k.o_lo_ready = signal("gm_o_lo_ready", a, TILES)
            k.o_taken = signal("gm_o_taken", a, TILES)
            k.sum_ready = signal("gm_sum_ready", a, TILES)
            k.rinv_ready = signal("gm_rinv_ready", a, TILES)
            k.biased = signal("gm_biased", a, TILES)
            k.residual_added = signal("gm_residual_added", a, 0)
            k.stats_ready = signal("gm_stats_ready", a, 0)
            k.mean_ready = signal("gm_mean_ready", a, 0)
            k.ve_ready = signal("gm_ve_ready", a, 0)
            k.rstd_ready = signal("gm_rstd_ready", a, 0)
            k.y_ready = signal("gm_y_ready", a, TILES)
            k.y_stored0 = signal("gm_y_stored0", a, 8 * TILES)
            k.y_stored1 = signal("gm_y_stored1", a, 8 * TILES)
            return s

        def att_layer(a):
            s = Space()
            with ExitStack() as kept:
                s.kt_hi = sb(kept, f"a{a}_kt_hi", [P, HALVES, N], F32R)
                s.kt_lo = sb(kept, f"a{a}_kt_lo", [P, HALVES, N], F32R)
                s.v = sb(kept, f"a{a}_v", [P, TILES, 2 * D], F32R)
                with ExitStack() as projection:
                    s.wn = sb(projection, f"ap{a}_wn", [P, 4, HALVES, D], F32)
                    s.wqk_hi = sb(projection, f"ap{a}_wqk_hi", [P, HALVES, 2 * D], F32R)
                    s.wqk_lo = sb(projection, f"ap{a}_wqk_lo", [P, HALVES, 2 * D], F32R)
                    s.wvr_hi = sb(projection, f"ap{a}_wvr_hi", [P, HALVES, 2 * D], F32R)
                    s.wvr_lo = sb(projection, f"ap{a}_wvr_lo", [P, HALVES, 2 * D], F32R)
                    s.bqk = sb(projection, f"ap{a}_bqk", [P, 2, HALVES], F32)
                    s.bvr = sb(projection, f"ap{a}_bvr", [P, 2 * D], F32)
                    s.xin0 = sb(projection, f"ap{a}_xin0", [P, GROUP, D], F32)
                    s.xin1 = sb(projection, f"ap{a}_xin1", [P, GROUP, D], F32)
                    s.xt_hi = sb(projection, f"ap{a}_xt_hi", [P, HALVES, CHUNK], F32R)
                    s.xt_lo = sb(projection, f"ap{a}_xt_lo", [P, HALVES, CHUNK], F32R)
                    s.q_hl = sb(projection, f"ap{a}_q_hl", [P, 2, HALVES, CHUNK], F32R)
                    s.vr = sb(projection, f"ap{a}_vr", [P, GROUP, 2 * D], F32)
                with ExitStack() as main:
                    s.adj = sb(main, f"am{a}_adj", [P, N], F32)
                    s.s0 = sb(main, f"am{a}_s0", [P, N], F32)
                    s.s1 = sb(main, f"am{a}_s1", [P, N], F32)
                    s.q0 = sb(main, f"am{a}_q0", [P, 2, HALVES, P], F32R)
                    s.q1 = sb(main, f"am{a}_q1", [P, 2, HALVES, P], F32R)
                    s.pt_hi0 = sb(main, f"am{a}_pt_hi0", [P, CHUNK], F32R)
                    s.pt_hi1 = sb(main, f"am{a}_pt_hi1", [P, CHUNK], F32R)
                    s.pt_lo0 = sb(main, f"am{a}_pt_lo0", [P, CHUNK], F32R)
                    s.pt_lo1 = sb(main, f"am{a}_pt_lo1", [P, CHUNK], F32R)
                    s.max8 = sb(main, f"am{a}_max8", [P, 2, CHUNKS], F32)
                    s.neg_max = sb(main, f"am{a}_neg_max", [P, 1], F32)
                    s.bias = sb(main, f"am{a}_bias", [P, 2], F32)
                    s.sum4 = sb(main, f"am{a}_sum4", [P, 2, QUARTERS], F32)
                    s.total = sb(main, f"am{a}_total", [P, 1], F32)
                    s.rinv = sb(main, f"am{a}_rinv", [P, 1], F32)
                    s.o_lo = sb(main, f"am{a}_o_lo", [P, D], F32)
                    s.o = sb(main, f"am{a}_o", [P, D], F32)
                    s.res0 = sb(main, f"am{a}_res0", [P, D], F32)
                    s.res1 = sb(main, f"am{a}_res1", [P, D], F32)
                    s.xln0 = sb(main, f"am{a}_xln0", [P, D], F32)
                    s.xln1 = sb(main, f"am{a}_xln1", [P, D], F32)
                    s.stats = sb(main, f"am{a}_stats", [P, 6], F32)
                    s.mv = sb(main, f"am{a}_mv", [P, 2], F32)
                    s.ve = sb(main, f"am{a}_ve", [P, 1], F32)
                    s.rstd = sb(main, f"am{a}_rstd", [P, 1], F32)
                    s.y0 = sb(main, f"am{a}_y0", [P, D], F32)
                    s.y1 = sb(main, f"am{a}_y1", [P, D], F32)
            s.ap = k = Space()
            k.consts_in = signal("ap_consts_in", a, 8 * 16)
            k.x_in0 = signal("ap_x_in0", a, 8 * GROUPS)
            k.x_in1 = signal("ap_x_in1", a, 8 * GROUPS)
            k.wt_ready = signal("ap_wt_ready", a, 1)
            k.wt_hi_ready = signal("ap_wt_hi_ready", a, 4)
            k.wt_lo_ready = signal("ap_wt_lo_ready", a, 4)
            k.xt_ready = signal("ap_xt_ready", a, HALVES * GROUPS)
            k.xt_hi_ready = signal("ap_xt_hi_ready", a, HALVES * GROUPS)
            k.xt_lo_ready = signal("ap_xt_lo_ready", a, HALVES * GROUPS)
            k.qk_ready = signal("ap_qk_ready", a, 4 * GROUPS)
            k.qk_hi_ready = signal("ap_qk_hi_ready", a, 4 * GROUPS)
            k.qk_lo_ready = signal("ap_qk_lo_ready", a, 4 * GROUPS)
            k.q_stored = signal("ap_q_stored", a, 16 * TILES)
            k.vr_ready = signal("ap_vr_ready", a, TILES)
            k.vr_biased = signal("ap_vr_biased", a, TILES)
            k.v_hi_ready = signal("ap_v_hi_ready", a, TILES)
            k.v_lo_ready = signal("ap_v_lo_ready", a, TILES)
            k.res_stored = signal("ap_res_stored", a, 16 * GROUPS)
            s.am = k = Space()
            k.q_in0 = signal("am_q_in0", a, 8 * TILES)
            k.q_in1 = signal("am_q_in1", a, 8 * TILES)
            k.adj_in0 = signal("am_adj_in0", a, 16 * TILES)
            k.adj_in1 = signal("am_adj_in1", a, 16 * TILES)
            k.adj_in2 = signal("am_adj_in2", a, 16 * TILES)
            k.adj_in3 = signal("am_adj_in3", a, 16 * TILES)
            k.res_in0 = signal("am_res_in0", a, 8 * TILES)
            k.res_in1 = signal("am_res_in1", a, 8 * TILES)
            k.scores_ready = signal("am_scores_ready", a, CHUNKS * TILES)
            k.scores_taken = signal("am_scores_taken", a, CHUNKS * TILES)
            k.max_ready = signal("am_max_ready", a, TILES)
            k.bias_ready = signal("am_bias_ready", a, TILES)
            k.exp_done = signal("am_exp_done", a, QUARTERS * TILES)
            k.att_ready = signal("am_att_ready", a, QUARTERS * TILES)
            k.transposed = signal("am_transposed", a, CHUNKS * TILES)
            k.hi_ready = signal("am_hi_ready", a, CHUNKS * TILES)
            k.lo_ready = signal("am_lo_ready", a, CHUNKS * TILES)
            k.pv_done = signal("am_pv_done", a, CHUNKS * TILES)
            k.o_lo_ready = signal("am_o_lo_ready", a, TILES)
            k.o_taken = signal("am_o_taken", a, TILES)
            k.sum_ready = signal("am_sum_ready", a, TILES)
            k.rinv_ready = signal("am_rinv_ready", a, TILES)
            k.residual_added = signal("am_residual_added", a, 0)
            k.x1_added = signal("am_x1_added", a, 0)
            k.stats_ready = signal("am_stats_ready", a, 0)
            k.mean_ready = signal("am_mean_ready", a, 0)
            k.ve_ready = signal("am_ve_ready", a, 0)
            k.rstd_ready = signal("am_rstd_ready", a, 0)
            k.y_ready = signal("am_y_ready", a, TILES)
            k.y_stored0 = signal("am_y_stored0", a, 8 * TILES)
            k.y_stored1 = signal("am_y_stored1", a, 8 * TILES)
            return s

        gat = [gat_layer(a) for a in range(2)]
        att = [att_layer(a) for a in range(2)]

        gat_args = [(x, W1, b1, asrc1, adst1, h1_dram), (h1_dram, W2, b2, asrc2, adst2, x1_dram)]
        att_args = [(x1_dram, wq0, bq0, wk0, bk0, wv0, bv0, wres, bres, xa_dram),
                    (xa_dram, wq1, bq1, wk1, bk1, wv1, bv1, None, None, out)]
        adj_quarters = adj.rearrange("(t p) (q n) -> t q p n", p=P, n=QUARTER)

        def node_tiles(t):
            return t.rearrange("(t p) d -> t p d", p=P)

        def node_groups(t):
            return t.rearrange("(g t p) d -> g p t d", p=P, t=GROUP)

        def on_all_partitions(v):
            return v.rearrange("(a d) -> a d", a=1).broadcast_to([P, v.shape[0]])

        def halves(w):
            return w.rearrange("(h p) d -> p h d", p=P)

        def behind(t, p, c, lag):
            return (t - 1, 1 - p, c - lag) if c >= lag else (t - 2, p, c - lag + CHUNKS)

        def apart(eng):
            eng.sem_inc(waits_passed, 1)

        def gp_over(eng, s, a):
            eng.wait_ge(*s.gp.h_ready(TILES))
            eng.wait_ge(*s.gp.hv_hi_ready(TILES))
            eng.wait_ge(*s.gp.hv_lo_ready(TILES))
            eng.wait_ge(*s.gp.s_row_ready(GROUPS))
            eng.wait_ge(*s.gp.d_ready(GROUPS))
            eng.wait_ge(*s.gp.s_bcast_ready(GROUPS))

        def gp_sync(sp, s, a):
            src, W, _, asrc, adst, _ = gat_args[a]
            sp.dma_start(s.w_in[:, :, :], halves(W)).then_inc(s.gp.consts_in.sem, 16)
            sp.dma_start(s.asrc[:, :], on_all_partitions(asrc)).then_inc(s.gp.consts_in.sem, 16)
            sp.dma_start(s.adst[:, :], on_all_partitions(adst)).then_inc(s.gp.consts_in.sem, 16)

            def load(g, p):
                if due(HALVES * (g - 1)):
                    sp.wait_ge(*s.gp.xt_ready(HALVES * (g - 1)))
                sp.dma_start([s.xin0, s.xin1][p][:, :, :], node_groups(src)[g]).then_inc([s.gp.x_in0, s.gp.x_in1][p].sem, 16)

            steps(sp, load, 0, 2, GROUPS, GROUPS)

        def gp_tensor(pe, s, a):
            pe.wait_ge(*s.gp.w_hi_ready(1))
            pe.wait_ge(*s.gp.w_lo_ready(1))

            def group(g, p):
                pe.wait_ge(*[s.gp.x_in0, s.gp.x_in1][p](8 * (g - p) + 16))
                if due(HALVES * (g - 1)):
                    pe.wait_ge(*s.gp.xt_hi_ready(HALVES * (g - 1)))
                if due(HALVES * (g - 1)):
                    pe.wait_ge(*s.gp.xt_lo_ready(HALVES * (g - 1)))
                xin = [s.xin0, s.xin1][p]
                for ch in range(HALVES):
                    for tt in range(GROUP):
                        last = nc.tensor.transpose(bank[2 * p + ch][:, tt * P:(tt + 1) * P],
                                                   xin[:, tt, ch * P:(ch + 1) * P], ident[:, :])
                    last.then_inc(s.gp.xt_ready.sem, 1)
                pe.wait_ge(*s.gp.xt_hi_ready(HALVES * (g + 1)))
                pe.wait_ge(*s.gp.xt_lo_ready(HALVES * (g + 1)))
                for tt in range(GROUP):
                    if due(GROUP * g + tt - 1):
                        pe.wait_ge(*s.gp.h_stored(GROUP * g + tt - 1))
                    o = bank[4 + tt % 2][:, 0:D]
                    c = slice(tt * P, (tt + 1) * P)
                    parts = [(x_, w_, ch) for ch in range(HALVES)
                             for x_, w_ in ((s.xt_hi, s.w_hi), (s.xt_hi, s.w_lo), (s.xt_lo, s.w_hi))]
                    for i, (x_, w_, ch) in enumerate(parts):
                        last = nc.tensor.matmul(o, x_[:, ch, c], w_[:, ch, :], start=i == 0, stop=i == len(parts) - 1)
                    last.then_inc(s.gp.h_ready.sem, 1)
                pe.wait_ge(*s.gp.diag_ready(g + 1))
                if due(g):
                    pe.wait_ge(*s.gp.s_row_ready(g))
                nc.tensor.matmul(bank[6][:, :], ones[:, :], s.diag[:, :], start=True, stop=True)\
                    .then_inc(s.gp.s_bcast_ready.sem, 1)

            steps(pe, group, 0, 2, GROUPS, GROUPS)

        def gp_scalar(act, s, a):
            act.wait_ge(*s.gp.consts_in(48))
            nc.scalar.activation(s.w_hi[:, :, :], s.w_in[:, :, :], ACT.Copy).then_inc(s.gp.w_hi_ready.sem, 1)

            def group(g, p):
                if due(GROUP * g):
                    act.wait_ge(*s.gp.h_ready(GROUP * g))
                for ch in range(HALVES):
                    act.wait_ge(*s.gp.xt_ready(HALVES * g + ch + 1))
                    nc.scalar.activation(s.xt_hi[:, ch, :], bank[2 * p + ch][:, :], ACT.Copy).then_inc(s.gp.xt_hi_ready.sem, 1)
                for tt in range(GROUP):
                    act.wait_ge(*s.gp.h_stored(GROUP * g + tt + 1))
                    apart(act)
                    nc.scalar.activation(s.hv[:, GROUP * g + tt, 0:D], s.h[:, tt, :], ACT.Copy)\
                        .then_inc(s.gp.hv_hi_ready.sem, 1)
                act.wait_ge(*s.gp.s_bcast_ready(g + 1))
                apart(act)
                nc.scalar.activation(s.s_row[:, bass.ds(g * CHUNK, CHUNK)], bank[6][:, :], ACT.Copy)\
                    .then_inc(s.gp.s_row_ready.sem, 1)

            steps(act, group, 0, 2, GROUPS, GROUPS)

        def gp_vector(dve, s, a):
            dve.wait_ge(*s.gp.w_hi_ready(1))
            nc.vector.tensor_tensor(s.w_lo[:, :, :], s.w_in[:, :, :], s.w_hi[:, :, :].bitcast(F32), ALU.subtract)\
                .then_inc(s.gp.w_lo_ready.sem, 1)

            def group(g, p):
                if due(GROUP * g):
                    dve.wait_ge(*s.gp.h_ready(GROUP * g))
                for ch in range(HALVES):
                    dve.wait_ge(*s.gp.xt_hi_ready(HALVES * g + ch + 1))
                    nc.vector.tensor_tensor(s.xt_lo[:, ch, :], bank[2 * p + ch][:, :],
                                            s.xt_hi[:, ch, :].bitcast(F32), ALU.subtract).then_inc(s.gp.xt_lo_ready.sem, 1)
                if due(GROUP * g):
                    dve.wait_ge(*s.gp.hv_hi_ready(GROUP * g))
                for tt in range(GROUP):
                    dve.wait_ge(*s.gp.h_ready(GROUP * g + tt + 1))
                    nc.vector.tensor_copy(s.h[:, tt, :], bank[4 + tt % 2][:, 0:D]).then_inc(s.gp.h_stored.sem, 1)
                for tt in range(GROUP):
                    dve.wait_ge(*s.gp.h_stored(GROUP * g + tt + 1))
                    if due(2 * (GROUP * g + tt)):
                        dve.wait_ge(*s.gp.dots_ready(2 * (GROUP * g + tt)))
                    nc.vector.tensor_tensor_reduce(out=s.junk[:, :], in0=s.h[:, tt, :], in1=s.asrc[:, :], scale=1.0,
                                                   scalar=0.0, op0=ALU.mult, op1=ALU.add,
                                                   accum_out=s.s4[:, tt:tt + 1]).then_inc(s.gp.dots_ready.sem, 1)
                    dve.wait_ge(*s.gp.dots_ready(2 * (GROUP * g + tt) + 1))
                    nc.vector.tensor_tensor_reduce(out=s.junk[:, :], in0=s.h[:, tt, :], in1=s.adst[:, :], scale=1.0,
                                                   scalar=0.0, op0=ALU.mult, op1=ALU.add,
                                                   accum_out=s.d4[:, tt:tt + 1]).then_inc(s.gp.dots_ready.sem, 1)
                if due(g):
                    dve.wait_ge(*s.gp.s_bcast_ready(g))
                dve.wait_ge(*s.gp.dots_ready(2 * GROUP * (g + 1)))
                for tt in range(GROUP):
                    last = nc.vector.tensor_scalar(s.diag[:, tt * P:(tt + 1) * P], ident[:, :], s.s4[:, tt:tt + 1],
                                                   None, ALU.mult)
                last.then_inc(s.gp.diag_ready.sem, 1)
                nc.vector.tensor_copy(s.d_col[:, bass.ds(g * GROUP, GROUP)], s.d4[:, :]).then_inc(s.gp.d_ready.sem, 1)
                for tt in range(GROUP):
                    dve.wait_ge(*s.gp.hv_hi_ready(GROUP * g + tt + 1))
                    nc.vector.tensor_tensor(s.hv[:, GROUP * g + tt, D:2 * D], s.h[:, tt, :],
                                            s.hv[:, GROUP * g + tt, 0:D].bitcast(F32), ALU.subtract)\
                        .then_inc(s.gp.hv_lo_ready.sem, 1)

            steps(dve, group, 0, 2, GROUPS, GROUPS)

        def gm_over(eng, s, a):
            eng.wait_ge(*s.gm.pv_done(TILES * CHUNKS))
            eng.wait_ge(*s.gm.hi_ready(TILES * CHUNKS))
            eng.wait_ge(*s.gm.lo_ready(TILES * (CHUNKS - len(LOW_BY_PE[a]))))
            eng.wait_ge(*s.gm.lo_act_ready(TILES * len(LOW_BY_PE[a])))
            eng.wait_ge(*s.gm.o_lo_ready(TILES))
            eng.wait_ge(*s.gm.y_ready(TILES))
            eng.wait_ge(*s.gm.y_stored0(8 * TILES))
            eng.wait_ge(*s.gm.y_stored1(8 * TILES))
            if a == 0:
                eng.wait_ge(*s.gm.mask_stored0(8 * TILES))
                eng.wait_ge(*s.gm.mask_stored1(8 * TILES))

        def low_count(a, t, c, by_pe):
            kind = [x for x in range(CHUNKS) if (x in LOW_BY_PE[a]) == by_pe]
            return len(kind) * t + len([x for x in kind if x <= c])

        def gm_sync(sp, s, a):
            src, _, bias, _, _, dst = gat_args[a]
            sp.dma_start(s.bias[:, :], on_all_partitions(bias)).then_inc(s.gm.bias_in.sem, 16)

            def tile(t, p):
                if exists(t + 1) and a == 0:
                    for q in range(QUARTERS):
                        if due(QUARTERS * t + q + 1):
                            sp.wait_ge(*s.gm.nb_ready(QUARTERS * t + q + 1))
                        sp.dma_start(s.adj[:, q * QUARTER:(q + 1) * QUARTER], adj_quarters[t + 1, q]).then_inc(
                            [s.gm.adj_in0, s.gm.adj_in1, s.gm.adj_in2, s.gm.adj_in3][q].sem, 16)
                if exists(t + 1) and a == 1:
                    if due(QUARTERS * t):
                        sp.wait_ge(*s.gm.t_ready(QUARTERS * t))
                        apart(sp)
                    sp.dma_start([s.mask1, s.mask0][p][:, :], mask_dram[t + 1]).then_inc(
                        [s.gm.mask_in1, s.gm.mask_in0][p].sem, 16)
                if exists(t) and a == 1:
                    if due(t - 1):
                        sp.wait_ge(*s.gm.y_ready(t - 1))
                    sp.dma_start([s.xres0, s.xres1][p][:, :], node_tiles(x)[t]).then_inc(
                        [s.gm.x_res_in0, s.gm.x_res_in1][p].sem, 16)
                if exists(t) and a == 0:
                    sp.wait_ge(*s.gm.mask_ready(t + 1))
                    apart(sp)
                    sp.dma_start(mask_dram[t], [s.mask0, s.mask1][p][:, :]).then_inc(
                        [s.gm.mask_stored0, s.gm.mask_stored1][p].sem, 16)
                if exists(t - 3):
                    sp.wait_ge(*s.gm.y_ready(t - 2))
                    sp.dma_start(node_tiles(dst)[t - 3], [s.y1, s.y0][p][:, :]).then_inc(
                        [s.gm.y_stored1, s.gm.y_stored0][p].sem, 16)

            steps(sp, tile, -1, 4, TILES - 2, TILES + 3)

        def gm_tensor(pe, s, a):
            def transposes(t, p, c):
                if c % CPQ == 0:
                    pe.wait_ge(*s.gm.p_ready(QUARTERS * t + c // CPQ + 1))
                by_pe = (c - 4) % CHUNKS in LOW_BY_PE[a]
                left = low_count(a, *((t, c - 4) if c >= 4 else (t - 1, c + 4)), by_pe)
                if due(left):
                    pe.wait_ge(*(s.gm.lo_act_ready if by_pe else s.gm.lo_ready)(left))
                for b in range(BLOCKS):
                    j = c * BLOCKS + b
                    last = nc.tensor.matmul(bank[c % 4][:, b * P:(b + 1) * P],
                                            [s.t0, s.t1][p][:, j * P:(j + 1) * P], ident[:, :], is_transpose=True,
                                            start=b == 0, stop=b == BLOCKS - 1)
                last.then_inc(s.gm.transposed.sem, 1)

            def subtract_high(t, c):
                pe.wait_ge(*s.gm.hi_ready(CHUNKS * t + c + 1))
                nc.tensor.matmul(bank[c % 4][:, :], neg_ident[:, :], s.pt_hi[c % 4][:, :], start=False, stop=True,
                                 skip_group_check=True).then_inc(s.gm.subtracted.sem, 1)

            def values(t, p, c):
                if c == 0:
                    if due(t - 1):
                        pe.wait_ge(*s.gm.o_taken(t - 1))
                by_pe = c in LOW_BY_PE[a]
                pe.wait_ge(*s.gm.hi_ready(CHUNKS * t + c + 1))
                pe.wait_ge(*(s.gm.lo_act_ready if by_pe else s.gm.lo_ready)(low_count(a, t, c, by_pe)))
                for b in range(BLOCKS):
                    j = c * BLOCKS + b
                    w = slice(b * P, (b + 1) * P)
                    nc.tensor.matmul(bank[4 + p][:, :], s.pt_hi[c % 4][:, w], s.hv[:, j, :], start=j == 0, stop=False)
                    last = nc.tensor.matmul(bank[4 + p][:, 0:D], s.pt_lo[c % 4][:, w], s.hv[:, j, 0:D], start=False,
                                            stop=j == TILES - 1)
                last.then_inc(s.gm.pv_done.sem, 1)

            def tile(t, p):
                for c in range(CHUNKS):
                    if exists(behind(t, p, c, GAT_LAG)[0]):
                        transposes(*behind(t, p, c, GAT_LAG))
                    before = behind(t, p, c, GAT_LAG + 1)
                    if exists(before[0]) and before[2] in LOW_BY_PE[a]:
                        subtract_high(before[0], before[2])
                    if exists(behind(t, p, c, GAT_LAG + 2)[0]):
                        values(*behind(t, p, c, GAT_LAG + 2))

            pe.wait_ge(neg_ident_ready, 1)
            steps(pe, tile, 1, 4, TILES, TILES + 2)

        def gm_scalar(act, s, a):
            def high(t, c):
                g = CHUNKS * t + c
                act.wait_ge(*s.gm.transposed(g + 1))
                if due(g - 3):
                    act.wait_ge(*s.gm.pv_done(g - 3))
                nc.scalar.activation(s.pt_hi[c % 4][:, :], bank[c % 4][:, :], ACT.Copy).then_inc(s.gm.hi_ready.sem, 1)

            def low(t, c):
                g = CHUNKS * t + c
                act.wait_ge(*s.gm.subtracted(low_count(a, t, c, True)))
                if due(g - 3):
                    act.wait_ge(*s.gm.pv_done(g - 3))
                nc.scalar.activation(s.pt_lo[c % 4][:, :], bank[c % 4][:, :], ACT.Copy)\
                    .then_inc(s.gm.lo_act_ready.sem, 1)

            def sloped(t, p, q):
                col = slice(q * QUARTER, (q + 1) * QUARTER)
                act.wait_ge(*s.gm.k_ready(2 * (t + 1)))
                nc.scalar.activation(s.v[:, col], [s.t0, s.t1][p][:, col], ACT.Identity, bias=s.k_neg[:, p:p + 1],
                                     scale=SLOPE).then_inc(s.gm.v_ready.sem, 1)

            def exponentials(t, p, q):
                buf = [s.t0, s.t1][p][:, q * QUARTER:(q + 1) * QUARTER]
                act.wait_ge(*s.gm.leaky_ready(QUARTERS * t + q + 1))
                nc.scalar.activation(buf, buf, ACT.Exp, bias=0.0, scale=1.0,
                                     accum_out=s.sum4[:, p, q:q + 1]).then_inc(s.gm.p_ready.sem, 1)

            def output_low(t, p):
                act.wait_ge(*s.gm.pv_done(CHUNKS * (t + 1)))
                if due(t):
                    act.wait_ge(*s.gm.o_taken(t))
                nc.scalar.activation(s.o_lo[:, :], bank[4 + p][:, D:2 * D], ACT.Copy).then_inc(s.gm.o_lo_ready.sem, 1)

            def tile(t, p):
                for c in range(CHUNKS):
                    if c == 7 and exists(t - 2):
                        output_low(t - 2, p)
                    before = behind(t, p, c, GAT_LAG)
                    if exists(before[0]):
                        high(before[0], before[2])
                    if exists(t - 1):
                        if c % 2 == 0:
                            sloped(t - 1, 1 - p, c // 2)
                    before = behind(t, p, c, 1 + EXP_LAG)
                    if exists(before[0]) and c % 2 == 1:
                        exponentials(before[0], before[1], before[2] // 2)
                    before = behind(t, p, c, GAT_LAG + 1)
                    if exists(before[0]) and before[2] in LOW_BY_PE[a]:
                        low(before[0], before[2])

            steps(act, tile, 1, 4, TILES, TILES + 2)

        def gm_vector(dve, s, a):
            def make_mask(t, p, q):
                col = slice(q * QUARTER, (q + 1) * QUARTER)
                dve.wait_ge(*[s.gm.adj_in0, s.gm.adj_in1, s.gm.adj_in2, s.gm.adj_in3][q](16 * (t + 1)))
                if q == 0 and due(8 * (t - p)):
                    dve.wait_ge(*[s.gm.mask_stored0, s.gm.mask_stored1][p](8 * (t - p)))
                nc.vector.tensor_scalar([s.mask0, s.mask1][p][:, col], s.adj[:, col], 0.0, MASKED, ALU.is_equal,
                                        ALU.mult).then_inc(s.gm.nb_ready.sem, 1)

            def join_self(t, p):
                dve.wait_ge(*s.gm.nb_ready(QUARTERS * (t + 1)))
                diagonal = [s.mask0, s.mask1][p][:, bass.ds(t * P, P)]
                nc.vector.tensor_tensor(diagonal, diagonal, off_diag[:, :], ALU.mult).then_inc(s.gm.mask_ready.sem, 1)
                dve.wait_ge(*s.gm.mask_ready(t + 1))
                apart(dve)

            def masked_scores(t, p, q):
                col = slice(q * QUARTER, (q + 1) * QUARTER)
                if due(CHUNKS * (t - 2) + CPQ * (q + 1)):
                    dve.wait_ge(*s.gm.transposed(CHUNKS * (t - 2) + CPQ * (q + 1)))
                    apart(dve)
                nc.vector.tensor_tensor_reduce(out=[s.t0, s.t1][p][:, col], in0=s.s_row[:, col],
                                               in1=[s.mask0, s.mask1][p][:, col], scale=1.0, scalar=-3e38,
                                               op0=ALU.add, op1=ALU.max, accum_out=s.max4[:, q:q + 1])\
                    .then_inc(s.gm.t_ready.sem, 1)

            def row_constants(t, p):
                d = s.d_col[:, bass.ds(t, 1)]
                dve.wait_ge(*s.gm.t_ready(QUARTERS * (t + 1)))
                nc.vector.reduce_max(s.smax[:, :], s.max4[:, :], AX.X).then_inc(s.gm.smax_ready.sem, 1)
                dve.wait_ge(*s.gm.smax_ready(t + 1))
                apart(dve)
                nc.vector.tensor_scalar(s.zmax[:, :], s.smax[:, :], d, None, ALU.add).then_inc(s.gm.zmax_ready.sem, 1)
                dve.wait_ge(*s.gm.zmax_ready(t + 1))
                nc.vector.scalar_tensor_tensor(s.m[:, :], s.zmax[:, :], SLOPE, s.zmax[:, :], ALU.mult, ALU.max)\
                    .then_inc(s.gm.m_ready.sem, 1)
                dve.wait_ge(*s.gm.m_ready(t + 1))
                apart(dve)
                nc.vector.scalar_tensor_tensor(s.k_neg[:, p:p + 1], d, SLOPE, s.m[:, :], ALU.mult, ALU.subtract)\
                    .then_inc(s.gm.k_ready.sem, 1)
                nc.vector.tensor_scalar(s.k_pos[:, p:p + 1], d, s.m[:, :], None, ALU.subtract).then_inc(s.gm.k_ready.sem, 1)

            def exponents(t, p, q):
                col = slice(q * QUARTER, (q + 1) * QUARTER)
                buf = [s.t0, s.t1][p][:, col]
                dve.wait_ge(*s.gm.v_ready(QUARTERS * t + q + 1))
                nc.vector.scalar_tensor_tensor(buf, buf, s.k_pos[:, p:p + 1], s.v[:, col], ALU.add, ALU.max)\
                    .then_inc(s.gm.leaky_ready.sem, 1)

            def low(t, c):
                g = CHUNKS * t + c
                dve.wait_ge(*s.gm.transposed(g + 1))
                dve.wait_ge(*s.gm.hi_ready(g + 1))
                if due(g - 3):
                    dve.wait_ge(*s.gm.pv_done(g - 3))
                nc.vector.tensor_tensor(s.pt_lo[c % 4][:, :], bank[c % 4][:, :], s.pt_hi[c % 4][:, :].bitcast(F32),
                                        ALU.subtract).then_inc(s.gm.lo_ready.sem, 1)

            def row_sum(t, p):
                dve.wait_ge(*s.gm.p_ready(QUARTERS * (t + 1)))
                nc.vector.reduce_sum(s.total[:, :], s.sum4[:, p, :], AX.X).then_inc(s.gm.sum_ready.sem, 1)
                dve.wait_ge(*s.gm.sum_ready(t + 1))
                nc.vector.reciprocal(s.rinv[:, p:p + 1], s.total[:, :]).then_inc(s.gm.rinv_ready.sem, 1)

            def finish(t, p):
                dve.wait_ge(*s.gm.o_lo_ready(t + 1))
                nc.vector.tensor_tensor(s.o[:, :], bank[4 + p][:, 0:D], s.o_lo[:, :], ALU.add)\
                    .then_inc(s.gm.o_taken.sem, 1)
                dve.wait_ge(*s.gm.o_taken(t + 1))
                dve.wait_ge(*s.gm.rinv_ready(t + 1))
                nc.vector.scalar_tensor_tensor(s.o[:, :], s.o[:, :], s.rinv[:, p:p + 1], s.bias[:, :], ALU.mult,
                                               ALU.add).then_inc(s.gm.biased.sem, 1)
                dve.wait_ge(*s.gm.biased(t + 1))
                if a == 0:
                    if due(8 * (t - p)):
                        dve.wait_ge(*[s.gm.y_stored0, s.gm.y_stored1][p](8 * (t - p)))
                    nc.vector.tensor_scalar([s.y0, s.y1][p][:, :], s.o[:, :], 0.0, None, ALU.max)\
                        .then_inc(s.gm.y_ready.sem, 1)
                else:
                    dve.wait_ge(*[s.gm.x_res_in0, s.gm.x_res_in1][p](8 * (t - p) + 16))
                    nc.vector.scalar_tensor_tensor(s.o[:, :], s.o[:, :], 0.0, [s.xres0, s.xres1][p][:, :],
                                                   ALU.max, ALU.add).then_inc(s.gm.residual_added.sem, 1)
                    dve.wait_ge(*s.gm.residual_added(t + 1))
                    statistics(dve, s, s.gm, t)

            def tile(t, p):
                for c in range(CHUNKS):
                    before = behind(t, p, c, GAT_LAG + 1)
                    if exists(before[0]) and before[2] not in LOW_BY_PE[a]:
                        low(before[0], before[2])
                    if exists(t - 1) and c % 2 == 1:
                        exponents(t - 1, 1 - p, c // 2)
                    if exists(t) and a == 1 and c == 0:
                        dve.wait_ge(*[s.gm.mask_in0, s.gm.mask_in1][p](8 * (t - p) + 16))
                        apart(dve)
                    if exists(t) and c % 2 == 0:
                        masked_scores(t, p, c // 2)
                    if exists(t) and c == CHUNKS - 2:
                        row_constants(t, p)
                    if exists(t + 1) and a == 0 and c % 2 == 1:
                        make_mask(t + 1, 1 - p, c // 2)
                    if exists(t + 1) and a == 0 and c == CHUNKS - 1:
                        join_self(t + 1, 1 - p)
                    if c == 3 and exists(t - 2):
                        row_sum(t - 2, p)
                    if c == 7 and exists(t - 2):
                        finish(t - 2, p)
                    if c == 1 and a == 1 and exists(t - 3):
                        normalize(dve, s, s.gm, [s.y1, s.y0][p], t - 3, 1 - p)

            dve.wait_ge(*s.gm.bias_in(16))
            steps(dve, tile, -1, 4, TILES - 2, TILES + 3)

        def gm_pool(pool, s):
            inverse_roots(pool, s, s.gm)

        def inverse_roots(pool, s, k):
            def tile(t, p):
                pool.wait_ge(*k.ve_ready(t + 1))
                nc.gpsimd.tensor_tensor(s.rstd[:, :], s.ve[:, :], power[:, :], ALU.pow).then_inc(k.rstd_ready.sem, 1)
            steps(pool, tile, 0, 2, TILES, TILES)

        def statistics(dve, s, k, t):
            nc.vector.bn_stats(s.stats[:, :], s.o[:, :]).then_inc(k.stats_ready.sem, 1)
            dve.wait_ge(*k.stats_ready(t + 1))
            apart(dve)
            nc.vector.bn_aggr(s.mv[:, :], s.stats[:, :]).then_inc(k.mean_ready.sem, 1)
            dve.wait_ge(*k.mean_ready(t + 1))
            nc.vector.tensor_scalar(s.ve[:, :], s.mv[:, 1:2], EPS, None, ALU.add).then_inc(k.ve_ready.sem, 1)

        def normalize(dve, s, k, y, t, p):
            dve.wait_ge(*k.rstd_ready(t + 1))
            if due(8 * (t - p)):
                dve.wait_ge(*[k.y_stored0, k.y_stored1][p](8 * (t - p)))
            nc.vector.tensor_scalar(y[:, :], s.o[:, :], s.mv[:, 0:1], s.rstd[:, :], ALU.subtract, ALU.mult)\
                .then_inc(k.y_ready.sem, 1)

        def ap_over(eng, s, a):
            eng.wait_ge(*s.ap.qk_hi_ready(4 * GROUPS))
            eng.wait_ge(*s.ap.qk_lo_ready(4 * GROUPS))
            eng.wait_ge(*s.ap.v_hi_ready(TILES))
            eng.wait_ge(*s.ap.v_lo_ready(TILES))
            eng.wait_ge(*s.ap.vr_ready(TILES))
            eng.wait_ge(*s.ap.q_stored(16 * TILES))
            if a == 0:
                eng.wait_ge(*s.ap.res_stored(16 * GROUPS))

        def ap_sync(sp, s, a):
            src, wq, bq, wk, bk, wv, bv, wr, br, _ = att_args[a]
            for i, w in enumerate([wq, wk, wv] + ([wr] if a == 0 else [])):
                sp.dma_start(s.wn[:, i, :, :], halves(w)).then_inc(s.ap.consts_in.sem, 16)
            for i, b in enumerate((bq, bk)):
                sp.dma_start(s.bqk[:, i, :], b.rearrange("(h p) -> p h", p=P),
                             allow_slow_non_contiguous=True).then_inc(s.ap.consts_in.sem, 16)
            for i, b in enumerate([bv] + ([br] if a == 0 else [])):
                sp.dma_start(s.bvr[:, i * D:(i + 1) * D], on_all_partitions(b)).then_inc(s.ap.consts_in.sem, 16)

            def load(g, p):
                if due(HALVES * (g - 1)):
                    sp.wait_ge(*s.ap.xt_ready(HALVES * (g - 1)))
                sp.dma_start([s.xin0, s.xin1][p][:, :, :], node_groups(src)[g]).then_inc([s.ap.x_in0, s.ap.x_in1][p].sem, 16)
                if exists(g - 1):
                    store(g - 1)

            def store(g):
                sp.wait_ge(*s.ap.qk_hi_ready(4 * g + 2))
                sp.wait_ge(*s.ap.qk_lo_ready(4 * g + 2))
                for tt in range(GROUP):
                    to = q_dram[a].rearrange("(g t) p (hl h n) -> g t p hl h n", t=GROUP, hl=2, h=HALVES)[g, tt]
                    last = sp.dma_start(to, s.q_hl[:, :, :, tt * P:(tt + 1) * P].bitcast(F32)).then_inc(s.ap.q_stored.sem, 16)
                if a == 0:
                    sp.wait_ge(*s.ap.vr_biased(GROUP * (g + 1)))
                    sp.dma_start(node_groups(res_dram)[g], s.vr[:, :, D:2 * D]).then_inc(s.ap.res_stored.sem, 16)

            steps(sp, load, 0, 2, GROUPS, GROUPS)
            store(GROUPS - 1)

        def ap_tensor(pe, s, a):
            nw = 4 if a == 0 else 3
            pe.wait_ge(*s.ap.consts_in(16 * (nw + 2 + nw - 2)))
            for w in range(nw):
                for ci in range(HALVES):
                    for co in range(HALVES):
                        last = nc.tensor.transpose(bank[(w // 2) * 4 + ci][:, ((w % 2) * HALVES + co) * P:
                                                                           ((w % 2) * HALVES + co + 1) * P],
                                                   s.wn[:, w, co, ci * P:(ci + 1) * P], ident[:, :])
            last.then_inc(s.ap.wt_ready.sem, 1)
            pe.wait_ge(*s.ap.wt_hi_ready(4))
            pe.wait_ge(*s.ap.wt_lo_ready(4))
            nvr = D * (nw - 2)

            def group(g, p):
                pe.wait_ge(*[s.ap.x_in0, s.ap.x_in1][p](8 * (g - p) + 16))
                if due(HALVES * g):
                    pe.wait_ge(*s.ap.xt_lo_ready(HALVES * g))
                for ch in range(HALVES):
                    for tt in range(GROUP):
                        last = nc.tensor.transpose(bank[ch][:, tt * P:(tt + 1) * P],
                                                   [s.xin0, s.xin1][p][:, tt, ch * P:(ch + 1) * P], ident[:, :])
                    last.then_inc(s.ap.xt_ready.sem, 1)
                pe.wait_ge(*s.ap.xt_hi_ready(HALVES * (g + 1)))
                pe.wait_ge(*s.ap.xt_lo_ready(HALVES * (g + 1)))
                for i in range(4):
                    if due(4 * (g - 1) + i + 1):
                        pe.wait_ge(*s.ap.qk_hi_ready(4 * (g - 1) + i + 1))
                    if due(4 * (g - 1) + i + 1):
                        pe.wait_ge(*s.ap.qk_lo_ready(4 * (g - 1) + i + 1))
                    w = slice(i * P, (i + 1) * P)
                    parts = [(w_, x_, ci) for ci in range(HALVES)
                             for w_, x_ in ((s.wqk_hi, s.xt_hi), (s.wqk_hi, s.xt_lo), (s.wqk_lo, s.xt_hi))]
                    for n, (w_, x_, ci) in enumerate(parts):
                        last = nc.tensor.matmul(bank[2 + i][:, :], w_[:, ci, w], x_[:, ci, :], start=n == 0,
                                                stop=n == len(parts) - 1)
                    last.then_inc(s.ap.qk_ready.sem, 1)
                for tt in range(GROUP):
                    if due(GROUP * g + tt - 1):
                        pe.wait_ge(*s.ap.vr_biased(GROUP * g + tt - 1))
                    c = slice(tt * P, (tt + 1) * P)
                    parts = [(x_, w_, ci) for ci in range(HALVES)
                             for x_, w_ in ((s.xt_hi, s.wvr_hi), (s.xt_hi, s.wvr_lo), (s.xt_lo, s.wvr_hi))]
                    for n, (x_, w_, ci) in enumerate(parts):
                        last = nc.tensor.matmul(bank[6 + tt % 2][:, 0:nvr], x_[:, ci, c], w_[:, ci, 0:nvr],
                                                start=n == 0, stop=n == len(parts) - 1)
                    last.then_inc(s.ap.vr_ready.sem, 1)

            steps(pe, group, 0, 2, GROUPS, GROUPS)

        def ap_scalar(act, s, a):
            act.wait_ge(*s.ap.wt_ready(1))
            nvr = D * (2 if a == 0 else 1)
            for ci in range(HALVES):
                nc.scalar.activation(s.wqk_hi[:, ci, :], bank[ci][:, :], ACT.Copy).then_inc(s.ap.wt_hi_ready.sem, 1)
                nc.scalar.activation(s.wvr_hi[:, ci, 0:nvr], bank[4 + ci][:, 0:nvr], ACT.Copy)\
                    .then_inc(s.ap.wt_hi_ready.sem, 1)
            act.wait_ge(*s.ap.consts_in(128 if a == 0 else 96))

            def group(g, p):
                if due(GROUP * g):
                    act.wait_ge(*s.ap.vr_ready(GROUP * g))
                for ch in range(HALVES):
                    act.wait_ge(*s.ap.xt_ready(HALVES * g + ch + 1))
                    nc.scalar.activation(s.xt_hi[:, ch, :], bank[ch][:, :], ACT.Copy).then_inc(s.ap.xt_hi_ready.sem, 1)
                if due(16 * GROUP * g):
                    act.wait_ge(*s.ap.q_stored(16 * GROUP * g))
                for i in range(4):
                    act.wait_ge(*s.ap.qk_ready(4 * g + i + 1))
                    to = s.q_hl[:, 0, i, :] if i < 2 else s.kt_hi[:, i - 2, bass.ds(g * CHUNK, CHUNK)]
                    apart(act)
                    nc.scalar.activation(to, bank[2 + i][:, :], ACT.Identity, bias=s.bqk[:, i // 2, i % 2:i % 2 + 1],
                                         scale=1.0).then_inc(s.ap.qk_hi_ready.sem, 1)
                for tt in range(GROUP):
                    act.wait_ge(*s.ap.vr_biased(GROUP * g + tt + 1))
                    apart(act)
                    nc.scalar.activation(s.v[:, GROUP * g + tt, 0:D], s.vr[:, tt, 0:D], ACT.Copy)\
                        .then_inc(s.ap.v_hi_ready.sem, 1)

            steps(act, group, 0, 2, GROUPS, GROUPS)

        def ap_vector(dve, s, a):
            nvr = D * (2 if a == 0 else 1)
            dve.wait_ge(*s.ap.wt_ready(1))
            dve.wait_ge(*s.ap.wt_hi_ready(4))
            for ci in range(HALVES):
                nc.vector.tensor_tensor(s.wqk_lo[:, ci, :], bank[ci][:, :], s.wqk_hi[:, ci, :].bitcast(F32),
                                        ALU.subtract).then_inc(s.ap.wt_lo_ready.sem, 1)
                nc.vector.tensor_tensor(s.wvr_lo[:, ci, 0:nvr], bank[4 + ci][:, 0:nvr],
                                        s.wvr_hi[:, ci, 0:nvr].bitcast(F32), ALU.subtract)\
                    .then_inc(s.ap.wt_lo_ready.sem, 1)
            dve.wait_ge(*s.ap.consts_in(128 if a == 0 else 96))

            def group(g, p):
                if due(GROUP * g):
                    dve.wait_ge(*s.ap.vr_ready(GROUP * g))
                for ch in range(HALVES):
                    dve.wait_ge(*s.ap.xt_hi_ready(HALVES * g + ch + 1))
                    nc.vector.tensor_tensor(s.xt_lo[:, ch, :], bank[ch][:, :], s.xt_hi[:, ch, :].bitcast(F32),
                                            ALU.subtract).then_inc(s.ap.xt_lo_ready.sem, 1)
                if due(16 * GROUP * g):
                    dve.wait_ge(*s.ap.q_stored(16 * GROUP * g))
                for i in range(4):
                    dve.wait_ge(*s.ap.qk_hi_ready(4 * g + i + 1))
                    cols = bass.ds(g * CHUNK, CHUNK)
                    hi = s.q_hl[:, 0, i, :] if i < 2 else s.kt_hi[:, i - 2, cols]
                    lo = s.q_hl[:, 1, i, :] if i < 2 else s.kt_lo[:, i - 2, cols]
                    nc.vector.scalar_tensor_tensor(lo, bank[2 + i][:, :], s.bqk[:, i // 2, i % 2:i % 2 + 1],
                                                   hi.bitcast(F32), ALU.add, ALU.subtract).then_inc(s.ap.qk_lo_ready.sem, 1)
                if due(GROUP * g):
                    dve.wait_ge(*s.ap.v_hi_ready(GROUP * g))
                if a == 0:
                    if due(16 * g):
                        dve.wait_ge(*s.ap.res_stored(16 * g))
                for tt in range(GROUP):
                    dve.wait_ge(*s.ap.vr_ready(GROUP * g + tt + 1))
                    nc.vector.tensor_tensor(s.vr[:, tt, 0:nvr], bank[6 + tt % 2][:, 0:nvr], s.bvr[:, 0:nvr], ALU.add)\
                        .then_inc(s.ap.vr_biased.sem, 1)
                for tt in range(GROUP):
                    dve.wait_ge(*s.ap.v_hi_ready(GROUP * g + tt + 1))
                    nc.vector.tensor_tensor(s.v[:, GROUP * g + tt, D:2 * D], s.vr[:, tt, 0:D],
                                            s.v[:, GROUP * g + tt, 0:D].bitcast(F32), ALU.subtract)\
                        .then_inc(s.ap.v_lo_ready.sem, 1)

            steps(dve, group, 0, 2, GROUPS, GROUPS)

        def am_over(eng, s, a):
            eng.wait_ge(*s.am.pv_done(TILES * CHUNKS))
            eng.wait_ge(*s.am.hi_ready(TILES * CHUNKS))
            eng.wait_ge(*s.am.lo_ready(TILES * CHUNKS))
            eng.wait_ge(*s.am.o_lo_ready(TILES))
            eng.wait_ge(*s.am.y_ready(TILES))
            eng.wait_ge(*s.am.y_stored0(8 * TILES))
            eng.wait_ge(*s.am.y_stored1(8 * TILES))

        def am_sync(sp, s, a):
            dst = att_args[a][-1]
            res = res_dram if a == 0 else xa_dram

            def load_q(t, p):
                if due(CHUNKS * (t - 1)):
                    sp.wait_ge(*s.am.scores_ready(CHUNKS * (t - 1)))
                sp.dma_start([s.q0, s.q1][p][:, :, :, :].bitcast(F32),
                             q_dram[a].rearrange("t p (hl h n) -> t p hl h n", hl=2, h=HALVES)[t])\
                    .then_inc([s.am.q_in0, s.am.q_in1][p].sem, 16)

            def load_adj(t, q):
                if due(QUARTERS * (t - 1) + q + 1):
                    sp.wait_ge(*s.am.att_ready(QUARTERS * (t - 1) + q + 1))
                sp.dma_start(s.adj[:, q * QUARTER:(q + 1) * QUARTER], adj_quarters[t, q]).then_inc(
                    [s.am.adj_in0, s.am.adj_in1, s.am.adj_in2, s.am.adj_in3][q].sem, 16)

            def load_res(t, p):
                if due(t - 1):
                    sp.wait_ge(*s.am.y_ready(t - 1))
                sp.dma_start([s.res0, s.res1][p][:, :], node_tiles(res)[t]).then_inc([s.am.res_in0, s.am.res_in1][p].sem, 16)
                if a == 1:
                    sp.dma_start([s.xln0, s.xln1][p][:, :], node_tiles(x1_dram)[t]).then_inc(
                        [s.am.res_in0, s.am.res_in1][p].sem, 16)

            def store(t, p):
                sp.wait_ge(*s.am.y_ready(t + 1))
                sp.dma_start(node_tiles(dst)[t], [s.y0, s.y1][p][:, :]).then_inc([s.am.y_stored0, s.am.y_stored1][p].sem, 16)

            load_q(0, 0)

            def tile(t, p):
                if exists(t + 1):
                    load_q(t + 1, 1 - p)
                for q in range(QUARTERS):
                    if exists(t):
                        load_adj(t, q)
                    if q == 2 and exists(t - 2):
                        store(t - 2, p)
                        if exists(t):
                            load_res(t, p)
                    elif q == 2 and exists(t):
                        load_res(t, p)

            steps(sp, tile, 0, 4, TILES - 2, TILES + 2)

        def am_tensor(pe, s, a):

            def scores(t, p, c):
                k = CHUNKS * t + c
                if c == 0:
                    pe.wait_ge(*[s.am.q_in0, s.am.q_in1][p](8 * (t - p) + 16))
                if due(k - 3):
                    pe.wait_ge(*s.am.scores_taken(k - 3))
                q = [s.q0, s.q1][p]
                cols = slice(c * CHUNK, (c + 1) * CHUNK)
                parts = [(0, s.kt_hi, ch) for ch in range(HALVES)] + [(0, s.kt_lo, ch) for ch in range(HALVES)]\
                    + [(1, s.kt_hi, ch) for ch in range(HALVES)]
                for n, (hl, k_, ch) in enumerate(parts):
                    last = nc.tensor.matmul(bank[c % 4][:, :], q[:, hl, ch, :], k_[:, ch, cols], start=n == 0,
                                            stop=n == len(parts) - 1)
                last.then_inc(s.am.scores_ready.sem, 1)

            def transposes(t, p, c):
                g = CHUNKS * t + c
                if c % CPQ == 0:
                    pe.wait_ge(*s.am.att_ready(QUARTERS * t + c // CPQ + 1))
                if due(g - 1):
                    pe.wait_ge(*s.am.hi_ready(g - 1))
                if due(g - 1):
                    pe.wait_ge(*s.am.lo_ready(g - 1))
                for b in range(BLOCKS):
                    j = c * BLOCKS + b
                    last = nc.tensor.transpose(bank[4 + c % 2][:, b * P:(b + 1) * P],
                                               [s.s0, s.s1][p][:, j * P:(j + 1) * P], ident[:, :])
                last.then_inc(s.am.transposed.sem, 1)

            def values(t, p, c):
                g = CHUNKS * t + c
                if c == 0:
                    if due(t - 1):
                        pe.wait_ge(*s.am.o_taken(t - 1))
                pe.wait_ge(*s.am.hi_ready(g + 1))
                pe.wait_ge(*s.am.lo_ready(g + 1))
                hi, lo = [s.pt_hi0, s.pt_hi1][c % 2], [s.pt_lo0, s.pt_lo1][c % 2]
                for b in range(BLOCKS):
                    j = c * BLOCKS + b
                    w = slice(b * P, (b + 1) * P)
                    nc.tensor.matmul(bank[6 + p][:, :], hi[:, w], s.v[:, j, :], start=j == 0, stop=False)
                    last = nc.tensor.matmul(bank[6 + p][:, 0:D], lo[:, w], s.v[:, j, 0:D], start=False,
                                            stop=j == TILES - 1)
                last.then_inc(s.am.pv_done.sem, 1)

            def tile(t, p):
                for c in range(CHUNKS):
                    if exists(t):
                        scores(t, p, c)
                    if exists(behind(t, p, c, LAG)[0]):
                        transposes(*behind(t, p, c, LAG))
                    if exists(behind(t, p, c, LAG + 1)[0]):
                        values(*behind(t, p, c, LAG + 1))

            steps(pe, tile, 0, 4, TILES, TILES + 2)

        def am_scalar(act, s, a):

            def exponentials(t, p, q):
                if q == 0:
                    act.wait_ge(*s.am.bias_ready(t + 1))
                col = slice(q * QUARTER, (q + 1) * QUARTER)
                buf = [s.s0, s.s1][p][:, col]
                nc.scalar.activation(buf, buf, ACT.Exp, bias=s.bias[:, p:p + 1], scale=SCALE,
                                     accum_out=s.sum4[:, p, q:q + 1]).then_inc(s.am.exp_done.sem, 1)

            def tile(t, p):
                for c in range(CHUNKS):
                    tt, tp, tc = behind(t, p, c, LAG)
                    if exists(tt):
                        g = CHUNKS * tt + tc
                        act.wait_ge(*s.am.transposed(g + 1))
                        if due(g - 1):
                            act.wait_ge(*s.am.pv_done(g - 1))
                        nc.scalar.activation([s.pt_hi0, s.pt_hi1][tc % 2][:, :], bank[4 + tc % 2][:, :], ACT.Copy)\
                            .then_inc(s.am.hi_ready.sem, 1)
                    if c < 2 and exists(t - 1):
                        exponentials(t - 1, 1 - p, 2 * c)
                        exponentials(t - 1, 1 - p, 2 * c + 1)
                    if c == LAG + 2 and exists(t - 2):
                        if due(CHUNKS * (t - 1)):
                            act.wait_ge(*s.am.pv_done(CHUNKS * (t - 1)))
                        if due(t - 2):
                            act.wait_ge(*s.am.o_taken(t - 2))
                        nc.scalar.activation(s.o_lo[:, :], bank[6 + p][:, D:2 * D], ACT.Copy).then_inc(s.am.o_lo_ready.sem, 1)

            steps(act, tile, 0, 4, TILES, TILES + 2)

        def am_vector(dve, s, a):

            def take_scores(t, p, c):
                dve.wait_ge(*s.am.scores_ready(CHUNKS * t + c + 1))
                nc.vector.tensor_scalar([s.s0, s.s1][p][:, c * CHUNK:(c + 1) * CHUNK], bank[c % 4][:, :], 1.0, None,
                                        ALU.mult, ALU.max, accum_out=s.max8[:, p, c:c + 1])\
                    .then_inc(s.am.scores_taken.sem, 1)

            def row_max(t, p):
                dve.wait_ge(*s.am.scores_taken(CHUNKS * (t + 1)))
                nc.vector.tensor_reduce(s.neg_max[:, :], s.max8[:, p, :], AX.X, ALU.max, negate=True)\
                    .then_inc(s.am.max_ready.sem, 1)
                dve.wait_ge(*s.am.max_ready(t + 1))
                nc.vector.tensor_scalar(s.bias[:, p:p + 1], s.neg_max[:, :], SCALE, None, ALU.mult)\
                    .then_inc(s.am.bias_ready.sem, 1)

            def row_sum(t, p):
                dve.wait_ge(*s.am.exp_done(QUARTERS * (t + 1)))
                nc.vector.reduce_sum(s.total[:, :], s.sum4[:, p, :], AX.X).then_inc(s.am.sum_ready.sem, 1)
                dve.wait_ge(*s.am.sum_ready(t + 1))
                nc.vector.reciprocal(s.rinv[:, :], s.total[:, :]).then_inc(s.am.rinv_ready.sem, 1)
                dve.wait_ge(*s.am.rinv_ready(t + 1))

            def attention_rows(t, p, q):
                col = slice(q * QUARTER, (q + 1) * QUARTER)
                dve.wait_ge(*[s.am.adj_in0, s.am.adj_in1, s.am.adj_in2, s.am.adj_in3][q](16 * (t + 1)))
                buf = [s.s0, s.s1][p][:, col]
                nc.vector.scalar_tensor_tensor(buf, buf, s.rinv[:, :], s.adj[:, col], ALU.mult, ALU.add)\
                    .then_inc(s.am.att_ready.sem, 1)

            def finish(t, p):
                dve.wait_ge(*s.am.o_lo_ready(t + 1))
                nc.vector.tensor_tensor(s.o[:, :], bank[6 + p][:, 0:D], s.o_lo[:, :], ALU.add).then_inc(s.am.o_taken.sem, 1)
                dve.wait_ge(*s.am.o_taken(t + 1))
                dve.wait_ge(*[s.am.res_in0, s.am.res_in1][p]((8 * (t - p) + 16) * (1 + a)))
                if due(8 * (t - p)):
                    dve.wait_ge(*[s.am.y_stored0, s.am.y_stored1][p](8 * (t - p)))
                y, res = [s.y0, s.y1][p], [s.res0, s.res1][p]
                if a == 0:
                    nc.vector.scalar_tensor_tensor(y[:, :], s.o[:, :], 0.0, res[:, :], ALU.max, ALU.add)\
                        .then_inc(s.am.y_ready.sem, 1)
                    return
                nc.vector.scalar_tensor_tensor(s.o[:, :], s.o[:, :], 0.0, res[:, :], ALU.max, ALU.add)\
                    .then_inc(s.am.residual_added.sem, 1)
                dve.wait_ge(*s.am.residual_added(t + 1))
                nc.vector.tensor_tensor(s.o[:, :], s.o[:, :], [s.xln0, s.xln1][p][:, :], ALU.add)\
                    .then_inc(s.am.x1_added.sem, 1)
                dve.wait_ge(*s.am.x1_added(t + 1))
                statistics(dve, s, s.am, t)

            def tile(t, p):
                for c in range(CHUNKS):
                    if exists(t):
                        take_scores(t, p, c)
                    tt, tp, tc = behind(t, p, c, LAG)
                    if exists(tt):
                        g = CHUNKS * tt + tc
                        dve.wait_ge(*s.am.transposed(g + 1))
                        dve.wait_ge(*s.am.hi_ready(g + 1))
                        if due(g - 1):
                            dve.wait_ge(*s.am.pv_done(g - 1))
                        nc.vector.tensor_tensor([s.pt_lo0, s.pt_lo1][tc % 2][:, :], bank[4 + tc % 2][:, :],
                                                [s.pt_hi0, s.pt_hi1][tc % 2][:, :].bitcast(F32), ALU.subtract)\
                            .then_inc(s.am.lo_ready.sem, 1)
                    if exists(t - 1):
                        if c == LAG - 1:
                            row_sum(t - 1, 1 - p)
                        if c in (LAG - 1, LAG, LAG + 2, LAG + 4):
                            attention_rows(t - 1, 1 - p, (LAG - 1, LAG, LAG + 2, LAG + 4).index(c))
                    if c == LAG + 2 and exists(t - 2):
                        finish(t - 2, p)
                    if c == LAG + 3 and a == 1 and exists(t - 2):
                        normalize(dve, s, s.am, [s.y0, s.y1][p], t - 2, p)
                    if c == CHUNKS - 1 and exists(t):
                        row_max(t, p)

            steps(dve, tile, 0, 4, TILES, TILES + 2)

        def am_pool(pool, s):
            inverse_roots(pool, s, s.am)

        block = top.enter_context(nc.Block())

        @block.sync
        def _(sp):
            for a, s in enumerate(gat):
                gp_sync(sp, s, a)
                gp_over(sp, s, a)
                gm_sync(sp, s, a)
                gm_over(sp, s, a)
            for a, s in enumerate(att):
                ap_sync(sp, s, a)
                ap_over(sp, s, a)
                am_sync(sp, s, a)
                am_over(sp, s, a)

        @block.gpsimd
        def _(pool):
            nc.gpsimd.memset(ident[:, :], 0.0).then_inc(ident_step, 1)
            nc.gpsimd.memset(off_diag[:, :], 1.0).then_inc(ident_step, 1)
            nc.gpsimd.memset(ones[:, :], 1.0).then_inc(consts_ready, 1)
            nc.gpsimd.memset(power[:, :], -0.5).then_inc(consts_ready, 1)
            pool.wait_ge(ident_step, 2)
            for m, fill in ((ident, 1.0), (off_diag, 0.0)):
                nc.gpsimd.affine_select(out=m[:, :], in_=m[:, :], compare_op=ALU.not_equal, fill=fill, base=0,
                                        pattern=[[-1, P]], channel_multiplier=1).then_inc(consts_ready, 1)
            pool.wait_ge(consts_ready, 4)
            gp_over(pool, gat[1], 1)
            gm_pool(pool, gat[1])
            ap_over(pool, att[1], 1)
            am_pool(pool, att[1])

        @block.tensor
        def _(pe):
            pe.wait_ge(consts_ready, 4)
            for a, s in enumerate(gat):
                gp_tensor(pe, s, a)
                gp_over(pe, s, a)
                gm_tensor(pe, s, a)
                gm_over(pe, s, a)
            for a, s in enumerate(att):
                ap_tensor(pe, s, a)
                ap_over(pe, s, a)
                am_tensor(pe, s, a)
                am_over(pe, s, a)

        @block.scalar
        def _(act):
            act.wait_ge(consts_ready, 4)
            nc.scalar.mul(neg_ident[:, :], ident[:, :], -1.0).then_inc(neg_ident_ready, 1)
            for a, s in enumerate(gat):
                gp_scalar(act, s, a)
                gp_over(act, s, a)
                gm_scalar(act, s, a)
                gm_over(act, s, a)
            for a, s in enumerate(att):
                ap_scalar(act, s, a)
                ap_over(act, s, a)
                am_scalar(act, s, a)
                am_over(act, s, a)

        @block.vector
        def _(dve):
            dve.wait_ge(consts_ready, 4)
            for a, s in enumerate(gat):
                gp_vector(dve, s, a)
                gp_over(dve, s, a)
                gm_vector(dve, s, a)
                gm_over(dve, s, a)
            for a, s in enumerate(att):
                ap_vector(dve, s, a)
                ap_over(dve, s, a)
                am_vector(dve, s, a)
                am_over(dve, s, a)


_INS = ['x', 'adj', 'L0_gnn_W1', 'L0_gnn_b1', 'L0_gnn_asrc1', 'L0_gnn_adst1', 'L0_gnn_W2', 'L0_gnn_b2',
        'L0_gnn_asrc2', 'L0_gnn_adst2', 'L1_gnn_wq0', 'L1_gnn_bq0', 'L1_gnn_wk0', 'L1_gnn_bk0', 'L1_gnn_wv0',
        'L1_gnn_bv0', 'L1_gnn_wres', 'L1_gnn_bres', 'L1_gnn_wq1', 'L1_gnn_bq1', 'L1_gnn_wk1', 'L1_gnn_bk1',
        'L1_gnn_wv1', 'L1_gnn_bv1']


def kernel(**inputs):
    import concourse.bacc as bacc
    from concourse.bass_utils import run_bass_kernel_spmd

    nc = bacc.Bacc("TRN2", target_bir_lowering=False, num_devices=1)
    arrays, args = {}, []
    for name in _INS:
        a = np.ascontiguousarray(inputs[name])
        arrays[f"in_{name}"] = a
        args.append(nc.dram_tensor(f"in_{name}", a.shape, mybir.dt.from_np(a.dtype), kind="ExternalInput").ap())
    out = nc.dram_tensor("out", (N, D), F32, kind="ExternalOutput").ap()
    build(nc, *args, out)
    r = run_bass_kernel_spmd(nc, [arrays], core_ids=[0])
    return r.results[0]["out"]
```

```python
import numpy as np
import concourse.bass as bass
from concourse import mybir
from contextlib import ExitStack

F32 = mybir.dt.float32
F32R = mybir.dt.float32r
BF16 = mybir.dt.bfloat16
ACT = mybir.ActivationFunctionType
ALU = mybir.AluOpType
AX = mybir.AxisListType

P = 128
N = 4096
D = 256
TILES = N // P
HALVES = D // P
CHUNK = 512
CHUNKS = N // CHUNK
BLOCKS = CHUNK // P
QUARTER = 1024
QUARTERS = N // QUARTER
CPQ = CHUNKS // QUARTERS
GROUP = 4
GROUPS = TILES // GROUP
SCALE = 1.0 / 16.0
SLOPE = 0.2
EPS = 1e-5
MASKED = -1e38
EXP_LAG = 2
GAT_LAG = 5
LOW_BY_PE = ((0, 1, 2, 3, 4, 5, 6), (1, 2, 4, 5, 6))
LAG = 3


class Signal:

    def __init__(self, sem, base):
        self.sem, self.base = sem, base

    def __call__(self, count):
        return self.sem, count + self.base


def due(count):
    return not isinstance(count, int) or count > 0


def steps(eng, body, first, steady, steady_end, last):
    for t in range(first, steady):
        body(t, t % 2)
    with eng.Fori(steady // 2, steady_end // 2) as u:
        body(2 * u, 0)
        body(2 * u + 1, 1)
    for t in range(steady_end, last):
        body(t, t % 2)


def exists(t):
    return not isinstance(t, int) or 0 <= t < TILES


def group_exists(g):
    return not isinstance(g, int) or 0 <= g < GROUPS


def build(nc, x, adj, W1, b1, asrc1, adst1, W2, b2, asrc2, adst2,
          wq0, bq0, wk0, bk0, wv0, bv0, wres, bres, wq1, bq1, wk1, bk1, wv1, bv1, out):
    top = ExitStack()
    count = [0]

    def sem(name):
        count[0] += 1
        return top.enter_context(nc.semaphore(name))

    def scratch(name, shape, dt):
        return nc.dram_tensor(name, shape, dt, kind="Internal").ap()

    mask_dram = scratch("mask_scratch", (TILES, P, N), BF16)
    h1_dram = scratch("h1_scratch", (N, D), F32)
    x1_dram = scratch("x1_scratch", (N, D), F32)
    xa_dram = scratch("xa_scratch", (N, D), F32)
    res_dram = scratch("res_scratch", (N, D), F32)
    q_dram = [scratch(f"q_scratch{a}", (TILES, P, 2 * HALVES * P), F32) for a in range(2)]

    with top:
        ident = top.enter_context(nc.sbuf_tensor("ident", [P, P], F32))
        ones = top.enter_context(nc.sbuf_tensor("ones", [P, P], F32))
        power = top.enter_context(nc.sbuf_tensor("power", [P, 1], F32))
        bank = [top.enter_context(nc.psum_tensor(f"bank{i}", [P, CHUNK], F32)) for i in range(8)]
        off_diag = top.enter_context(nc.sbuf_tensor("off_diag", [P, P], F32))
        neg_ident = top.enter_context(nc.sbuf_tensor("neg_ident", [P, P], F32R))
        neg_ident_ready = sem("neg_ident_ready")
        ident_step = sem("ident_step")
        consts_ready = sem("consts_ready")
        waits_passed = sem("waits_passed")

        o_lo = top.enter_context(nc.sbuf_tensor("o_lo", [P, D], F32))
        o = top.enter_context(nc.sbuf_tensor("o", [P, D], F32))
        y0 = top.enter_context(nc.sbuf_tensor("y0", [P, D], F32))
        y1 = top.enter_context(nc.sbuf_tensor("y1", [P, D], F32))
        res0 = top.enter_context(nc.sbuf_tensor("res0", [P, D], F32))
        res1 = top.enter_context(nc.sbuf_tensor("res1", [P, D], F32))
        stats = top.enter_context(nc.sbuf_tensor("stats", [P, 6], F32))
        mv = top.enter_context(nc.sbuf_tensor("mv", [P, 2], F32))
        ve = top.enter_context(nc.sbuf_tensor("ve", [P, 1], F32))
        rstd = top.enter_context(nc.sbuf_tensor("rstd", [P, 1], F32))
        wn = top.enter_context(nc.sbuf_tensor("wn", [P, 4, HALVES, D], F32))

        class Space:
            pass

        def sb(mem, name, shape, dt):
            return mem.enter_context(nc.sbuf_tensor(name, shape, dt))

        handles = {}

        def signal(name, a, total):
            if name not in handles:
                handles[name] = sem(name)
            return Signal(handles[name], a * total)

        def finishing(s):
            s.o_lo, s.o, s.y0, s.y1, s.res0, s.res1, s.stats, s.mv, s.ve, s.rstd = (
                o_lo, o, y0, y1, res0, res1, stats, mv, ve, rstd)

        def gat_layer(a):
            s = Space()
            finishing(s)
            s.w, s.asrc, s.adst = w_in[a], asrc_in[a], adst_in[a]
            with ExitStack() as kept:
                s.hv = sb(kept, f"g{a}_hv", [P, TILES, 2 * D], F32R)
                s.s_row = sb(kept, f"g{a}_s_row", [P, N], F32)
                s.d_col = sb(kept, f"g{a}_d_col", [P, TILES], F32)
                s.adj = sb(kept, f"g{a}_adj", [P, N], F32)
                s.mask0 = sb(kept, f"g{a}_mask0", [P, N], BF16)
                s.mask1 = sb(kept, f"g{a}_mask1", [P, N], BF16)
                s.t0 = sb(kept, f"g{a}_t0", [P, N], F32)
                s.max4 = sb(kept, f"g{a}_max4", [P, QUARTERS], F32)
                with ExitStack() as projection:
                    s.w_hi = sb(projection, f"gp{a}_w_hi", [P, HALVES, D + 2], F32R)
                    s.w_lo = sb(projection, f"gp{a}_w_lo", [P, HALVES, D + 2], F32R)
                    s.ws = sb(projection, f"gp{a}_ws", [P, HALVES, P], F32)
                    s.ws_hi = sb(projection, f"gp{a}_ws_hi", [P, HALVES, P], F32R)
                    s.ws_lo = sb(projection, f"gp{a}_ws_lo", [P, HALVES, P], F32R)
                    s.products = sb(projection, f"gp{a}_products", [P, HALVES, 2, D], F32)
                    s.xin0 = sb(projection, f"gp{a}_xin0", [P, GROUP, D], F32)
                    s.xin1 = sb(projection, f"gp{a}_xin1", [P, GROUP, D], F32)
                    s.xt_hi = sb(projection, f"gp{a}_xt_hi", [P, 2, HALVES, CHUNK], F32R)
                    s.xt_lo = sb(projection, f"gp{a}_xt_lo", [P, 2, HALVES, CHUNK], F32R)
                with ExitStack() as main:
                    s.bias = sb(main, f"gm{a}_bias", [P, D], F32)
                    s.t1 = sb(main, f"gm{a}_t1", [P, N], F32)
                    s.pt_hi = [sb(main, f"gm{a}_pt_hi{i}", [P, CHUNK], F32R) for i in range(4)]
                    s.pt_lo = [sb(main, f"gm{a}_pt_lo{i}", [P, CHUNK], F32R) for i in range(4)]
                    s.smax = sb(main, f"gm{a}_smax", [P, 1], F32)
                    s.zmax = sb(main, f"gm{a}_zmax", [P, 1], F32)
                    s.m = sb(main, f"gm{a}_m", [P, 1], F32)
                    s.k_pos = sb(main, f"gm{a}_k_pos", [P, 2], F32)
                    s.k_neg = sb(main, f"gm{a}_k_neg", [P, 2], F32)
                    s.v = sb(main, f"gm{a}_v", [P, N], F32)
                    s.sum4 = sb(main, f"gm{a}_sum4", [P, 2, QUARTERS], F32)
                    s.total = sb(main, f"gm{a}_total", [P, 1], F32)
                    s.rinv = sb(main, f"gm{a}_rinv", [P, 2], F32)
            s.gp = k = Space()
            k.consts_in = signal("gp_consts_in", a, 3 * 16)
            k.x_in0 = signal("gp_x_in0", a, 8 * GROUPS)
            k.x_in1 = signal("gp_x_in1", a, 8 * GROUPS)
            k.ws_columns_ready = signal("gp_ws_columns_ready", a, 2 * HALVES)
            k.ws_ready = signal("gp_ws_ready", a, HALVES)
            k.w_hi_ready = signal("gp_w_hi_ready", a, 2)
            k.w_lo_ready = signal("gp_w_lo_ready", a, 2)
            k.xt_ready = signal("gp_xt_ready", a, HALVES * GROUPS)
            k.xt_hi_ready = signal("gp_xt_hi_ready", a, HALVES * GROUPS)
            k.xt_lo_ready = signal("gp_xt_lo_ready", a, HALVES * GROUPS)
            k.h_ready = signal("gp_h_ready", a, TILES)
            k.hv_hi_ready = signal("gp_hv_hi_ready", a, TILES)
            k.hv_lo_ready = signal("gp_hv_lo_ready", a, TILES)
            k.d_ready = signal("gp_d_ready", a, TILES)
            k.s_bcast_ready = signal("gp_s_bcast_ready", a, GROUPS)
            k.s_row_ready = signal("gp_s_row_ready", a, GROUPS)
            s.gm = k = Space()
            k.bias_in = signal("gm_bias_in", a, 16)
            k.adj_in0 = signal("gm_adj_in0", a, 16 * TILES)
            k.adj_in1 = signal("gm_adj_in1", a, 16 * TILES)
            k.adj_in2 = signal("gm_adj_in2", a, 16 * TILES)
            k.adj_in3 = signal("gm_adj_in3", a, 16 * TILES)
            k.x_res_in0 = signal("gm_x_res_in0", a, 0)
            k.x_res_in1 = signal("gm_x_res_in1", a, 0)
            k.mask_in0 = signal("gm_mask_in0", a, 0)
            k.mask_in1 = signal("gm_mask_in1", a, 0)
            k.nb_ready = signal("gm_nb_ready", a, QUARTERS * TILES)
            k.mask_ready = signal("gm_mask_ready", a, TILES)
            k.mask_stored0 = signal("gm_mask_stored0", a, 8 * TILES)
            k.mask_stored1 = signal("gm_mask_stored1", a, 8 * TILES)
            k.subtracted = signal("gm_subtracted", a, len(LOW_BY_PE[0]) * TILES)
            k.lo_act_ready = signal("gm_lo_act_ready", a, len(LOW_BY_PE[0]) * TILES)
            k.t_ready = signal("gm_t_ready", a, QUARTERS * TILES)
            k.smax_ready = signal("gm_smax_ready", a, TILES)
            k.zmax_ready = signal("gm_zmax_ready", a, TILES)
            k.m_ready = signal("gm_m_ready", a, TILES)
            k.k_ready = signal("gm_k_ready", a, 2 * TILES)
            k.v_ready = signal("gm_v_ready", a, QUARTERS * TILES)
            k.leaky_ready = signal("gm_leaky_ready", a, QUARTERS * TILES)
            k.p_ready = signal("gm_p_ready", a, QUARTERS * TILES)
            k.transposed = signal("gm_transposed", a, CHUNKS * TILES)
            k.hi_ready = signal("gm_hi_ready", a, CHUNKS * TILES)
            k.lo_ready = signal("gm_lo_ready", a, (CHUNKS - len(LOW_BY_PE[0])) * TILES)
            k.pv_done = signal("gm_pv_done", a, CHUNKS * TILES)
            k.o_lo_ready = signal("gm_o_lo_ready", a, TILES)
            k.o_taken = signal("gm_o_taken", a, TILES)
            k.sum_ready = signal("gm_sum_ready", a, TILES)
            k.rinv_ready = signal("gm_rinv_ready", a, TILES)
            k.biased = signal("gm_biased", a, TILES)
            k.summed = signal("gm_summed", a, 0)
            k.stats_ready = signal("gm_stats_ready", a, 0)
            k.mean_ready = signal("gm_mean_ready", a, 0)
            k.ve_ready = signal("gm_ve_ready", a, 0)
            k.rstd_ready = signal("gm_rstd_ready", a, 0)
            k.y_ready = signal("gm_y_ready", a, TILES)
            k.y_stored0 = signal("gm_y_stored0", a, 8 * TILES)
            k.y_stored1 = signal("gm_y_stored1", a, 8 * TILES)
            return s

        def att_layer(a):
            s = Space()
            finishing(s)
            s.xln0, s.xln1 = xln0, xln1
            s.wn = wn
            with ExitStack() as kept:
                s.kt_hi = sb(kept, f"a{a}_kt_hi", [P, HALVES, N], F32R)
                s.kt_lo = sb(kept, f"a{a}_kt_lo", [P, HALVES, N], F32R)
                s.v = sb(kept, f"a{a}_v", [P, TILES, 2 * D], F32R)
                s.q0 = sb(kept, f"a{a}_q0", [P, 2, HALVES, P], F32R)
                with ExitStack() as projection:
                    s.wqk_hi = sb(projection, f"ap{a}_wqk_hi", [P, HALVES, 2 * D], F32R)
                    s.wqk_lo = sb(projection, f"ap{a}_wqk_lo", [P, HALVES, 2 * D], F32R)
                    s.wvr_hi = sb(projection, f"ap{a}_wvr_hi", [P, HALVES, 2 * D], F32R)
                    s.wvr_lo = sb(projection, f"ap{a}_wvr_lo", [P, HALVES, 2 * D], F32R)
                    s.bqk = sb(projection, f"ap{a}_bqk", [P, 2, HALVES], F32)
                    s.bvr = sb(projection, f"ap{a}_bvr", [P, 2 * D], F32)
                    s.xin0 = sb(projection, f"ap{a}_xin0", [P, GROUP, D], F32)
                    s.xin1 = sb(projection, f"ap{a}_xin1", [P, GROUP, D], F32)
                    s.xt_hi = sb(projection, f"ap{a}_xt_hi", [P, 2, HALVES, CHUNK], F32R)
                    s.xt_lo = sb(projection, f"ap{a}_xt_lo", [P, 2, HALVES, CHUNK], F32R)
                    s.q_hl = sb(projection, f"ap{a}_q_hl", [P, 2, HALVES, CHUNK], F32R)
                    s.vr = sb(projection, f"ap{a}_vr", [P, GROUP, 2 * D], F32)
                with ExitStack() as main:
                    s.adj = sb(main, f"am{a}_adj", [P, N], F32)
                    s.s0 = sb(main, f"am{a}_s0", [P, N], F32)
                    s.s1 = sb(main, f"am{a}_s1", [P, N], F32)
                    s.q1 = sb(main, f"am{a}_q1", [P, 2, HALVES, P], F32R)
                    s.pt_hi0 = sb(main, f"am{a}_pt_hi0", [P, CHUNK], F32R)
                    s.pt_hi1 = sb(main, f"am{a}_pt_hi1", [P, CHUNK], F32R)
                    s.pt_lo0 = sb(main, f"am{a}_pt_lo0", [P, CHUNK], F32R)
                    s.pt_lo1 = sb(main, f"am{a}_pt_lo1", [P, CHUNK], F32R)
                    s.max8 = sb(main, f"am{a}_max8", [P, 2, CHUNKS], F32)
                    s.neg_max = sb(main, f"am{a}_neg_max", [P, 1], F32)
                    s.bias = sb(main, f"am{a}_bias", [P, 2], F32)
                    s.sum4 = sb(main, f"am{a}_sum4", [P, 2, QUARTERS], F32)
                    s.total = sb(main, f"am{a}_total", [P, 1], F32)
                    s.rinv = sb(main, f"am{a}_rinv", [P, 1], F32)
            s.ap = k = Space()
            k.wn_in = signal("ap_wn_in", a, 4 * 16)
            k.consts_in = signal("ap_consts_in", a, 4 * 16)
            k.x_in0 = signal("ap_x_in0", a, 8 * GROUPS)
            k.x_in1 = signal("ap_x_in1", a, 8 * GROUPS)
            k.wt_ready = signal("ap_wt_ready", a, 1)
            k.wt_hi_ready = signal("ap_wt_hi_ready", a, 4)
            k.wt_lo_ready = signal("ap_wt_lo_ready", a, 4)
            k.xt_ready = signal("ap_xt_ready", a, HALVES * GROUPS)
            k.xt_hi_ready = signal("ap_xt_hi_ready", a, HALVES * GROUPS)
            k.xt_lo_ready = signal("ap_xt_lo_ready", a, HALVES * GROUPS)
            k.qk_ready = signal("ap_qk_ready", a, 4 * GROUPS)
            k.qk_hi_ready = signal("ap_qk_hi_ready", a, 4 * GROUPS)
            k.qk_lo_ready = signal("ap_qk_lo_ready", a, 4 * GROUPS)
            k.q_stored = signal("ap_q_stored", a, 16 * TILES)
            k.vr_ready = signal("ap_vr_ready", a, TILES)
            k.vr_biased = signal("ap_vr_biased", a, TILES)
            k.v_hi_ready = signal("ap_v_hi_ready", a, TILES)
            k.v_lo_ready = signal("ap_v_lo_ready", a, TILES)
            k.res_stored = signal("ap_res_stored", a, 16 * GROUPS)
            s.am = k = Space()
            k.q_in0 = signal("am_q_in0", a, 8 * TILES)
            k.q_in1 = signal("am_q_in1", a, 8 * TILES)
            k.adj_in0 = signal("am_adj_in0", a, 16 * TILES)
            k.adj_in1 = signal("am_adj_in1", a, 16 * TILES)
            k.adj_in2 = signal("am_adj_in2", a, 16 * TILES)
            k.adj_in3 = signal("am_adj_in3", a, 16 * TILES)
            k.res_in0 = signal("am_res_in0", a, 8 * TILES)
            k.res_in1 = signal("am_res_in1", a, 8 * TILES)
            k.scores_ready = signal("am_scores_ready", a, CHUNKS * TILES)
            k.scores_taken = signal("am_scores_taken", a, CHUNKS * TILES)
            k.max_ready = signal("am_max_ready", a, TILES)
            k.bias_ready = signal("am_bias_ready", a, TILES)
            k.exp_done = signal("am_exp_done", a, QUARTERS * TILES)
            k.att_ready = signal("am_att_ready", a, QUARTERS * TILES)
            k.transposed = signal("am_transposed", a, CHUNKS * TILES)
            k.hi_ready = signal("am_hi_ready", a, CHUNKS * TILES)
            k.lo_ready = signal("am_lo_ready", a, CHUNKS * TILES)
            k.pv_done = signal("am_pv_done", a, CHUNKS * TILES)
            k.o_lo_ready = signal("am_o_lo_ready", a, TILES)
            k.o_taken = signal("am_o_taken", a, TILES)
            k.sum_ready = signal("am_sum_ready", a, TILES)
            k.rinv_ready = signal("am_rinv_ready", a, TILES)
            k.residual_added = signal("am_residual_added", a, 0)
            k.summed = signal("am_summed", a, 0)
            k.stats_ready = signal("am_stats_ready", a, 0)
            k.mean_ready = signal("am_mean_ready", a, 0)
            k.ve_ready = signal("am_ve_ready", a, 0)
            k.rstd_ready = signal("am_rstd_ready", a, 0)
            k.y_ready = signal("am_y_ready", a, TILES)
            k.y_stored0 = signal("am_y_stored0", a, 8 * TILES)
            k.y_stored1 = signal("am_y_stored1", a, 8 * TILES)
            return s

        with ExitStack() as gat_inputs:
            w_in = [sb(gat_inputs, f"w_in{a}", [P, HALVES, D + 2], F32) for a in range(2)]
            asrc_in = [sb(gat_inputs, f"asrc_in{a}", [P, D], F32) for a in range(2)]
            adst_in = [sb(gat_inputs, f"adst_in{a}", [P, D], F32) for a in range(2)]
            gat = [gat_layer(a) for a in range(2)]
        with ExitStack() as att_inputs:
            xln0 = sb(att_inputs, "xln0", [P, D], F32)
            xln1 = sb(att_inputs, "xln1", [P, D], F32)
            att = [att_layer(a) for a in range(2)]

        gat_args = [(x, W1, b1, asrc1, adst1, h1_dram), (h1_dram, W2, b2, asrc2, adst2, x1_dram)]
        att_args = [(x1_dram, wq0, bq0, wk0, bk0, wv0, bv0, wres, bres, xa_dram),
                    (xa_dram, wq1, bq1, wk1, bk1, wv1, bv1, None, None, out)]
        adj_quarters = adj.rearrange("(t p) (q n) -> t q p n", p=P, n=QUARTER)

        def node_tiles(t):
            return t.rearrange("(t p) d -> t p d", p=P)

        def node_groups(t):
            return t.rearrange("(g t p) d -> g p t d", p=P, t=GROUP)

        def on_all_partitions(v):
            return v.rearrange("(a d) -> a d", a=1).broadcast_to([P, v.shape[0]])

        def halves(w):
            return w.rearrange("(h p) d -> p h d", p=P)

        def behind(t, p, c, lag):
            return (t - 1, 1 - p, c - lag) if c >= lag else (t - 2, p, c - lag + CHUNKS)

        def apart(eng):
            eng.sem_inc(waits_passed, 1)

        def gp_over(eng, s, a):
            eng.wait_ge(*s.gp.h_ready(TILES))
            eng.wait_ge(*s.gp.hv_hi_ready(TILES))
            eng.wait_ge(*s.gp.hv_lo_ready(TILES))
            eng.wait_ge(*s.gp.s_row_ready(GROUPS))
            eng.wait_ge(*s.gp.d_ready(TILES))
            eng.wait_ge(*s.gp.s_bcast_ready(GROUPS))

        def load_gat_inputs(sp, s, a):
            _, W, _, asrc, adst, _ = gat_args[a]
            sp.dma_start(s.w[:, :, 0:D], halves(W)).then_inc(s.gp.consts_in.sem, 16)
            sp.dma_start(s.adst[:, :], on_all_partitions(adst)).then_inc(s.gp.consts_in.sem, 16)
            sp.dma_start(s.asrc[:, :], on_all_partitions(asrc)).then_inc(s.gp.consts_in.sem, 16)

        def gp_sync(sp, s, a):
            src = gat_args[a][0]

            def load(g, p):
                if due(HALVES * (g - 1)):
                    sp.wait_ge(*s.gp.xt_ready(HALVES * (g - 1)))
                sp.dma_start([s.xin0, s.xin1][p][:, :, :], node_groups(src)[g]).then_inc([s.gp.x_in0, s.gp.x_in1][p].sem, 16)

            load(0, 0)
            load(1, 1)
            load_first_mask(sp, s, a)
            if a == 1:
                last_store(sp, gat[0], gat[0].gm, h1_dram)
            steps(sp, load, 2, 2, GROUPS, GROUPS)
            load_second_mask(sp, s, a)

        def gp_tensor(pe, s, a):
            def transposes(g, p):
                pe.wait_ge(*[s.gp.x_in0, s.gp.x_in1][p](8 * (g - p) + 16))
                if due(HALVES * g):
                    pe.wait_ge(*s.gp.xt_hi_ready(HALVES * g))
                    pe.wait_ge(*s.gp.xt_lo_ready(HALVES * g))
                for ch in range(HALVES):
                    for tt in range(GROUP):
                        last = nc.tensor.transpose(bank[ch][:, tt * P:(tt + 1) * P],
                                                   [s.xin0, s.xin1][p][:, tt, ch * P:(ch + 1) * P], ident[:, :])
                    last.then_inc(s.gp.xt_ready.sem, 1)

            def products(g, p):
                pe.wait_ge(*s.gp.xt_hi_ready(HALVES * (g + 1)))
                pe.wait_ge(*s.gp.xt_lo_ready(HALVES * (g + 1)))
                if due(g - 1):
                    pe.wait_ge(*s.gp.s_row_ready(g - 1))
                parts = [(w_, x_, ch) for ch in range(HALVES)
                         for w_, x_ in ((s.ws_hi, s.xt_hi), (s.ws_hi, s.xt_lo), (s.ws_lo, s.xt_hi))]
                for i, (w_, x_, ch) in enumerate(parts):
                    last = nc.tensor.matmul(bank[6 + p][:, :], w_[:, ch, :], x_[:, p, ch, :], start=i == 0,
                                            stop=i == len(parts) - 1)
                last.then_inc(s.gp.s_bcast_ready.sem, 1)
                for tt in range(GROUP):
                    if due(GROUP * (g - 1) + tt + 1):
                        pe.wait_ge(*s.gp.d_ready(GROUP * (g - 1) + tt + 1))
                        pe.wait_ge(*s.gp.hv_lo_ready(GROUP * (g - 1) + tt + 1))
                    c = slice(tt * P, (tt + 1) * P)
                    parts = [(x_, w_, ch) for ch in range(HALVES)
                             for x_, w_ in ((s.xt_hi, s.w_hi), (s.xt_hi, s.w_lo), (s.xt_lo, s.w_hi))]
                    for i, (x_, w_, ch) in enumerate(parts):
                        last = nc.tensor.matmul(bank[2 + tt][:, 0:D + 2], x_[:, p, ch, c], w_[:, ch, :], start=i == 0,
                                                stop=i == len(parts) - 1)
                    last.then_inc(s.gp.h_ready.sem, 1)

            def group(g, p):
                if group_exists(g + 1):
                    transposes(g + 1, 1 - p)
                if isinstance(g, int) and g == 0:
                    pe.wait_ge(*s.gp.w_hi_ready(2))
                    pe.wait_ge(*s.gp.w_lo_ready(2))
                if group_exists(g):
                    products(g, p)

            steps(pe, group, -1, 2, GROUPS - 2, GROUPS)

        def gp_scalar(act, s, a):
            act.wait_ge(*s.gp.ws_columns_ready(2 * HALVES))
            nc.scalar.activation(s.w_hi[:, :, :], s.w[:, :, :], ACT.Copy).then_inc(s.gp.w_hi_ready.sem, 1)
            act.wait_ge(*s.gp.ws_ready(HALVES))
            nc.scalar.activation(s.ws_hi[:, :, :], s.ws[:, :, :], ACT.Copy).then_inc(s.gp.w_hi_ready.sem, 1)

            def features_high(g, p):
                if due(GROUP * (g - 1)):
                    act.wait_ge(*s.gp.h_ready(GROUP * (g - 1)))
                for ch in range(HALVES):
                    act.wait_ge(*s.gp.xt_ready(HALVES * g + ch + 1))
                    nc.scalar.activation(s.xt_hi[:, p, ch, :], bank[ch][:, :], ACT.Copy).then_inc(s.gp.xt_hi_ready.sem, 1)

            def group(g, p):
                if group_exists(g + 1):
                    features_high(g + 1, 1 - p)
                if group_exists(g):
                    act.wait_ge(*s.gp.s_bcast_ready(g + 1))
                    apart(act)
                    nc.scalar.activation(s.s_row[:, bass.ds(g * CHUNK, CHUNK)], bank[6 + p][:, :], ACT.Copy)\
                        .then_inc(s.gp.s_row_ready.sem, 1)
                    for tt in range(GROUP):
                        act.wait_ge(*s.gp.h_ready(GROUP * g + tt + 1))
                        apart(act)
                        nc.scalar.activation(s.hv[:, GROUP * g + tt, 0:D], bank[2 + tt][:, 0:D], ACT.Copy)\
                            .then_inc(s.gp.hv_hi_ready.sem, 1)

            steps(act, group, -1, 2, GROUPS - 2, GROUPS)

        def gp_vector(dve, s, a):
            dve.wait_ge(*s.gp.consts_in(48))
            for i, att in enumerate((s.adst, s.asrc)):
                for ch in range(HALVES):
                    nc.vector.tensor_tensor_reduce(out=s.products[:, ch, i, :], in0=s.w[:, ch, 0:D], in1=att[:, :],
                                                   scale=1.0, scalar=0.0, op0=ALU.mult, op1=ALU.add,
                                                   accum_out=s.w[:, ch, D + i:D + i + 1])\
                        .then_inc(s.gp.ws_columns_ready.sem, 1)
            dve.wait_ge(*s.gp.ws_columns_ready(2 * HALVES))
            for ch in range(HALVES):
                nc.vector.tensor_scalar(s.ws[:, ch, :], ones[:, :], s.w[:, ch, D + 1:D + 2], None, ALU.mult)\
                    .then_inc(s.gp.ws_ready.sem, 1)
            dve.wait_ge(*s.gp.w_hi_ready(1))
            nc.vector.tensor_tensor(s.w_lo[:, :, :], s.w[:, :, :], s.w_hi[:, :, :].bitcast(F32), ALU.subtract)\
                .then_inc(s.gp.w_lo_ready.sem, 1)
            dve.wait_ge(*s.gp.ws_ready(HALVES))
            dve.wait_ge(*s.gp.w_hi_ready(2))
            nc.vector.tensor_tensor(s.ws_lo[:, :, :], s.ws[:, :, :], s.ws_hi[:, :, :].bitcast(F32), ALU.subtract)\
                .then_inc(s.gp.w_lo_ready.sem, 1)

            def features_low(g, p):
                if due(GROUP * (g - 1)):
                    dve.wait_ge(*s.gp.h_ready(GROUP * (g - 1)))
                for ch in range(HALVES):
                    dve.wait_ge(*s.gp.xt_hi_ready(HALVES * g + ch + 1))
                    nc.vector.tensor_tensor(s.xt_lo[:, p, ch, :], bank[ch][:, :],
                                            s.xt_hi[:, p, ch, :].bitcast(F32), ALU.subtract)\
                        .then_inc(s.gp.xt_lo_ready.sem, 1)

            def group(g, p):
                if group_exists(g + 1):
                    features_low(g + 1, 1 - p)
                if group_exists(g):
                    for tt in range(GROUP):
                        dve.wait_ge(*s.gp.hv_hi_ready(GROUP * g + tt + 1))
                        apart(dve)
                        nc.vector.tensor_copy(s.d_col[:, bass.ds(GROUP * g + tt, 1)], bank[2 + tt][:, D:D + 1])\
                            .then_inc(s.gp.d_ready.sem, 1)
                        nc.vector.tensor_tensor(s.hv[:, GROUP * g + tt, D:2 * D], bank[2 + tt][:, 0:D],
                                                s.hv[:, GROUP * g + tt, 0:D].bitcast(F32), ALU.subtract)\
                            .then_inc(s.gp.hv_lo_ready.sem, 1)
                if isinstance(g, int) and g == 1:
                    make_first_mask(dve, s, a)
                if isinstance(g, int) and g >= GROUPS - 2:
                    for q in ((0, 1), (2,))[g - (GROUPS - 2)]:
                        dve.wait_ge(*s.gp.s_row_ready(2 * (q + 1)))
                        masked_scores(dve, s, a, 0, 0, q)

            steps(dve, group, -1, 2, GROUPS - 2, GROUPS)

        def first_groups_stored(sp, k):
            sp.wait_ge(*k.y_stored0(8 * 2 * GROUP))
            sp.wait_ge(*k.y_stored1(8 * 2 * GROUP))

        def last_store(sp, s, k, dst):
            sp.wait_ge(*k.y_ready(TILES))
            sp.dma_start(node_tiles(dst)[TILES - 1], s.y1[:, :]).then_inc(k.y_stored1.sem, 16)
            sp.wait_ge(*k.y_stored0(8 * TILES))
            sp.wait_ge(*k.y_stored1(8 * TILES))

        def gm_over(eng, s, a):
            eng.wait_ge(*s.gm.pv_done(TILES * CHUNKS))
            eng.wait_ge(*s.gm.hi_ready(TILES * CHUNKS))
            eng.wait_ge(*s.gm.lo_ready(TILES * (CHUNKS - len(LOW_BY_PE[a]))))
            eng.wait_ge(*s.gm.lo_act_ready(TILES * len(LOW_BY_PE[a])))
            eng.wait_ge(*s.gm.o_lo_ready(TILES))
            eng.wait_ge(*s.gm.biased(TILES))
            if a == 0:
                eng.wait_ge(*s.gm.mask_stored0(8 * TILES))
                eng.wait_ge(*s.gm.mask_stored1(8 * TILES))

        def low_count(a, t, c, by_pe):
            kind = [x for x in range(CHUNKS) if (x in LOW_BY_PE[a]) == by_pe]
            return len(kind) * t + len([x for x in kind if x <= c])

        def load_first_mask(sp, s, a):
            if a == 0:
                load_adj(sp, s, 0)
            else:
                sp.dma_start(s.mask0[:, :], mask_dram[0]).then_inc(s.gm.mask_in0.sem, 16)

        def load_second_mask(sp, s, a):
            if a == 0:
                load_adj(sp, s, 1)
            else:
                sp.dma_start(s.mask1[:, :], mask_dram[1]).then_inc(s.gm.mask_in1.sem, 16)

        def load_adj(sp, s, t):
            for q in range(QUARTERS):
                if due(QUARTERS * (t - 1) + q + 1):
                    sp.wait_ge(*s.gm.nb_ready(QUARTERS * (t - 1) + q + 1))
                sp.dma_start(s.adj[:, q * QUARTER:(q + 1) * QUARTER], adj_quarters[t, q]).then_inc(
                    [s.gm.adj_in0, s.gm.adj_in1, s.gm.adj_in2, s.gm.adj_in3][q].sem, 16)

        def gm_sync(sp, s, a):
            src, _, bias, _, _, dst = gat_args[a]
            sp.dma_start(s.bias[:, :], on_all_partitions(bias)).then_inc(s.gm.bias_in.sem, 16)

            def tile(t, p):
                at_start = isinstance(t, int) and t == 0
                if exists(t + 1) and a == 0 and not at_start:
                    load_adj(sp, s, t + 1)
                if exists(t + 1) and a == 1 and not at_start:
                    if due(QUARTERS * t):
                        sp.wait_ge(*s.gm.t_ready(QUARTERS * t))
                        apart(sp)
                    sp.dma_start([s.mask1, s.mask0][p][:, :], mask_dram[t + 1]).then_inc(
                        [s.gm.mask_in1, s.gm.mask_in0][p].sem, 16)
                if exists(t - 1) and a == 1:
                    if due(t - 2):
                        sp.wait_ge(*s.gm.y_ready(t - 2))
                    sp.dma_start([s.res1, s.res0][p][:, :], node_tiles(x)[t - 1]).then_inc(
                        [s.gm.x_res_in1, s.gm.x_res_in0][p].sem, 16)
                if exists(t) and a == 0:
                    sp.wait_ge(*s.gm.mask_ready(t + 1))
                    apart(sp)
                    sp.dma_start(mask_dram[t], [s.mask0, s.mask1][p][:, :]).then_inc(
                        [s.gm.mask_stored0, s.gm.mask_stored1][p].sem, 16)
                if exists(t - 3):
                    sp.wait_ge(*s.gm.y_ready(t - 2))
                    sp.dma_start(node_tiles(dst)[t - 3], [s.y1, s.y0][p][:, :]).then_inc(
                        [s.gm.y_stored1, s.gm.y_stored0][p].sem, 16)

            steps(sp, tile, 0, 4, TILES - 2, TILES + 2)
            first_groups_stored(sp, s.gm)

        def gm_tensor(pe, s, a):
            def transposes(t, p, c):
                if c % CPQ == 0:
                    pe.wait_ge(*s.gm.p_ready(QUARTERS * t + c // CPQ + 1))
                by_pe = (c - 4) % CHUNKS in LOW_BY_PE[a]
                left = low_count(a, *((t, c - 4) if c >= 4 else (t - 1, c + 4)), by_pe)
                if due(left):
                    pe.wait_ge(*(s.gm.lo_act_ready if by_pe else s.gm.lo_ready)(left))
                for b in range(BLOCKS):
                    j = c * BLOCKS + b
                    last = nc.tensor.matmul(bank[c % 4][:, b * P:(b + 1) * P],
                                            [s.t0, s.t1][p][:, j * P:(j + 1) * P], ident[:, :], is_transpose=True,
                                            start=b == 0, stop=b == BLOCKS - 1)
                last.then_inc(s.gm.transposed.sem, 1)

            def subtract_high(t, c):
                pe.wait_ge(*s.gm.hi_ready(CHUNKS * t + c + 1))
                nc.tensor.matmul(bank[c % 4][:, :], neg_ident[:, :], s.pt_hi[c % 4][:, :], start=False, stop=True,
                                 skip_group_check=True).then_inc(s.gm.subtracted.sem, 1)

            def values(t, p, c):
                if c == 0:
                    if due(t - 1):
                        pe.wait_ge(*s.gm.o_taken(t - 1))
                by_pe = c in LOW_BY_PE[a]
                pe.wait_ge(*s.gm.hi_ready(CHUNKS * t + c + 1))
                pe.wait_ge(*(s.gm.lo_act_ready if by_pe else s.gm.lo_ready)(low_count(a, t, c, by_pe)))
                for b in range(BLOCKS):
                    j = c * BLOCKS + b
                    w = slice(b * P, (b + 1) * P)
                    nc.tensor.matmul(bank[4 + p][:, :], s.pt_hi[c % 4][:, w], s.hv[:, j, :], start=j == 0, stop=False)
                    last = nc.tensor.matmul(bank[4 + p][:, 0:D], s.pt_lo[c % 4][:, w], s.hv[:, j, 0:D], start=False,
                                            stop=j == TILES - 1)
                last.then_inc(s.gm.pv_done.sem, 1)

            def tile(t, p):
                for c in range(CHUNKS):
                    if exists(behind(t, p, c, GAT_LAG)[0]):
                        transposes(*behind(t, p, c, GAT_LAG))
                    before = behind(t, p, c, GAT_LAG + 1)
                    if exists(before[0]) and before[2] in LOW_BY_PE[a]:
                        subtract_high(before[0], before[2])
                    if exists(behind(t, p, c, GAT_LAG + 3)[0]):
                        values(*behind(t, p, c, GAT_LAG + 3))

            pe.wait_ge(neg_ident_ready, 1)
            steps(pe, tile, 1, 4, TILES, TILES + 2)

        def gm_scalar(act, s, a):
            def high(t, c):
                g = CHUNKS * t + c
                act.wait_ge(*s.gm.transposed(g + 1))
                if due(g - 3):
                    act.wait_ge(*s.gm.pv_done(g - 3))
                nc.scalar.activation(s.pt_hi[c % 4][:, :], bank[c % 4][:, :], ACT.Copy).then_inc(s.gm.hi_ready.sem, 1)

            def low(t, c):
                g = CHUNKS * t + c
                act.wait_ge(*s.gm.subtracted(low_count(a, t, c, True)))
                if due(g - 3):
                    act.wait_ge(*s.gm.pv_done(g - 3))
                nc.scalar.activation(s.pt_lo[c % 4][:, :], bank[c % 4][:, :], ACT.Copy)\
                    .then_inc(s.gm.lo_act_ready.sem, 1)

            def sloped(t, p, q):
                col = slice(q * QUARTER, (q + 1) * QUARTER)
                act.wait_ge(*s.gm.k_ready(2 * (t + 1)))
                nc.scalar.activation(s.v[:, col], [s.t0, s.t1][p][:, col], ACT.Identity, bias=s.k_neg[:, p:p + 1],
                                     scale=SLOPE).then_inc(s.gm.v_ready.sem, 1)

            def exponentials(t, p, q):
                buf = [s.t0, s.t1][p][:, q * QUARTER:(q + 1) * QUARTER]
                act.wait_ge(*s.gm.leaky_ready(QUARTERS * t + q + 1))
                nc.scalar.activation(buf, buf, ACT.Exp, bias=0.0, scale=1.0,
                                     accum_out=s.sum4[:, p, q:q + 1]).then_inc(s.gm.p_ready.sem, 1)

            def output_low(t, p):
                act.wait_ge(*s.gm.pv_done(CHUNKS * (t + 1)))
                if due(t):
                    act.wait_ge(*s.gm.o_taken(t))
                nc.scalar.activation(s.o_lo[:, :], bank[4 + p][:, D:2 * D], ACT.Copy).then_inc(s.gm.o_lo_ready.sem, 1)

            def tile(t, p):
                for c in range(CHUNKS):
                    if c == 0 and exists(t - 3):
                        output_low(t - 3, 1 - p)
                    before = behind(t, p, c, GAT_LAG)
                    if exists(before[0]):
                        high(before[0], before[2])
                    if exists(t - 1):
                        if c % 2 == 0:
                            sloped(t - 1, 1 - p, c // 2)
                    before = behind(t, p, c, 1 + EXP_LAG)
                    if exists(before[0]) and c % 2 == 1:
                        exponentials(before[0], before[1], before[2] // 2)
                    before = behind(t, p, c, GAT_LAG + 1)
                    if exists(before[0]) and before[2] in LOW_BY_PE[a]:
                        low(before[0], before[2])

            steps(act, tile, 1, 4, TILES, TILES + 3)

        def make_mask(dve, s, t, p, q):
            col = slice(q * QUARTER, (q + 1) * QUARTER)
            dve.wait_ge(*[s.gm.adj_in0, s.gm.adj_in1, s.gm.adj_in2, s.gm.adj_in3][q](16 * (t + 1)))
            if q == 0 and due(8 * (t - p)):
                dve.wait_ge(*[s.gm.mask_stored0, s.gm.mask_stored1][p](8 * (t - p)))
            nc.vector.tensor_scalar([s.mask0, s.mask1][p][:, col], s.adj[:, col], 0.0, MASKED, ALU.is_equal,
                                    ALU.mult).then_inc(s.gm.nb_ready.sem, 1)

        def join_self(dve, s, t, p):
            dve.wait_ge(*s.gm.nb_ready(QUARTERS * (t + 1)))
            diagonal = [s.mask0, s.mask1][p][:, bass.ds(t * P, P)]
            nc.vector.tensor_tensor(diagonal, diagonal, off_diag[:, :], ALU.mult).then_inc(s.gm.mask_ready.sem, 1)

        def masked_scores(dve, s, a, t, p, q):
            col = slice(q * QUARTER, (q + 1) * QUARTER)
            if q == 0 and a == 0:
                dve.wait_ge(*s.gm.mask_ready(t + 1))
                apart(dve)
            if q == 0 and a == 1:
                dve.wait_ge(*[s.gm.mask_in0, s.gm.mask_in1][p](8 * (t - p) + 16))
                apart(dve)
            if due(CHUNKS * (t - 2) + CPQ * (q + 1)):
                dve.wait_ge(*s.gm.transposed(CHUNKS * (t - 2) + CPQ * (q + 1)))
                apart(dve)
            nc.vector.tensor_tensor_reduce(out=[s.t0, s.t1][p][:, col], in0=s.s_row[:, col],
                                           in1=[s.mask0, s.mask1][p][:, col], scale=1.0, scalar=-3e38,
                                           op0=ALU.add, op1=ALU.max, accum_out=s.max4[:, q:q + 1])\
                .then_inc(s.gm.t_ready.sem, 1)

        def make_first_mask(dve, s, a):
            if a == 0:
                for q in range(QUARTERS):
                    make_mask(dve, s, 0, 0, q)
                join_self(dve, s, 0, 0)

        def gm_vector(dve, s, a):
            def row_maximum(t):
                dve.wait_ge(*s.gm.t_ready(QUARTERS * (t + 1)))
                nc.vector.reduce_max(s.smax[:, :], s.max4[:, :], AX.X).then_inc(s.gm.smax_ready.sem, 1)

            def d_added(t):
                dve.wait_ge(*s.gm.smax_ready(t + 1))
                apart(dve)
                nc.vector.tensor_scalar(s.zmax[:, :], s.smax[:, :], s.d_col[:, bass.ds(t, 1)], None, ALU.add)\
                    .then_inc(s.gm.zmax_ready.sem, 1)

            def row_leaky(t):
                dve.wait_ge(*s.gm.zmax_ready(t + 1))
                nc.vector.scalar_tensor_tensor(s.m[:, :], s.zmax[:, :], SLOPE, s.zmax[:, :], ALU.mult, ALU.max)\
                    .then_inc(s.gm.m_ready.sem, 1)

            def row_constants(t, p):
                d = s.d_col[:, bass.ds(t, 1)]
                dve.wait_ge(*s.gm.m_ready(t + 1))
                apart(dve)
                nc.vector.scalar_tensor_tensor(s.k_neg[:, p:p + 1], d, SLOPE, s.m[:, :], ALU.mult, ALU.subtract)\
                    .then_inc(s.gm.k_ready.sem, 1)
                nc.vector.tensor_scalar(s.k_pos[:, p:p + 1], d, s.m[:, :], None, ALU.subtract).then_inc(s.gm.k_ready.sem, 1)

            def exponents(t, p, q):
                col = slice(q * QUARTER, (q + 1) * QUARTER)
                buf = [s.t0, s.t1][p][:, col]
                dve.wait_ge(*s.gm.v_ready(QUARTERS * t + q + 1))
                nc.vector.scalar_tensor_tensor(buf, buf, s.k_pos[:, p:p + 1], s.v[:, col], ALU.add, ALU.max)\
                    .then_inc(s.gm.leaky_ready.sem, 1)

            def low(t, c):
                g = CHUNKS * t + c
                dve.wait_ge(*s.gm.transposed(g + 1))
                dve.wait_ge(*s.gm.hi_ready(g + 1))
                if due(g - 3):
                    dve.wait_ge(*s.gm.pv_done(g - 3))
                nc.vector.tensor_tensor(s.pt_lo[c % 4][:, :], bank[c % 4][:, :], s.pt_hi[c % 4][:, :].bitcast(F32),
                                        ALU.subtract).then_inc(s.gm.lo_ready.sem, 1)

            def row_sum(t, p):
                dve.wait_ge(*s.gm.p_ready(QUARTERS * (t + 1)))
                nc.vector.reduce_sum(s.total[:, :], s.sum4[:, p, :], AX.X).then_inc(s.gm.sum_ready.sem, 1)
                dve.wait_ge(*s.gm.sum_ready(t + 1))
                nc.vector.reciprocal(s.rinv[:, p:p + 1], s.total[:, :]).then_inc(s.gm.rinv_ready.sem, 1)

            def take_output(t, p):
                if due(t):
                    dve.wait_ge(*s.gm.y_ready(t))
                dve.wait_ge(*s.gm.o_lo_ready(t + 1))
                nc.vector.tensor_tensor(s.o[:, :], bank[4 + p][:, 0:D], s.o_lo[:, :], ALU.add)\
                    .then_inc(s.gm.o_taken.sem, 1)

            def divide(t, p):
                dve.wait_ge(*s.gm.o_taken(t + 1))
                dve.wait_ge(*s.gm.rinv_ready(t + 1))
                if isinstance(t, int) and t == 0:
                    dve.wait_ge(*s.gm.bias_in(16))
                nc.vector.scalar_tensor_tensor(s.o[:, :], s.o[:, :], s.rinv[:, p:p + 1], s.bias[:, :], ALU.mult,
                                               ALU.add).then_inc(s.gm.biased.sem, 1)

            def rectify(t, p):
                dve.wait_ge(*s.gm.biased(t + 1))
                if a == 0:
                    if due(8 * (t - p)):
                        dve.wait_ge(*[s.gm.y_stored0, s.gm.y_stored1][p](8 * (t - p)))
                    nc.vector.tensor_scalar([s.y0, s.y1][p][:, :], s.o[:, :], 0.0, None, ALU.max)\
                        .then_inc(s.gm.y_ready.sem, 1)
                else:
                    dve.wait_ge(*[s.gm.x_res_in0, s.gm.x_res_in1][p](8 * (t - p) + 16))
                    nc.vector.scalar_tensor_tensor(s.o[:, :], s.o[:, :], 0.0, [s.res0, s.res1][p][:, :],
                                                   ALU.max, ALU.add).then_inc(s.gm.summed.sem, 1)

            def tile(t, p):
                ended, ended_p = t - 3, 1 - p
                for c in range(CHUNKS):
                    before = behind(t, p, c, GAT_LAG + 1)
                    if exists(before[0]) and before[2] not in LOW_BY_PE[a]:
                        low(before[0], before[2])
                    if c == 1 and exists(ended):
                        take_output(ended, ended_p)
                    if exists(t) and c == CHUNKS - 1:
                        d_added(t)
                    if exists(t - 1) and c % 2 == 1:
                        exponents(t - 1, 1 - p, c // 2)
                    if c == 1 and exists(ended):
                        divide(ended, ended_p)
                    if exists(t) and c == CHUNKS - 1:
                        row_leaky(t)
                    if exists(t) and c % 2 == 0 and not (isinstance(t, int) and t == 0 and c < 6):
                        masked_scores(dve, s, a, t, p, c // 2)
                    if c == 2 and exists(ended):
                        rectify(ended, ended_p)
                    if exists(t) and c == CHUNKS - 2:
                        row_maximum(t)
                    if exists(t + 1) and a == 0 and c % 2 == 1:
                        make_mask(dve, s, t + 1, 1 - p, c // 2)
                    if exists(t) and c == CHUNKS - 1:
                        row_constants(t, p)
                    if exists(t + 1) and a == 0 and c == CHUNKS - 1:
                        join_self(dve, s, t + 1, 1 - p)
                    if c == 3 and exists(t - 2):
                        row_sum(t - 2, p)
                    if a == 1 and exists(ended):
                        if c == 3:
                            feature_sums(dve, s, s.gm, ended)
                        if c == 4:
                            mean_variance(dve, s, s.gm, ended)
                        if c == 5:
                            variance_eps(dve, s, s.gm, ended)
                        if c == 6:
                            normalize(dve, s, s.gm, [s.y1, s.y0][p], ended, ended_p)

            steps(dve, tile, 0, 4, TILES - 2, TILES + 3)

        def gm_pool(pool, s):
            inverse_roots(pool, s, s.gm)

        def inverse_roots(pool, s, k):
            def tile(t, p):
                pool.wait_ge(*k.ve_ready(t + 1))
                nc.gpsimd.tensor_tensor(s.rstd[:, :], s.ve[:, :], power[:, :], ALU.pow).then_inc(k.rstd_ready.sem, 1)
            steps(pool, tile, 0, 2, TILES, TILES)

        def feature_sums(dve, s, k, t):
            dve.wait_ge(*k.summed(t + 1))
            nc.vector.bn_stats(s.stats[:, :], s.o[:, :]).then_inc(k.stats_ready.sem, 1)

        def mean_variance(dve, s, k, t):
            dve.wait_ge(*k.stats_ready(t + 1))
            apart(dve)
            nc.vector.bn_aggr(s.mv[:, :], s.stats[:, :]).then_inc(k.mean_ready.sem, 1)

        def variance_eps(dve, s, k, t):
            dve.wait_ge(*k.mean_ready(t + 1))
            nc.vector.tensor_scalar(s.ve[:, :], s.mv[:, 1:2], EPS, None, ALU.add).then_inc(k.ve_ready.sem, 1)

        def normalize(dve, s, k, y, t, p):
            dve.wait_ge(*k.rstd_ready(t + 1))
            if due(8 * (t - p)):
                dve.wait_ge(*[k.y_stored0, k.y_stored1][p](8 * (t - p)))
            nc.vector.tensor_scalar(y[:, :], s.o[:, :], s.mv[:, 0:1], s.rstd[:, :], ALU.subtract, ALU.mult)\
                .then_inc(k.y_ready.sem, 1)

        def ap_over(eng, s, a):
            eng.wait_ge(*s.ap.qk_hi_ready(4 * GROUPS))
            eng.wait_ge(*s.ap.qk_lo_ready(4 * GROUPS))
            eng.wait_ge(*s.ap.v_hi_ready(TILES))
            eng.wait_ge(*s.ap.v_lo_ready(TILES))
            eng.wait_ge(*s.ap.vr_ready(TILES))

        def ap_stored(eng, s, a):
            eng.wait_ge(*s.ap.q_stored(16 * TILES))
            if a == 0:
                eng.wait_ge(*s.ap.res_stored(16 * GROUPS))

        def load_att_weights(sp, s, a):
            _, wq, _, wk, _, wv, _, wr, _, _ = att_args[a]
            for i, w in enumerate([wq, wk, wv] + ([wr] if a == 0 else [])):
                sp.dma_start(s.wn[:, i, :, :], halves(w)).then_inc(s.ap.wn_in.sem, 16)

        def ap_sync(sp, s, a):
            src, _, bq, _, bk, _, bv, _, br, _ = att_args[a]
            for i, b in enumerate((bq, bk)):
                sp.dma_start(s.bqk[:, i, :], b.rearrange("(h p) -> p h", p=P),
                             allow_slow_non_contiguous=True).then_inc(s.ap.consts_in.sem, 16)
            for i, b in enumerate([bv] + ([br] if a == 0 else [])):
                sp.dma_start(s.bvr[:, i * D:(i + 1) * D], on_all_partitions(b)).then_inc(s.ap.consts_in.sem, 16)

            def load(g, p):
                if due(HALVES * (g - 1)):
                    sp.wait_ge(*s.ap.xt_ready(HALVES * (g - 1)))
                sp.dma_start([s.xin0, s.xin1][p][:, :, :], node_groups(src)[g]).then_inc([s.ap.x_in0, s.ap.x_in1][p].sem, 16)

            def store(g):
                sp.wait_ge(*s.ap.qk_hi_ready(4 * g + 2))
                sp.wait_ge(*s.ap.qk_lo_ready(4 * g + 2))
                for tt in range(GROUP):
                    to = q_dram[a].rearrange("(g t) p (hl h n) -> g t p hl h n", t=GROUP, hl=2, h=HALVES)[g, tt]
                    last = sp.dma_start(to, s.q_hl[:, :, :, tt * P:(tt + 1) * P].bitcast(F32)).then_inc(s.ap.q_stored.sem, 16)
                if a == 0:
                    sp.wait_ge(*s.ap.vr_biased(GROUP * (g + 1)))
                    sp.dma_start(node_groups(res_dram)[g], s.vr[:, :, D:2 * D]).then_inc(s.ap.res_stored.sem, 16)

            def group(g, p):
                if isinstance(g, int) and g == 0:
                    if a == 0:
                        last_store(sp, gat[1], gat[1].gm, x1_dram)
                    else:
                        last_store(sp, att[0], att[0].am, xa_dram)
                if group_exists(g + 2):
                    load(g + 2, p)
                if group_exists(g):
                    store(g)

            steps(sp, group, -2, 2, GROUPS - 2, GROUPS)
            sp.wait_ge(*s.ap.q_stored(16 * GROUP * (GROUPS - 1)))
            load_q(sp, s, a, 0, 0)

        def ap_tensor(pe, s, a):
            nw = 4 if a == 0 else 3
            pe.wait_ge(*s.ap.wn_in(16 * nw))
            for w in range(nw):
                for ci in range(HALVES):
                    for co in range(HALVES):
                        last = nc.tensor.transpose(bank[(w // 2) * 4 + ci][:, ((w % 2) * HALVES + co) * P:
                                                                           ((w % 2) * HALVES + co + 1) * P],
                                                   s.wn[:, w, co, ci * P:(ci + 1) * P], ident[:, :])
            last.then_inc(s.ap.wt_ready.sem, 1)
            pe.wait_ge(*s.ap.wt_hi_ready(4))
            pe.wait_ge(*s.ap.wt_lo_ready(4))
            nvr = D * (nw - 2)

            def transposes(g, p):
                pe.wait_ge(*[s.ap.x_in0, s.ap.x_in1][p](8 * (g - p) + 16))
                if due(HALVES * g):
                    pe.wait_ge(*s.ap.xt_lo_ready(HALVES * g))
                for ch in range(HALVES):
                    for tt in range(GROUP):
                        last = nc.tensor.transpose(bank[ch][:, tt * P:(tt + 1) * P],
                                                   [s.xin0, s.xin1][p][:, tt, ch * P:(ch + 1) * P], ident[:, :])
                    last.then_inc(s.ap.xt_ready.sem, 1)

            def products(g, p):
                pe.wait_ge(*s.ap.xt_hi_ready(HALVES * (g + 1)))
                pe.wait_ge(*s.ap.xt_lo_ready(HALVES * (g + 1)))
                for i in range(4):
                    if due(4 * (g - 1) + i + 1):
                        pe.wait_ge(*s.ap.qk_hi_ready(4 * (g - 1) + i + 1))
                    if due(4 * (g - 1) + i + 1):
                        pe.wait_ge(*s.ap.qk_lo_ready(4 * (g - 1) + i + 1))
                    w = slice(i * P, (i + 1) * P)
                    parts = [(w_, x_, ci) for ci in range(HALVES)
                             for w_, x_ in ((s.wqk_hi, s.xt_hi), (s.wqk_hi, s.xt_lo), (s.wqk_lo, s.xt_hi))]
                    for n, (w_, x_, ci) in enumerate(parts):
                        last = nc.tensor.matmul(bank[2 + i][:, :], w_[:, ci, w], x_[:, p, ci, :], start=n == 0,
                                                stop=n == len(parts) - 1)
                    last.then_inc(s.ap.qk_ready.sem, 1)
                for tt in range(GROUP):
                    if due(GROUP * g + tt - 1):
                        pe.wait_ge(*s.ap.vr_biased(GROUP * g + tt - 1))
                    c = slice(tt * P, (tt + 1) * P)
                    parts = [(x_, w_, ci) for ci in range(HALVES)
                             for x_, w_ in ((s.xt_hi, s.wvr_hi), (s.xt_hi, s.wvr_lo), (s.xt_lo, s.wvr_hi))]
                    for n, (x_, w_, ci) in enumerate(parts):
                        last = nc.tensor.matmul(bank[6 + tt % 2][:, 0:nvr], x_[:, p, ci, c], w_[:, ci, 0:nvr],
                                                start=n == 0, stop=n == len(parts) - 1)
                    last.then_inc(s.ap.vr_ready.sem, 1)

            def group(g, p):
                if group_exists(g + 1):
                    transposes(g + 1, 1 - p)
                if group_exists(g):
                    products(g, p)

            steps(pe, group, -1, 2, GROUPS - 2, GROUPS)

        def ap_scalar(act, s, a):
            act.wait_ge(*s.ap.wt_ready(1))
            nvr = D * (2 if a == 0 else 1)
            for ci in range(HALVES):
                nc.scalar.activation(s.wqk_hi[:, ci, :], bank[ci][:, :], ACT.Copy).then_inc(s.ap.wt_hi_ready.sem, 1)
                nc.scalar.activation(s.wvr_hi[:, ci, 0:nvr], bank[4 + ci][:, 0:nvr], ACT.Copy)\
                    .then_inc(s.ap.wt_hi_ready.sem, 1)
            act.wait_ge(*s.ap.consts_in(16 * (4 if a == 0 else 3)))

            def features_high(g, p):
                if due(GROUP * (g - 1)):
                    act.wait_ge(*s.ap.vr_ready(GROUP * (g - 1)))
                for ch in range(HALVES):
                    act.wait_ge(*s.ap.xt_ready(HALVES * g + ch + 1))
                    nc.scalar.activation(s.xt_hi[:, p, ch, :], bank[ch][:, :], ACT.Copy).then_inc(s.ap.xt_hi_ready.sem, 1)

            def products_high(g, p):
                if due(16 * GROUP * g):
                    act.wait_ge(*s.ap.q_stored(16 * GROUP * g))
                for i in range(4):
                    act.wait_ge(*s.ap.qk_ready(4 * g + i + 1))
                    to = s.q_hl[:, 0, i, :] if i < 2 else s.kt_hi[:, i - 2, bass.ds(g * CHUNK, CHUNK)]
                    apart(act)
                    nc.scalar.activation(to, bank[2 + i][:, :], ACT.Identity, bias=s.bqk[:, i // 2, i % 2:i % 2 + 1],
                                         scale=1.0).then_inc(s.ap.qk_hi_ready.sem, 1)
                for tt in range(GROUP):
                    act.wait_ge(*s.ap.vr_biased(GROUP * g + tt + 1))
                    apart(act)
                    nc.scalar.activation(s.v[:, GROUP * g + tt, 0:D], s.vr[:, tt, 0:D], ACT.Copy)\
                        .then_inc(s.ap.v_hi_ready.sem, 1)

            def group(g, p):
                if group_exists(g + 1):
                    features_high(g + 1, 1 - p)
                if group_exists(g):
                    products_high(g, p)

            steps(act, group, -1, 2, GROUPS - 2, GROUPS)

        def ap_vector(dve, s, a):
            nvr = D * (2 if a == 0 else 1)
            dve.wait_ge(*s.ap.wt_ready(1))
            dve.wait_ge(*s.ap.wt_hi_ready(4))
            for ci in range(HALVES):
                nc.vector.tensor_tensor(s.wqk_lo[:, ci, :], bank[ci][:, :], s.wqk_hi[:, ci, :].bitcast(F32),
                                        ALU.subtract).then_inc(s.ap.wt_lo_ready.sem, 1)
                nc.vector.tensor_tensor(s.wvr_lo[:, ci, 0:nvr], bank[4 + ci][:, 0:nvr],
                                        s.wvr_hi[:, ci, 0:nvr].bitcast(F32), ALU.subtract)\
                    .then_inc(s.ap.wt_lo_ready.sem, 1)
            dve.wait_ge(*s.ap.consts_in(16 * (4 if a == 0 else 3)))

            def features_low(g, p):
                if due(GROUP * (g - 1)):
                    dve.wait_ge(*s.ap.vr_ready(GROUP * (g - 1)))
                for ch in range(HALVES):
                    dve.wait_ge(*s.ap.xt_hi_ready(HALVES * g + ch + 1))
                    nc.vector.tensor_tensor(s.xt_lo[:, p, ch, :], bank[ch][:, :], s.xt_hi[:, p, ch, :].bitcast(F32),
                                            ALU.subtract).then_inc(s.ap.xt_lo_ready.sem, 1)

            def products_low(g, p):
                if due(16 * GROUP * g):
                    dve.wait_ge(*s.ap.q_stored(16 * GROUP * g))
                for i in range(4):
                    dve.wait_ge(*s.ap.qk_hi_ready(4 * g + i + 1))
                    cols = bass.ds(g * CHUNK, CHUNK)
                    hi = s.q_hl[:, 0, i, :] if i < 2 else s.kt_hi[:, i - 2, cols]
                    lo = s.q_hl[:, 1, i, :] if i < 2 else s.kt_lo[:, i - 2, cols]
                    nc.vector.scalar_tensor_tensor(lo, bank[2 + i][:, :], s.bqk[:, i // 2, i % 2:i % 2 + 1],
                                                   hi.bitcast(F32), ALU.add, ALU.subtract).then_inc(s.ap.qk_lo_ready.sem, 1)
                if due(GROUP * g):
                    dve.wait_ge(*s.ap.v_hi_ready(GROUP * g))
                    dve.wait_ge(*s.ap.v_lo_ready(GROUP * g))
                if a == 0:
                    if due(16 * g):
                        dve.wait_ge(*s.ap.res_stored(16 * g))
                for tt in range(GROUP):
                    dve.wait_ge(*s.ap.vr_ready(GROUP * g + tt + 1))
                    nc.vector.tensor_tensor(s.vr[:, tt, 0:nvr], bank[6 + tt % 2][:, 0:nvr], s.bvr[:, 0:nvr], ALU.add)\
                        .then_inc(s.ap.vr_biased.sem, 1)
                for tt in range(GROUP):
                    dve.wait_ge(*s.ap.v_hi_ready(GROUP * g + tt + 1))
                    nc.vector.tensor_tensor(s.v[:, GROUP * g + tt, D:2 * D], s.vr[:, tt, 0:D],
                                            s.v[:, GROUP * g + tt, 0:D].bitcast(F32), ALU.subtract)\
                        .then_inc(s.ap.v_lo_ready.sem, 1)

            def group(g, p):
                if group_exists(g + 1):
                    features_low(g + 1, 1 - p)
                if group_exists(g):
                    products_low(g, p)

            steps(dve, group, -1, 2, GROUPS - 2, GROUPS)

        def am_over(eng, s, a):
            eng.wait_ge(*s.am.pv_done(TILES * CHUNKS))
            eng.wait_ge(*s.am.hi_ready(TILES * CHUNKS))
            eng.wait_ge(*s.am.lo_ready(TILES * CHUNKS))
            eng.wait_ge(*s.am.o_lo_ready(TILES))
            eng.wait_ge(*s.am.o_taken(TILES))

        def load_q(sp, s, a, t, p):
            if due(CHUNKS * (t - 1)):
                sp.wait_ge(*s.am.scores_ready(CHUNKS * (t - 1)))
            sp.dma_start([s.q0, s.q1][p][:, :, :, :].bitcast(F32),
                         q_dram[a].rearrange("t p (hl h n) -> t p hl h n", hl=2, h=HALVES)[t])\
                .then_inc([s.am.q_in0, s.am.q_in1][p].sem, 16)

        def am_sync(sp, s, a):
            dst = att_args[a][-1]
            res = res_dram if a == 0 else xa_dram

            def load_adj(t, q):
                if due(QUARTERS * (t - 1) + q + 1):
                    sp.wait_ge(*s.am.att_ready(QUARTERS * (t - 1) + q + 1))
                sp.dma_start(s.adj[:, q * QUARTER:(q + 1) * QUARTER], adj_quarters[t, q]).then_inc(
                    [s.am.adj_in0, s.am.adj_in1, s.am.adj_in2, s.am.adj_in3][q].sem, 16)

            def load_res(t, p):
                if due(t - 1):
                    sp.wait_ge(*s.am.y_ready(t - 1))
                sp.dma_start([s.res0, s.res1][p][:, :], node_tiles(res)[t]).then_inc([s.am.res_in0, s.am.res_in1][p].sem, 16)
                if a == 1:
                    sp.dma_start([s.xln0, s.xln1][p][:, :], node_tiles(x1_dram)[t]).then_inc(
                        [s.am.res_in0, s.am.res_in1][p].sem, 16)

            def store(t, p):
                sp.wait_ge(*s.am.y_ready(t + 1))
                sp.dma_start(node_tiles(dst)[t], [s.y0, s.y1][p][:, :]).then_inc([s.am.y_stored0, s.am.y_stored1][p].sem, 16)

            if a == 0:
                load_att_weights(sp, att[1], 1)

            def tile(t, p):
                if exists(t + 1):
                    load_q(sp, s, a, t + 1, 1 - p)
                for q in range(QUARTERS):
                    if exists(t):
                        load_adj(t, q)
                    if q == 2 and exists(t - 2):
                        store(t - 2, p)
                        if exists(t):
                            load_res(t, p)
                    elif q == 2 and exists(t):
                        load_res(t, p)

            steps(sp, tile, 0, 4, TILES - 2, TILES + 1)
            first_groups_stored(sp, s.am)

        def am_tensor(pe, s, a):

            def scores(t, p, c):
                k = CHUNKS * t + c
                if c == 0:
                    pe.wait_ge(*[s.am.q_in0, s.am.q_in1][p](8 * (t - p) + 16))
                if due(k - 3):
                    pe.wait_ge(*s.am.scores_taken(k - 3))
                q = [s.q0, s.q1][p]
                cols = slice(c * CHUNK, (c + 1) * CHUNK)
                parts = [(0, s.kt_hi, ch) for ch in range(HALVES)] + [(0, s.kt_lo, ch) for ch in range(HALVES)]\
                    + [(1, s.kt_hi, ch) for ch in range(HALVES)]
                for n, (hl, k_, ch) in enumerate(parts):
                    last = nc.tensor.matmul(bank[c % 4][:, :], q[:, hl, ch, :], k_[:, ch, cols], start=n == 0,
                                            stop=n == len(parts) - 1)
                last.then_inc(s.am.scores_ready.sem, 1)

            def transposes(t, p, c):
                g = CHUNKS * t + c
                if c % CPQ == 0:
                    pe.wait_ge(*s.am.att_ready(QUARTERS * t + c // CPQ + 1))
                if due(g - 1):
                    pe.wait_ge(*s.am.hi_ready(g - 1))
                if due(g - 1):
                    pe.wait_ge(*s.am.lo_ready(g - 1))
                for b in range(BLOCKS):
                    j = c * BLOCKS + b
                    last = nc.tensor.transpose(bank[4 + c % 2][:, b * P:(b + 1) * P],
                                               [s.s0, s.s1][p][:, j * P:(j + 1) * P], ident[:, :])
                last.then_inc(s.am.transposed.sem, 1)

            def values(t, p, c):
                g = CHUNKS * t + c
                if c == 0:
                    if due(t - 1):
                        pe.wait_ge(*s.am.o_taken(t - 1))
                pe.wait_ge(*s.am.hi_ready(g + 1))
                pe.wait_ge(*s.am.lo_ready(g + 1))
                hi, lo = [s.pt_hi0, s.pt_hi1][c % 2], [s.pt_lo0, s.pt_lo1][c % 2]
                for b in range(BLOCKS):
                    j = c * BLOCKS + b
                    w = slice(b * P, (b + 1) * P)
                    nc.tensor.matmul(bank[6 + p][:, :], hi[:, w], s.v[:, j, :], start=j == 0, stop=False)
                    last = nc.tensor.matmul(bank[6 + p][:, 0:D], lo[:, w], s.v[:, j, 0:D], start=False,
                                            stop=j == TILES - 1)
                last.then_inc(s.am.pv_done.sem, 1)

            def tile(t, p):
                for c in range(CHUNKS):
                    if exists(t):
                        scores(t, p, c)
                    if exists(behind(t, p, c, LAG)[0]):
                        transposes(*behind(t, p, c, LAG))
                    if exists(behind(t, p, c, LAG + 1)[0]):
                        values(*behind(t, p, c, LAG + 1))

            steps(pe, tile, 0, 4, TILES, TILES + 2)

        def am_scalar(act, s, a):

            def exponentials(t, p, q):
                if q == 0:
                    act.wait_ge(*s.am.bias_ready(t + 1))
                col = slice(q * QUARTER, (q + 1) * QUARTER)
                buf = [s.s0, s.s1][p][:, col]
                nc.scalar.activation(buf, buf, ACT.Exp, bias=s.bias[:, p:p + 1], scale=SCALE,
                                     accum_out=s.sum4[:, p, q:q + 1]).then_inc(s.am.exp_done.sem, 1)

            def tile(t, p):
                for c in range(CHUNKS):
                    tt, tp, tc = behind(t, p, c, LAG)
                    if exists(tt):
                        g = CHUNKS * tt + tc
                        act.wait_ge(*s.am.transposed(g + 1))
                        if due(g - 1):
                            act.wait_ge(*s.am.pv_done(g - 1))
                        nc.scalar.activation([s.pt_hi0, s.pt_hi1][tc % 2][:, :], bank[4 + tc % 2][:, :], ACT.Copy)\
                            .then_inc(s.am.hi_ready.sem, 1)
                    if c < 2 and exists(t - 1):
                        exponentials(t - 1, 1 - p, 2 * c)
                        exponentials(t - 1, 1 - p, 2 * c + 1)
                    if c == LAG + 2 and exists(t - 2):
                        if due(CHUNKS * (t - 1)):
                            act.wait_ge(*s.am.pv_done(CHUNKS * (t - 1)))
                        if due(t - 2):
                            act.wait_ge(*s.am.o_taken(t - 2))
                        nc.scalar.activation(s.o_lo[:, :], bank[6 + p][:, D:2 * D], ACT.Copy).then_inc(s.am.o_lo_ready.sem, 1)

            steps(act, tile, 0, 4, TILES, TILES + 2)

        def am_vector(dve, s, a):

            def take_scores(t, p, c):
                dve.wait_ge(*s.am.scores_ready(CHUNKS * t + c + 1))
                nc.vector.tensor_scalar([s.s0, s.s1][p][:, c * CHUNK:(c + 1) * CHUNK], bank[c % 4][:, :], 1.0, None,
                                        ALU.mult, ALU.max, accum_out=s.max8[:, p, c:c + 1])\
                    .then_inc(s.am.scores_taken.sem, 1)

            def row_max(t, p):
                dve.wait_ge(*s.am.scores_taken(CHUNKS * (t + 1)))
                nc.vector.tensor_reduce(s.neg_max[:, :], s.max8[:, p, :], AX.X, ALU.max, negate=True)\
                    .then_inc(s.am.max_ready.sem, 1)
                dve.wait_ge(*s.am.max_ready(t + 1))
                nc.vector.tensor_scalar(s.bias[:, p:p + 1], s.neg_max[:, :], SCALE, None, ALU.mult)\
                    .then_inc(s.am.bias_ready.sem, 1)

            def row_sum(t, p):
                dve.wait_ge(*s.am.exp_done(QUARTERS * (t + 1)))
                nc.vector.reduce_sum(s.total[:, :], s.sum4[:, p, :], AX.X).then_inc(s.am.sum_ready.sem, 1)
                dve.wait_ge(*s.am.sum_ready(t + 1))
                nc.vector.reciprocal(s.rinv[:, :], s.total[:, :]).then_inc(s.am.rinv_ready.sem, 1)
                dve.wait_ge(*s.am.rinv_ready(t + 1))

            def attention_rows(t, p, q):
                col = slice(q * QUARTER, (q + 1) * QUARTER)
                dve.wait_ge(*[s.am.adj_in0, s.am.adj_in1, s.am.adj_in2, s.am.adj_in3][q](16 * (t + 1)))
                buf = [s.s0, s.s1][p][:, col]
                nc.vector.scalar_tensor_tensor(buf, buf, s.rinv[:, :], s.adj[:, col], ALU.mult, ALU.add)\
                    .then_inc(s.am.att_ready.sem, 1)

            def finish(t, p):
                dve.wait_ge(*s.am.o_lo_ready(t + 1))
                nc.vector.tensor_tensor(s.o[:, :], bank[6 + p][:, 0:D], s.o_lo[:, :], ALU.add).then_inc(s.am.o_taken.sem, 1)
                dve.wait_ge(*s.am.o_taken(t + 1))
                dve.wait_ge(*[s.am.res_in0, s.am.res_in1][p]((8 * (t - p) + 16) * (1 + a)))
                if due(8 * (t - p)):
                    dve.wait_ge(*[s.am.y_stored0, s.am.y_stored1][p](8 * (t - p)))
                y, res = [s.y0, s.y1][p], [s.res0, s.res1][p]
                if a == 0:
                    nc.vector.scalar_tensor_tensor(y[:, :], s.o[:, :], 0.0, res[:, :], ALU.max, ALU.add)\
                        .then_inc(s.am.y_ready.sem, 1)
                    return
                nc.vector.scalar_tensor_tensor(s.o[:, :], s.o[:, :], 0.0, res[:, :], ALU.max, ALU.add)\
                    .then_inc(s.am.residual_added.sem, 1)
                dve.wait_ge(*s.am.residual_added(t + 1))
                nc.vector.tensor_tensor(s.o[:, :], s.o[:, :], [s.xln0, s.xln1][p][:, :], ALU.add)\
                    .then_inc(s.am.summed.sem, 1)
                feature_sums(dve, s, s.am, t)
                mean_variance(dve, s, s.am, t)
                variance_eps(dve, s, s.am, t)

            def tile(t, p):
                for c in range(CHUNKS):
                    if exists(t):
                        take_scores(t, p, c)
                    if exists(t - 1) and c == LAG - 1:
                        row_sum(t - 1, 1 - p)
                        attention_rows(t - 1, 1 - p, 0)
                    tt, tp, tc = behind(t, p, c, LAG)
                    if exists(tt):
                        g = CHUNKS * tt + tc
                        dve.wait_ge(*s.am.transposed(g + 1))
                        dve.wait_ge(*s.am.hi_ready(g + 1))
                        if due(g - 1):
                            dve.wait_ge(*s.am.pv_done(g - 1))
                        nc.vector.tensor_tensor([s.pt_lo0, s.pt_lo1][tc % 2][:, :], bank[4 + tc % 2][:, :],
                                                [s.pt_hi0, s.pt_hi1][tc % 2][:, :].bitcast(F32), ALU.subtract)\
                            .then_inc(s.am.lo_ready.sem, 1)
                    if exists(t - 1):
                        if c in (LAG, LAG + 2, LAG + 4):
                            attention_rows(t - 1, 1 - p, 1 + (LAG, LAG + 2, LAG + 4).index(c))
                    if c == LAG + 2 and exists(t - 2):
                        finish(t - 2, p)
                    if c == LAG + 3 and a == 1 and exists(t - 2):
                        normalize(dve, s, s.am, [s.y0, s.y1][p], t - 2, p)
                    if c == CHUNKS - 1 and exists(t):
                        row_max(t, p)

            steps(dve, tile, 0, 4, TILES, TILES + 2)

        def am_pool(pool, s):
            inverse_roots(pool, s, s.am)

        block = top.enter_context(nc.Block())

        @block.sync
        def _(sp):
            for a, s in enumerate(gat):
                if a == 0:
                    load_gat_inputs(sp, s, 0)
                gp_sync(sp, s, a)
                gp_over(sp, s, a)
                if a == 0:
                    load_gat_inputs(sp, gat[1], 1)
                else:
                    load_att_weights(sp, att[0], 0)
                gm_sync(sp, s, a)
                gm_over(sp, s, a)
            for a, s in enumerate(att):
                ap_sync(sp, s, a)
                ap_over(sp, s, a)
                ap_stored(sp, s, a)
                am_sync(sp, s, a)
                am_over(sp, s, a)
            last_store(sp, att[1], att[1].am, out)

        @block.gpsimd
        def _(pool):
            nc.gpsimd.memset(ident[:, :], 0.0).then_inc(ident_step, 1)
            nc.gpsimd.memset(off_diag[:, :], 1.0).then_inc(ident_step, 1)
            nc.gpsimd.memset(ones[:, :], 1.0).then_inc(consts_ready, 1)
            nc.gpsimd.memset(power[:, :], -0.5).then_inc(consts_ready, 1)
            pool.wait_ge(ident_step, 2)
            for m, fill in ((ident, 1.0), (off_diag, 0.0)):
                nc.gpsimd.affine_select(out=m[:, :], in_=m[:, :], compare_op=ALU.not_equal, fill=fill, base=0,
                                        pattern=[[-1, P]], channel_multiplier=1).then_inc(consts_ready, 1)
            pool.wait_ge(consts_ready, 4)
            gm_pool(pool, gat[1])
            am_pool(pool, att[1])

        @block.tensor
        def _(pe):
            pe.wait_ge(consts_ready, 4)
            for a, s in enumerate(gat):
                gp_tensor(pe, s, a)
                gp_over(pe, s, a)
                gm_tensor(pe, s, a)
                gm_over(pe, s, a)
            for a, s in enumerate(att):
                ap_tensor(pe, s, a)
                ap_over(pe, s, a)
                am_tensor(pe, s, a)
                am_over(pe, s, a)

        @block.scalar
        def _(act):
            act.wait_ge(consts_ready, 4)
            nc.scalar.mul(neg_ident[:, :], ident[:, :], -1.0).then_inc(neg_ident_ready, 1)
            for a, s in enumerate(gat):
                gp_scalar(act, s, a)
                gp_over(act, s, a)
                gm_scalar(act, s, a)
                gm_over(act, s, a)
            for a, s in enumerate(att):
                ap_scalar(act, s, a)
                ap_over(act, s, a)
                ap_stored(act, s, a)
                am_scalar(act, s, a)
                am_over(act, s, a)

        @block.vector
        def _(dve):
            dve.wait_ge(consts_ready, 4)
            for a, s in enumerate(gat):
                gp_vector(dve, s, a)
                gp_over(dve, s, a)
                gm_vector(dve, s, a)
                gm_over(dve, s, a)
            for a, s in enumerate(att):
                ap_vector(dve, s, a)
                ap_over(dve, s, a)
                ap_stored(dve, s, a)
                am_vector(dve, s, a)
                am_over(dve, s, a)


_INS = ['x', 'adj', 'L0_gnn_W1', 'L0_gnn_b1', 'L0_gnn_asrc1', 'L0_gnn_adst1', 'L0_gnn_W2', 'L0_gnn_b2',
        'L0_gnn_asrc2', 'L0_gnn_adst2', 'L1_gnn_wq0', 'L1_gnn_bq0', 'L1_gnn_wk0', 'L1_gnn_bk0', 'L1_gnn_wv0',
        'L1_gnn_bv0', 'L1_gnn_wres', 'L1_gnn_bres', 'L1_gnn_wq1', 'L1_gnn_bq1', 'L1_gnn_wk1', 'L1_gnn_bk1',
        'L1_gnn_wv1', 'L1_gnn_bv1']


def kernel(**inputs):
    import concourse.bacc as bacc
    from concourse.bass_utils import run_bass_kernel_spmd

    nc = bacc.Bacc("TRN2", target_bir_lowering=False, num_devices=1)
    arrays, args = {}, []
    for name in _INS:
        a = np.ascontiguousarray(inputs[name])
        arrays[f"in_{name}"] = a
        args.append(nc.dram_tensor(f"in_{name}", a.shape, mybir.dt.from_np(a.dtype), kind="ExternalInput").ap())
    out = nc.dram_tensor("out", (N, D), F32, kind="ExternalOutput").ap()
    build(nc, *args, out)
    r = run_bass_kernel_spmd(nc, [arrays], core_ids=[0])
    return r.results[0]["out"]
```
